# Optimizing a Trainium2 kernel written in Bass

```python
import numpy as np
import jax
import jax.numpy as jnp

def _softmax(x, axis=-1):
    return jax.nn.softmax(x, axis=axis)

def _gelu(x):
    return jax.nn.gelu(x, approximate=True)

def _silu(x):
    return jax.nn.silu(x)

def _sigmoid(x):
    return jax.nn.sigmoid(x)

def _layernorm(x, axis=-1, eps=1e-05):
    m = jnp.mean(x, axis=axis, keepdims=True)
    v = jnp.var(x, axis=axis, keepdims=True)
    return (x - m) / jnp.sqrt(v + eps)

def _scatter_add(tgt, idx, src, axis=0):
    return tgt.at[idx].add(src)

def _segment_sum(src, seg, n):
    return jax.ops.segment_sum(src, seg, n)
kernel_name = 'mk_adaln_attn_ffn_d1_seqx_r4_ec648b'

def setup_inputs(seed: int=0):
    np.random.seed(seed)
    _w = jnp.asarray

    def _rec_inputs():
        import jax
        import jax.numpy as jnp
        _rk = jax.random.key(seed)
        x = -0.000125 + 0.9999 * jax.random.normal(jax.random.fold_in(_rk, 1), (128, 64, 1024), jnp.float32)
        _lenS = 64 - jax.random.randint(jax.random.fold_in(_rk, 7), (128,), 0, max(1, 64 // 4) + 1, jnp.int32)
        _lenS2 = 64 - jax.random.randint(jax.random.fold_in(_rk, 8), (128,), 0, max(1, 64 // 4) + 1, jnp.int32)
        itok_B_3_7 = jax.random.randint(jax.random.fold_in(_rk, 11), (128,), 3, 8, jnp.int32)
        itok_B_4_50 = jax.random.randint(jax.random.fold_in(_rk, 12), (128,), 4, 51, jnp.int32)
        return (x, itok_B_3_7, itok_B_4_50)
    x, itok_B_3_7, itok_B_4_50 = _rec_inputs()

    def _L0_cond_setup():
        import jax, jax.numpy as jnp
        import numpy as np
        RANK = 16
        ALPHA = 16.0
        SCALING = ALPHA / RANK
        N_ADAPTERS = 8
        IN_F = 1024
        OUT_F = 1024
        BATCH = 4
        SEQ = 512
        key = jax.random.key(seed)
        kx, ka, kb, ki = jax.random.split(key, 4)
        x = jax.random.normal(kx, (BATCH, SEQ, IN_F), dtype=jnp.float32)
        A = jax.random.normal(ka, (N_ADAPTERS, OUT_F, RANK), dtype=jnp.float32) * 0.02
        B = jax.random.normal(kb, (N_ADAPTERS, RANK, IN_F), dtype=jnp.float32) * 0.02
        adapter_ids = jax.random.randint(ki, (BATCH,), 0, N_ADAPTERS, dtype=jnp.int32)
        return {'x': x, 'A': A, 'B': B, 'adapter_ids': adapter_ids}
    _L0_cond_all = _L0_cond_setup()
    _L0_cond_in = {k: v for k, v in _L0_cond_all.items() if k in ('A', 'B')}
    del _L0_cond_all

    def _L0_attn_setup():
        import jax, jax.numpy as jnp
        import numpy as np
        HDC_DIM = 1024
        N_HEADS = 4
        HEAD_DIM = HDC_DIM // N_HEADS

        def _ste_sign(w):
            alpha = jnp.mean(jnp.abs(w), axis=-1, keepdims=True)
            hard = alpha * jnp.sign(w)
            hard = jnp.where(hard == 0, alpha, hard)
            return jax.lax.stop_gradient(hard - w) + w
        key = jax.random.key(seed)
        kx, kq, kk, kv = jax.random.split(key, 4)
        B, T = (4, 512)
        x = jax.random.normal(kx, (B, T, HDC_DIM), dtype=jnp.float32)
        bv_q = jax.random.normal(kq, (N_HEADS, HEAD_DIM), dtype=jnp.float32) * 0.02
        bv_k = jax.random.normal(kk, (N_HEADS, HEAD_DIM), dtype=jnp.float32) * 0.02
        bv_v = jax.random.normal(kv, (N_HEADS, HEAD_DIM), dtype=jnp.float32) * 0.02
        return {'x': x, 'bv_q': bv_q, 'bv_k': bv_k, 'bv_v': bv_v}
    _L0_attn_all = _L0_attn_setup()
    _L0_attn_in = {k: v for k, v in _L0_attn_all.items() if k in ('bv_q', 'bv_k', 'bv_v')}
    del _L0_attn_all

    def _L0_cond2_setup():
        import jax, jax.numpy as jnp
        import numpy as np
        RANK = 16
        ALPHA = 16.0
        SCALING = ALPHA / RANK
        key = jax.random.key(seed)
        k1, k2, k3, k4 = jax.random.split(key, 4)
        batch, n_tok, d_in, d_out, n_adapters, rank = (8, 512, 1024, 1024, 64, RANK)
        x = jax.random.normal(k1, (batch, n_tok, d_in), dtype=jnp.float32)
        A = jax.random.normal(k2, (n_adapters, d_out, rank), dtype=jnp.float32) * 0.02
        B = jax.random.normal(k3, (n_adapters, rank, d_in), dtype=jnp.float32)
        adapter_ids = jax.random.randint(k4, (batch,), 0, n_adapters, dtype=jnp.int32)
        return {'x': x, 'A': A, 'B': B, 'adapter_ids': adapter_ids}
    _L0_cond2_all = _L0_cond2_setup()
    _L0_cond2_in = {k: v for k, v in _L0_cond2_all.items() if k in ('A', 'B')}
    del _L0_cond2_all

    def _L0_ffn_setup():
        import jax, jax.numpy as jnp
        import numpy as np
        N_STREAMS = 4
        DIM = 256
        SINKHORN_ITERS = 50
        SINKHORN_TAU = 0.1
        RMS_EPS = 1.1920929e-07

        def sinkhorn_log(logits, num_iters=SINKHORN_ITERS, tau=SINKHORN_TAU):
            Z = logits / tau
            u0 = jnp.zeros(Z.shape[:-1], Z.dtype)
            v0 = jnp.zeros_like(u0)

            def step(carry, _):
                u, v = carry
                u = -jax.nn.logsumexp(Z + v[..., None, :], axis=-1)
                v = -jax.nn.logsumexp(Z + u[..., :, None], axis=-2)
                return ((u, v), None)
            (u, v), _ = jax.lax.scan(step, (u0, v0), None, length=num_iters)
            return jnp.exp(Z + u[..., :, None] + v[..., None, :])
        key = jax.random.key(seed)
        ks = jax.random.split(key, 6)
        B, T = (4, 512)
        n, C = (N_STREAMS, DIM)
        wd = n * C
        x = jax.random.normal(ks[0], (B, T, wd), dtype=jnp.float32)
        W_res = 0.01 * jax.random.normal(ks[1], (n * n, wd), dtype=jnp.float32)
        W_pre = 0.01 * jax.random.normal(ks[2], (n, wd), dtype=jnp.float32)
        W_post = 0.01 * jax.random.normal(ks[3], (n, wd), dtype=jnp.float32)
        H_res_base = jnp.full((n, n), -0.5, dtype=jnp.float32)
        H_res_base = H_res_base.at[jnp.arange(n), jnp.arange(n)].set(0.0)
        H_pre_base = jnp.zeros((n,), dtype=jnp.float32).at[0].set(1.0)
        H_post_base = jnp.zeros((n,), dtype=jnp.float32)
        gate = jnp.array([5.0], dtype=jnp.float32)
        W_branch = 1.0 / np.sqrt(C) * jax.random.normal(ks[4], (C, C), dtype=jnp.float32)
        return {'x': x, 'W_res': W_res, 'W_pre': W_pre, 'W_post': W_post, 'H_res_base': H_res_base, 'H_pre_base': H_pre_base, 'H_post_base': H_post_base, 'gate': gate, 'W_branch': W_branch}
    _L0_ffn_all = _L0_ffn_setup()
    _L0_ffn_in = {k: v for k, v in _L0_ffn_all.items() if k in ('W_res', 'W_pre', 'W_post', 'H_res_base', 'H_pre_base', 'H_post_base', 'gate', 'W_branch')}
    del _L0_ffn_all
    return {'x': x, 'itok_B_3_7': itok_B_3_7, 'itok_B_4_50': itok_B_4_50, 'L0_cond_A': _L0_cond_in['A'], 'L0_cond_B': _L0_cond_in['B'], 'L0_attn_bv_q': _L0_attn_in['bv_q'], 'L0_attn_bv_k': _L0_attn_in['bv_k'], 'L0_attn_bv_v': _L0_attn_in['bv_v'], 'L0_cond2_A': _L0_cond2_in['A'], 'L0_cond2_B': _L0_cond2_in['B'], 'L0_ffn_W_res': _L0_ffn_in['W_res'], 'L0_ffn_W_pre': _L0_ffn_in['W_pre'], 'L0_ffn_W_post': _L0_ffn_in['W_post'], 'L0_ffn_H_res_base': _L0_ffn_in['H_res_base'], 'L0_ffn_H_pre_base': _L0_ffn_in['H_pre_base'], 'L0_ffn_H_post_base': _L0_ffn_in['H_post_base'], 'L0_ffn_gate': _L0_ffn_in['gate'], 'L0_ffn_W_branch': _L0_ffn_in['W_branch']}

def reference(x, itok_B_3_7, itok_B_4_50, L0_cond_A, L0_cond_B, L0_attn_bv_q, L0_attn_bv_k, L0_attn_bv_v, L0_cond2_A, L0_cond2_B, L0_ffn_W_res, L0_ffn_W_pre, L0_ffn_W_post, L0_ffn_H_res_base, L0_ffn_H_pre_base, L0_ffn_H_post_base, L0_ffn_gate, L0_ffn_W_branch):
    import jax
    import jax.numpy as jnp

    def _L0_cond_ref(x, A, B, adapter_ids):
        import jax, jax.numpy as jnp
        import numpy as np
        RANK = 16
        ALPHA = 16.0
        SCALING = ALPHA / RANK
        N_ADAPTERS = 8
        IN_F = 1024
        OUT_F = 1024
        BATCH = 4
        SEQ = 512
        B_sel = B[adapter_ids]
        A_sel = A[adapter_ids]
        Bx = jnp.einsum('bni,bri->bnr', x, B_sel)
        out = jnp.einsum('bnr,bor->bno', Bx, A_sel)
        return out * SCALING

    def _L0_attn_ref(x, bv_q, bv_k, bv_v):
        import jax, jax.numpy as jnp
        import numpy as np
        HDC_DIM = 1024
        N_HEADS = 4
        HEAD_DIM = HDC_DIM // N_HEADS

        def _ste_sign(w):
            alpha = jnp.mean(jnp.abs(w), axis=-1, keepdims=True)
            hard = alpha * jnp.sign(w)
            hard = jnp.where(hard == 0, alpha, hard)
            return jax.lax.stop_gradient(hard - w) + w
        B, T, D = x.shape
        H, HD = (N_HEADS, HEAD_DIM)
        scale = HD ** (-0.5)
        q_bind = _ste_sign(bv_q)
        k_bind = _ste_sign(bv_k)
        v_bind = _ste_sign(bv_v)
        xh = x.reshape(B, T, H, HD)
        Q = xh * q_bind
        K = xh * k_bind
        V = xh * v_bind
        scores = jnp.einsum('bthd,bshd->bhts', Q, K) * scale
        causal = jnp.tril(jnp.ones((T, T), dtype=bool))
        attn = jnp.where(causal, jax.nn.sigmoid(scores * 4.0), 0.0)
        out = jnp.einsum('bhts,bshd->bthd', attn, V)
        return out.reshape(B, T, D)

    def _L0_cond2_ref(x, A, B, adapter_ids):
        import jax, jax.numpy as jnp
        import numpy as np
        RANK = 16
        ALPHA = 16.0
        SCALING = ALPHA / RANK
        B_req = B[adapter_ids]
        A_req = A[adapter_ids]
        Bx = jnp.einsum('bni,bri->bnr', x, B_req)
        out = jnp.einsum('bnr,bor->bno', Bx, A_req)
        return out * SCALING

    def _L0_ffn_ref(x, W_res, W_pre, W_post, H_res_base, H_pre_base, H_post_base, gate, W_branch):
        import jax, jax.numpy as jnp
        import numpy as np
        N_STREAMS = 4
        DIM = 256
        SINKHORN_ITERS = 50
        SINKHORN_TAU = 0.1
        RMS_EPS = 1.1920929e-07

        def sinkhorn_log(logits, num_iters=SINKHORN_ITERS, tau=SINKHORN_TAU):
            Z = logits / tau
            u0 = jnp.zeros(Z.shape[:-1], Z.dtype)
            v0 = jnp.zeros_like(u0)

            def step(carry, _):
                u, v = carry
                u = -jax.nn.logsumexp(Z + v[..., None, :], axis=-1)
                v = -jax.nn.logsumexp(Z + u[..., :, None], axis=-2)
                return ((u, v), None)
            (u, v), _ = jax.lax.scan(step, (u0, v0), None, length=num_iters)
            return jnp.exp(Z + u[..., :, None] + v[..., None, :])
        B, T, nC = x.shape
        n = N_STREAMS
        C = nC // n
        x_norm = x * jax.lax.rsqrt(jnp.mean(x * x, axis=-1, keepdims=True) + RMS_EPS)
        H_res_logits = (x_norm @ W_res.T).reshape(B, T, n, n) + H_res_base
        H_pre_logits = x_norm @ W_pre.T + H_pre_base
        H_post_logits = x_norm @ W_post.T + H_post_base
        H_res = sinkhorn_log(H_res_logits)
        H_pre = jax.nn.softmax(H_pre_logits, axis=-1)
        H_post = jax.nn.softmax(H_post_logits, axis=-1)
        g = jax.nn.sigmoid(gate)[0]
        I = jnp.eye(n, dtype=H_res.dtype)
        H_res = (1.0 - g) * I + g * H_res
        x_streams = x.reshape(B, T, n, C)
        x_pre = jnp.einsum('btnc,btn->btc', x_streams, H_pre)
        y = x_pre @ W_branch
        x_mixed = jnp.einsum('btij,btjc->btic', H_res, x_streams)
        y_distributed = jnp.einsum('btc,btn->btnc', y, H_post)
        return (x_mixed + y_distributed).reshape(B, T, nC)
    x = x + _L0_attn_ref(_L0_cond_ref(x, L0_cond_A, L0_cond_B, itok_B_3_7), L0_attn_bv_q, L0_attn_bv_k, L0_attn_bv_v)
    x = x + _L0_ffn_ref(_L0_cond2_ref(x, L0_cond2_A, L0_cond2_B, itok_B_4_50), L0_ffn_W_res, L0_ffn_W_pre, L0_ffn_W_post, L0_ffn_H_res_base, L0_ffn_H_pre_base, L0_ffn_H_post_base, L0_ffn_gate, L0_ffn_W_branch)
    return x

_drawn_inputs = setup_inputs


def setup_inputs(seed=0):
    import zlib

    import numpy as np

    out = dict(_drawn_inputs(seed))
    spreads = {'L0_ffn_H_post_base': (0.0, 0.8)}
    factors = {'L0_cond_A': 8.0,
     'L0_cond_B': 8.0,
     'L0_attn_bv_q': 8.0,
     'L0_attn_bv_k': 8.0,
     'L0_attn_bv_v': 8.0}
    for name, (base, spread) in spreads.items():
        noise = np.random.default_rng([zlib.crc32(name.encode()), seed]).standard_normal(out[name].shape)
        drawn = base * np.exp(spread * noise) if base else spread * noise
        out[name] = jnp.asarray(drawn.astype(out[name].dtype))
    for name, factor in factors.items():
        out[name] = (out[name] * factor).astype(out[name].dtype)
    return out
```

```python
from contextlib import ExitStack

import concourse.bass as bass
from concourse import mybir

ALU = mybir.AluOpType
ACT = mybir.ActivationFunctionType
AX = mybir.AxisListType.X
F32 = mybir.dt.float32
I32 = mybir.dt.int32
U32 = mybir.dt.uint32

P = 128
B, T, D = 128, 64, 1024
H, HD, R = 4, 256, 16
NA1, NA2 = 8, 64
NPAIR = B // 2
NGRP = NPAIR // 4
NBODY = NGRP // 2
NCH = D // P
NLG = 24 + R
TAU = 0.1
EPS = 1.1920929e-07
SCALE = 4.0 * float(HD) ** -0.5
CP = 16
NCHAIN = 2
NBATCH = NPAIR // (CP * NCHAIN)
HALF = 50
PER_BODY = 24
BPB = NBODY // NBATCH

C_ID, C_I2, C_MQ, C_MR, C_M8, C_M4, C_CAU, C_EYE = 0, 128, 192, 194, 196, 204, 208, 272
NCON = 288


def program(nc, io):
    with ExitStack() as ctx:
        def sb(name, shape, dt=F32):
            return ctx.enter_context(nc.sbuf_tensor(name, shape, dt))

        def sem(name, n=None):
            if n is None:
                return ctx.enter_context(nc.semaphore(name))
            return [ctx.enter_context(nc.semaphore(f"{name}{i}")) for i in range(n)]

        tab_m = nc.dram_tensor("tab_m", [NA1 * R, H * R], F32).ap()
        tab_c = nc.dram_tensor("tab_c", [NA1 * R * NA2, H * R], F32).ap()
        tab_lg = nc.dram_tensor("tab_lg", [NA2 * R, NLG], F32).ap()
        tab_av = nc.dram_tensor("tab_av", [NA1 * R, D], F32).ap()
        tab_aw = nc.dram_tensor("tab_aw", [NA2, H, R, HD], F32).ap()

        con = sb("con", [P, NCON])
        ident = con[:, C_ID:C_ID + P]
        ident2 = con[:, C_I2:C_I2 + T]
        ids = sb("ids", [1, 2 * B], I32)
        rowno = sb("rowno", [P, NGRP], I32)
        id1r = sb("id1r", [P, NGRP], I32)
        id2r = sb("id2r", [P, NGRP], I32)
        idx_m = sb("idx_m", [P, NGRP], U32)
        idx_c = sb("idx_c", [P, NGRP], U32)
        idx_l = sb("idx_l", [P, NGRP], U32)
        m_g = sb("m_g", [P, NGRP, H * R])
        c_g = sb("c_g", [P, NGRP, H * R])
        lg_g = sb("lg_g", [P, NGRP, NLG])
        o_all = sb("o_all", [P, NGRP, H * T])
        lg_all = sb("lg_all", [P, NPAIR, 24])
        ms_all = sb("ms_all", [P, NPAIR])
        u2_all = sb("u2_all", [P, NPAIR, R])
        d_all = sb("d_all", [P, NPAIR, H * 8])
        base24 = sb("base24", [P, 24])
        gate = sb("gate", [P, 6])
        eyeg = sb("eyeg", [P, 16])

        xt = sb("xt", [P, 2, 4, NCH * P])
        b2_tab = xt[:, :, :, :].rearrange("p u j c -> p (u j c)")
        bb = sb("bb", [P, 2, 4, 4, NCH * R])
        cbuf = sb("cbuf", [P, 8192])
        a2_tab = cbuf[:, :]
        ut = cbuf[:, 0:4096].rearrange("p (u j c) -> p u j c", u=2, j=4)
        t2 = cbuf[:, 4096:8192].rearrange("p (u k c) -> p u k c", u=2, k=8)
        av = sb("av", [P, 2, D])
        soft = sb("soft", [P, 2, 4, H * T])
        prob = sb("prob", [P, 2, 4, H * T])
        c_stage = soft[:, :, :, :].rearrange("p u j c -> p (u j c)")
        obd = sb("obd", [P, 2, H * P])
        ubuf = sb("ubuf", [P, 2, H * P])
        mbd = sb("mbd", [P, 2, H, P])
        cbd = sb("cbd", [P, 2, H, 4 * R])
        lbd = sb("lbd", [P, 2, 4 * NLG])
        bn1 = sb("bn1", [P, 2, P])
        bn2 = sb("bn2", [P, 2, P])
        cr = sb("cr", [P, 2, P])
        btc = sb("btc", [P, 2, P + T])
        qt = sb("qt", [P, 2, H * T])
        b2t = sb("b2t", [P, 2, P])
        gy = sb("gy", [P, 2, 4 * R])

        z24 = sb("z24", [P, NCHAIN, CP, 24])
        zz = sb("zz", [P, NCHAIN, 16 * CP])
        kr = sb("kr", [P, NCHAIN, 16 * CP])
        kc = sb("kc", [P, NCHAIN, 16 * CP])
        rho = sb("rho", [P, NCHAIN, 16 * CP])
        st = sb("st", [P, NCHAIN, 16 * CP])
        lrow = sb("lrow", [P, NCHAIN, 4 * CP])
        lcol = sb("lcol", [P, NCHAIN, 4 * CP])
        dif = sb("dif", [P, NCHAIN, 4 * CP])
        small = sb("small", [P, NCHAIN, 4 * CP])
        hp = sb("hp", [P, NCHAIN, CP, 8])
        rstd = sb("rstd", [P, NCHAIN, CP])

        ps = ctx.enter_context(nc.psum_tensor("ps", [P, 8, 512], F32))

        a1c = o_all[:, 0:4, :].rearrange("p g c -> p (g c)")
        a1qk = o_all[:, 4:8, :].rearrange("p g c -> p (g c)")
        a1v = o_all[:, 8:12, :].rearrange("p g c -> p (g c)")
        a1t = o_all[:, 12:16, :].rearrange("p g c -> p (g c)")
        wct = ubuf[:, 0, 0:NCH * 24]
        wbr = ubuf[:, 1, :]
        bvt = sb("bvt", [H, 3, HD])
        bst = sb("bst", [H, 3, HD])
        bal = sb("bal", [H, 4])
        vqc = sb("vqc", [P, 2, 2, H])
        mst = mbd[:, 0, :, :]
        c24 = mbd[0:24, :, :, :].rearrange("p u h c -> p (u h c)")
        ws = sb("ws", [P, 2, HD])
        eps_c = sb("eps_c", [P, 1])
        idx_av = sb("idx_av", [P, 2], U32)
        mout = cbd[:, 0, 0, :]
        lgs = prob[:, 0, :, :].rearrange("p j c -> p (j c)")
        lgo = prob[:, 1, :, :].rearrange("p j c -> p (j c)")

        in_con = sem("in_con"); in_ids = sem("in_ids"); in_a1 = sem("in_a1"); in_b2 = sem("in_b2")
        in_a2 = sem("in_a2"); in_w = sem("in_w"); in_bv = sem("in_bv"); in_h = sem("in_h")
        bind = sem("bind"); bind_t = sem("bind_t"); bind_c = sem("bind_c")
        a1_scaled = sem("a1_scaled"); vrow = sem("vrow"); avt_made = sem("avt_made")
        tm_mm = sem("tm_mm"); tm_mask = sem("tm_mask"); tm_made = sem("tm_made")
        tc_mm = sem("tc_mm"); tc_ev = sem("tc_ev"); tc_out = sem("tc_out")
        tl_mm = sem("tl_mm"); tl_ev = sem("tl_ev"); tl_t = sem("tl_t"); tl_ev2 = sem("tl_ev2")
        tw_mm = sem("tw_mm"); tw_ev = sem("tw_ev")
        tw_out = sem("tw_out", 2)
        tab_out = sem("tab_out"); tg_out = sem("tg_out"); gate_ok = sem("gate_ok")
        gexp = sem("gexp"); link_ok = sem("link_ok"); ix_ok = sem("ix_ok", 2)
        idx_ok = sem("idx_ok"); gathered = sem("gathered"); zeros_ok = sem("zeros_ok")

        x_in = sem("x_in", 4); bb_in = sem("bb_in", 2)
        xb_mm = sem("xb_mm", 2); bn_ok = sem("bn_ok", 2); bt_mm = sem("bt_mm", 2)
        bt_ok = sem("bt_ok", 2); q_mm = sem("q_mm", 2); q_ok = sem("q_ok", 2)
        s_mm = sem("s_mm", 2); s_abs = sem("s_abs", 2); s_e = sem("s_e", 2); s_ln = sem("s_ln", 2)
        s_min = sem("s_min", 2); s_exp = sem("s_exp", 2); p_ok = sem("p_ok", 2)
        o_mm = sem("o_mm", 2); obd_ok = sem("obd_ok", 2); oc_ok = sem("oc_ok", 2)
        c_mm = sem("c_mm", 2); cr_ok = sem("cr_ok", 2); b2_ok = sem("b2_ok", 2)
        u2_ok = sem("u2_ok", 2); b2t_mm = sem("b2t_mm", 2); b2t_ok = sem("b2t_ok", 2)
        lg_mm = sem("lg_mm", 2); lg_ok = sem("lg_ok", 2); gy_ok = sem("gy_ok", 2)
        ms_ok = sem("ms_ok", 2); bd_ok = sem("bd_ok", 2)

        k_sum = sem("k_sum", 2); k_ln = sem("k_ln", 2); k_dif = sem("k_dif", 2)
        k_rho = sem("k_rho", 2); k_m = sem("k_m", 2); k_b = sem("k_b", 2)
        k_i = sem("k_i", 2); k_ia = sem("k_ia", 2); k_f = sem("k_f", 2)
        d_ok = sem("d_ok", 2)

        t2_in = sem("t2_in", 2); av_in = sem("av_in", 2); ob_ok = sem("ob_ok", 2)
        u_ok = sem("u_ok", 2); ut_mm = sem("ut_mm", 2); ut_ok = sem("ut_ok", 2)
        f_mm = sem("f_mm", 4); f_ok = sem("f_ok", 4); out_ok = sem("out_ok", 4)

        def bc(ap, axis, shape):
            return ap.unsqueeze(axis).broadcast_to(shape)

        block = ctx.enter_context(nc.Block())

        @block.sync
        def _(sp):
            sp.dma_start(ids[:, 0:B], io["ids1"].unsqueeze(0)).then_inc(in_ids, 16)
            sp.dma_start(ids[:, B:2 * B], io["ids2"].unsqueeze(0)).then_inc(in_ids, 16)
            sp.dma_start(con[:, :], io["con"]).then_inc(in_con, 16)
            sp.dma_start(rowno[:, :], io["rowno"]).then_inc(in_con, 16)
            sp.dma_start(id1r[:, :], io["id1r"]).then_inc(in_con, 16)
            sp.dma_start(id2r[:, :], io["id2r"]).then_inc(in_con, 16)
            sp.dma_start(bvt[:, :, :], io["bv"].rearrange("k h c -> h k c")).then_inc(in_bv, 16)
            sp.dma_start(a1c, io["a1c"]).then_inc(in_a1, 16)
            sp.dma_start(a1t, io["a1t"]).then_inc(in_a1, 16)
            sp.dma_start(b2_tab.rearrange("p (i c) -> p i c", i=NA2),
                         io["b2g"].rearrange("i p c -> p i c")).then_inc(in_b2, 16)
            sp.dma_start(wct, io["wct"]).then_inc(in_w, 16)
            sp.dma_start(wbr.rearrange("p (k c) -> p k c", k=2),
                         io["w_branch"].rearrange("(k p) c -> p k c", p=P)).then_inc(in_w, 16)
            sp.dma_start(a2_tab, io["a2c"]).then_inc(in_a2, 16)
            for k, w in enumerate(("h_res", "h_pre", "h_post")):
                n0, n1 = (0, 16, 20, 24)[k:k + 2]
                sp.dma_start(base24[:, n0:n1], bass.AP(io[w].tensor, 0, [[0, P], [1, n1 - n0]])
                             ).then_inc(in_h, 16)
            sp.dma_start(gate[:, 0:1], bass.AP(io["gate"].tensor, 0, [[0, P], [1, 1]])
                         ).then_inc(in_h, 16)
            sp.wait_ge(avt_made, 2)
            sp.dma_start(tab_av, a1t).then_inc(tab_out, 16)
            sp.wait_ge(tm_made, 1)
            sp.dma_start(tab_m, mout).then_inc(tab_out, 16)
            for k in range(2):
                sp.wait_ge(tc_ev, 8 * (k + 1))
                sp.dma_start(tab_c.rearrange("(p i) c -> p i c", p=P)[:, 32 * k:32 * k + 32, :],
                             c_stage.rearrange("p (i c) -> p i c", c=H * R)).then_inc(tc_out, 16)
                sp.wait_ge(tc_out, 16 * (k + 1))
            sp.wait_ge(tl_ev2, 8)
            sp.dma_start(tab_lg.rearrange("(k p) c -> p k c", p=P)[:, :, 0:24],
                         lgo[:, 0:8 * 24].rearrange("p (k c) -> p k c", c=24)).then_inc(tg_out, 16)
            sp.wait_ge(tl_ev, 4)
            sp.dma_start(tab_lg.rearrange("(i r) c -> r i c", r=R)[:, :, 24:NLG],
                         lgs[0:R, :].rearrange("p (i c) -> p i c", c=R)).then_inc(tg_out, 16)
            sp.wait_ge(tc_mm, 16)

            def load_a(body):
                for u in range(2):
                    sp.wait_ge(xb_mm[u], body)
                    for q in range(8):
                        req = (body * 2 + u) * 8 + q
                        i1 = sp.value_load(ids[0:1, bass.ds(req, 1)], min_val=0, max_val=NA1 - 1)
                        i2 = sp.value_load(ids[0:1, bass.ds(req + B, 1)], min_val=0, max_val=NA2 - 1)
                        sp.dma_start(bb[:, u, q // 2, 2 * (q % 2), :],
                                     io["b1g"][bass.ds(i1, 1)].rearrange("i p c -> (i p) c")
                                     ).then_inc(bb_in[u], 16)
                        sp.dma_start(bb[:, u, q // 2, 2 * (q % 2) + 1, :],
                                     io["b2g"][bass.ds(i2, 1)].rearrange("i p c -> (i p) c")
                                     ).then_inc(bb_in[u], 16)
                        if q % 4 == 0:
                            k = q // 4
                            sp.dma_start(xt[:, u, 2 * k:2 * k + 2, :],
                                         io["x"][bass.ds(((body * 2 + u) * 2 + k) * 2, 2)]
                                         .rearrange("n p c -> p n c")).then_inc(x_in[2 * u + k], 16)

            sp.wait_ge(in_ids, 32)
            with sp.Fori(0, NBODY) as body:
                load_a(body)

            def load_c(u, body):
                for k in range(2):
                    sp.wait_ge(out_ok[2 * u + k], 16 * body)
                    sp.dma_start(xt[:, u, 2 * k:2 * k + 2, :],
                                 io["x"][bass.ds(((body * 2 + u) * 2 + k) * 2, 2)]
                                 .rearrange("n p c -> p n c")).then_inc(x_in[2 * u + k], 16)
                    for q in range(4 * k, 4 * k + 4):
                        req = (body * 2 + u) * 8 + q
                        i2 = sp.value_load(ids[0:1, bass.ds(req + B, 1)], min_val=0,
                                           max_val=NA2 - 1)
                        sp.dma_start(t2[0:64, u, q, :],
                                     io["a2t"][bass.ds(i2, 1)].rearrange("i k c -> (i k) c")
                                     ).then_inc(t2_in[u], 16)
                        sp.dma_start(t2[64:P, u, q, :],
                                     tab_aw[bass.ds(i2, 1)].rearrange("i j r c -> (i j r) c")
                                     ).then_inc(t2_in[u], 16)

            def store_c(u, body):
                for k in range(2):
                    for j in (2 * k, 2 * k + 1):
                        sp.wait_ge(f_ok[j], 4 * body + 2 * u + 2)
                    sp.dma_start(io["out"][bass.ds(((body * 2 + u) * 2 + k) * 2, 2)]
                                 .rearrange("n p c -> p n c"),
                                 xt[:, u, 2 * k:2 * k + 2, :]).then_inc(out_ok[2 * u + k], 16)

            for u in range(2):
                sp.wait_ge(xb_mm[u], NBODY)
            for k in range(2):
                sp.wait_ge(tw_out[k], 16 * 16)
            sp.wait_ge(tw_mm, 32)
            for u in range(2):
                load_c(u, 0)
            with sp.Fori(0, NBODY - 1) as body:
                for u in range(2):
                    store_c(u, body)
                    load_c(u, body + 1)
            for u in range(2):
                store_c(u, NBODY - 1)
            for k in range(4):
                sp.wait_ge(out_ok[k], 16 * NBODY)

        @block.tensor
        def _(pe):
            pe.wait_ge(in_con, 64)
            pe.wait_ge(bind, 1)
            for w in range(2):
                for k in range(2):
                    mm = pe.transpose(ps[:, 0, (2 * w + k) * H:(2 * w + k + 1) * H],
                                      bst[:, w, k * P:(k + 1) * P], ident[0:H, 0:H])
            mm.then_inc(bind_t, 1)
            for h in range(H):
                mm = pe.matmul(ps[:, 1 + h // 2, (h % 2) * HD:(h % 2 + 1) * HD],
                               ident[0:H, h:h + 1].broadcast_to([H, P]), bst[:, 1, :],
                               start=True, stop=True)
            mm.then_inc(vrow, 1)
            pe.wait_ge(a1_scaled, 2)
            for h in range(H):
                for k in range(2):
                    c = (2 * h + k) * P
                    mm = pe.matmul(ps[:, 3, h * P:(h + 1) * P], a1qk[:, c:c + P], a1c[:, c:c + P],
                                   start=(k == 0), stop=(k == 1))
            mm.then_inc(tm_mm, 1)
            pe.wait_ge(in_b2, 16)
            b2v = b2_tab.rearrange("p (i k r) -> p i k r", i=NA2, k=NCH)
            n = 0
            for half in range(2):
                for h in range(H):
                    for s in range(2):
                        if n >= 4:
                            pe.wait_ge(tc_ev, n - 3)
                        for k in range(2):
                            c = 2 * h + k
                            mm = pe.matmul(ps[:, 4 + n % 4, 0:HD], a1v[:, c * P:(c + 1) * P],
                                           b2v[:, 32 * half + 16 * s:32 * half + 16 * s + 16, c, :],
                                           start=(k == 0), stop=(k == 1))
                        mm.then_inc(tc_mm, 1)
                        n += 1
            pe.wait_ge(in_w, 32)
            pe.wait_ge(in_a2, 16)
            pe.wait_ge(bind_c, 1)
            pe.wait_ge(avt_made, 2)
            for s in range(2):
                for c in range(NCH):
                    mm = pe.matmul(ps[0:24, s, :], wct[:, c * 24:(c + 1) * 24],
                                   a2_tab[:, c * D + s * 512:c * D + (s + 1) * 512],
                                   start=(c == 0), stop=(c == NCH - 1))
                mm.then_inc(tl_mm, 1)
            for s in range(2):
                for i in range(32):
                    for c in range(NCH):
                        a = a2_tab[:, c * D + (s * 32 + i) * R:c * D + (s * 32 + i + 1) * R]
                        mm = pe.matmul(ps[0:R, 2 + s, i * R:(i + 1) * R], a, a,
                                       start=(c == 0), stop=(c == NCH - 1))
                mm.then_inc(tl_mm, 1)
            pe.wait_ge(tl_ev, 2)
            for k in range(8):
                mm = pe.matmul(ps[:, 0, k * 24:(k + 1) * 24],
                               c24[:, k * P:(k + 1) * P], ident[0:24, 0:24],
                               start=True, stop=True)
            mm.then_inc(tl_t, 1)
            n = 0
            for j in range(H):
                for g in range(8):
                    if n == 0:
                        pe.wait_ge(tc_ev, 16)
                    if n >= 4:
                        pe.wait_ge(tw_ev, n - 3)
                    for k in range(2):
                        c = 2 * j + k
                        mm = pe.matmul(ps[:, 4 + n % 4, 0:HD],
                                       a2_tab[:, c * D + g * P:c * D + (g + 1) * P],
                                       wbr[:, k * HD:(k + 1) * HD], start=(k == 0), stop=(k == 1))
                    mm.then_inc(tw_mm, 1)
                    n += 1

            def xb(u, body):
                for k in range(2):
                    pe.wait_ge(x_in[2 * u + k], 16 * (body + 1))
                pe.wait_ge(bb_in[u], 256 * (body + 1))
                pe.wait_ge(q_ok[u], body)
                for j in range(4):
                    for c in range(NCH):
                        mm = pe.matmul(ps[:, u, j * 64:(j + 1) * 64],
                                       xt[:, u, j, c * P:(c + 1) * P],
                                       bb[:, u, j, :, c * R:(c + 1) * R],
                                       start=(c == 0), stop=(c == NCH - 1))
                mm.then_inc(xb_mm[u], 1)

            def turn(u, body):
                pe.wait_ge(bn_ok[u], 2 * body + 2)
                pe.transpose(ps[:, u, 256:384], bn1[:, u, :], ident)
                pe.matmul(ps[:, u, 384:448], bn1[:, u, :], ident2, start=True,
                          stop=True).then_inc(bt_mm[u], 1)

            def query(u, body):
                pe.wait_ge(bt_ok[u], body + 1)
                pe.wait_ge(bd_ok[u], 3 * body + 1)
                for h in range(H):
                    mm = pe.matmul(ps[:, u, h * T:(h + 1) * T], mbd[:, u, h, :],
                                   btc[:, u, P:P + T], start=True, stop=True)
                mm.then_inc(q_mm[u], 1)

            def score(u, body):
                pe.wait_ge(q_ok[u], body + 1)
                pe.wait_ge(s_min[1 - u], 2 * body + 2 * u)
                for j in range(4):
                    pe.matmul(ps[:, 4 + j, 0:H * T], btc[32 * j:32 * j + 32, u, 0:P],
                              qt[32 * j:32 * j + 32, u, :], start=True,
                              stop=True).then_inc(s_mm[u], 1)

            def attend(u, body):
                pe.wait_ge(p_ok[u], 2 * body + 2)
                pe.wait_ge(ms_ok[u], body)
                for j in range(4):
                    pe.matmul(ps[32 * j:32 * j + 32, 2 + u, 0:H * T],
                              bn1[:, u, 32 * j:32 * j + 32], prob[:, u, j, :], start=True,
                              stop=True).then_inc(o_mm[u], 1)

            def cross(u, body):
                pe.wait_ge(obd_ok[u], body + 1)
                pe.wait_ge(oc_ok[u], body + 1)
                pe.wait_ge(bd_ok[u], 3 * body + 2)
                for h in range(H):
                    mm = pe.matmul(ps[:, 2 + u, 256:320], obd[:, u, h * P:(h + 1) * P],
                                   cbd[:, u, h, :], start=(h == 0), stop=(h == H - 1))
                mm.then_inc(c_mm[u], 1)

            def turn2(u, body):
                pe.wait_ge(b2_ok[u], body + 1)
                pe.transpose(ps[:, 2 + u, 320:448], bn2[:, u, :], ident).then_inc(b2t_mm[u], 1)

            def logit(u, body):
                pe.wait_ge(b2t_ok[u], body + 1)
                pe.wait_ge(bd_ok[u], 3 * body + 3)
                pe.matmul(ps[:, 2 + u, 0:4 * NLG], b2t[:, u, :], lbd[:, u, :], start=True,
                          stop=True).then_inc(lg_mm[u], 1)

            def body_a(body):
                xb(0, body)
                turn(0, body)
                xb(1, body)
                query(0, body)
                turn(1, body)
                score(0, body)
                query(1, body)
                attend(0, body)
                score(1, body)
                cross(0, body)
                turn2(0, body)
                logit(0, body)
                attend(1, body)
                cross(1, body)
                turn2(1, body)
                logit(1, body)

            pe.wait_ge(tl_ev2, 8)
            pe.wait_ge(tl_ev, 4)
            pe.wait_ge(tw_ev, 32)
            with pe.Fori(0, NBODY) as body:
                body_a(body)

            def turn_u(u, body):
                for j in range(4):
                    n = 4 * u + j
                    pe.wait_ge(u_ok[j % 2], 4 * body + n // 2 + 1)
                    pe.wait_ge(ut_ok[j % 2], 4 * body + n // 2)
                    for h in range(H):
                        mm = pe.transpose(ps[:, j % 2, h * P:(h + 1) * P],
                                          ubuf[:, j % 2, h * P:(h + 1) * P], ident)
                    mm.then_inc(ut_mm[j % 2], 1)

            def final(u, half, body):
                if half == 0:
                    pe.wait_ge(t2_in[u], 256 * (body + 1))
                    pe.wait_ge(av_in[u], 16 * (body + 1))
                    pe.wait_ge(ob_ok[u], body + 1)
                for j in range(4):
                    if half == 0 and j < 2:
                        pe.wait_ge(ut_ok[0], 4 * body + 2 * u + j + 1)
                        pe.wait_ge(ut_ok[1], 4 * body + 2 * u + j + 1)
                    pe.wait_ge(f_ok[j], 4 * body + 2 * u + half)
                    bank = ps[:, 4 + j, :].rearrange("p (n q t) -> p n q t", n=H, q=2)
                    mov = ut[:, u, j, :].rearrange("p (n q t) -> p n q t", n=H, q=2)
                    for q in range(2):
                        pe.matmul(bank[:, :, q, :], t2[:, u, 2 * j + q, half * P:(half + 1) * P],
                                  mov[:, :, q, :], start=(q == 0), stop=False,
                                  skip_group_check=True)
                for h in range(H):
                    for j in range(4):
                        rows = slice(32 * j, 32 * j + 32)
                        mm = pe.matmul(ps[:, 4 + j, h * P:(h + 1) * P],
                                       av[rows, u, h * HD + half * P:h * HD + (half + 1) * P],
                                       obd[rows, u, h * P:(h + 1) * P], start=False,
                                       stop=(h == H - 1), skip_group_check=True)
                        if h == H - 1:
                            mm.then_inc(f_mm[j], 1)

            def body_c(body):
                turn_u(0, body)
                final(0, 0, body)
                turn_u(1, body)
                final(0, 1, body)
                final(1, 0, body)
                final(1, 1, body)

            for u in range(2):
                pe.wait_ge(q_ok[u], NBODY)
                pe.wait_ge(s_min[u], 2 * NBODY)
            with pe.Fori(0, NBODY) as body:
                body_c(body)

        @block.scalar
        def _(act):
            act.preload_act_table_set("natural_log_exp_and_others")
            act.wait_ge(in_h, 64)
            act.activation(gate[:, 1:2], gate[:, 0:1], ACT.Abs).then_inc(gexp, 1)
            act.wait_ge(gexp, 1)
            act.activation(gate[:, 2:3], gate[:, 1:2], ACT.Exp, scale=-1.0).then_inc(gexp, 1)
            for n in range(16):
                act.wait_ge(tc_mm, n + 1)
                half, h, s = n // 8, (n // 2) % 4, n % 2
                if n == 8:
                    act.wait_ge(tc_out, 16)
                dst = c_stage.rearrange("p (i h r) -> p i h r", h=H, r=R)[:, 16 * s:16 * s + 16, h, :]
                act.activation(dst, ps[:, 4 + n % 4, 0:HD].rearrange("p (i r) -> p i r", r=R),
                               ACT.Copy).then_inc(tc_ev, 1)
            for s in range(2):
                act.wait_ge(tl_mm, s + 1)
                act.activation(c24[:, s * 512:(s + 1) * 512], ps[0:24, s, :], ACT.Copy
                               ).then_inc(tl_ev, 1)
            for s in range(2):
                act.wait_ge(tl_mm, s + 3)
                act.activation(lgs[0:R, s * 512:(s + 1) * 512], ps[0:R, 2 + s, :], ACT.Copy
                               ).then_inc(tl_ev, 1)
            act.wait_ge(tl_t, 1)
            for k in range(8):
                act.activation(lgo[:, k * 24:(k + 1) * 24], ps[:, 0, k * 24:(k + 1) * 24],
                               ACT.Copy).then_inc(tl_ev2, 1)
            for n in range(32):
                j, g = n // 8, n % 8
                act.wait_ge(tw_mm, n + 1)
                if n >= 2:
                    act.wait_ge(tw_out[n % 2], 16 * (n // 2))
                act.activation(ws[:, n % 2, :], ps[:, 4 + n % 4, 0:HD], ACT.Copy).then_inc(tw_ev, 1)
                act.wait_ge(tw_ev, n + 1)
                act.dma_start(tab_aw[8 * g:8 * g + 8, j].rearrange("i r c -> i r c"),
                              ws[:, n % 2, :]).then_inc(tw_out[n % 2], 16)

            def turned(u, body):
                act.wait_ge(bt_mm[u], body + 1)
                act.activation(btc[:, u, :], ps[:, u, 256:448], ACT.Copy).then_inc(bt_ok[u], 1)

            def query(u, body):
                act.wait_ge(q_mm[u], body + 1)
                act.activation(qt[:, u, :], ps[:, u, 0:256], ACT.Copy).then_inc(q_ok[u], 1)

            def sigmoid(u, k, body):
                act.wait_ge(s_mm[u], 4 * body + 2 * k + 2)
                w = soft[:, u, 2 * k:2 * k + 2, :]
                e = 2 * body + k + 1
                act.activation(w, ps[:, 4 + 2 * k:6 + 2 * k, 0:H * T], ACT.Abs).then_inc(s_abs[u], 1)
                act.wait_ge(s_abs[u], e)
                act.activation(w, w, ACT.Exp, scale=-1.0).then_inc(s_e[u], 1)
                act.wait_ge(s_e[u], e)
                act.activation(w, w, ACT.Ln, bias=1.0).then_inc(s_ln[u], 1)

            def weight(u, k, body):
                e = 2 * body + k + 1
                act.wait_ge(s_min[u], e)
                w = prob[:, u, 2 * k:2 * k + 2, :]
                act.activation(w, w, ACT.Exp).then_inc(s_exp[u], 1)

            def keep_o(u, body):
                act.wait_ge(o_mm[u], 4 * body + 4)
                act.wait_ge(obd_ok[u], body + 1)
                act.activation(o_all[:, bass.ds(2 * body + u, 1), :],
                               ps[:, 2 + u, 0:H * T].unsqueeze(1), ACT.Copy).then_inc(oc_ok[u], 1)

            def turned2(u, body):
                act.wait_ge(b2t_mm[u], body + 1)
                act.activation(b2t[:, u, :], ps[:, 2 + u, 320:448], ACT.Copy).then_inc(b2t_ok[u], 1)

            def sums(c):
                return st[:, c, :].rearrange("p (t j k) -> p t j k", j=4, k=4)[:, :, :, 3]

            def k_ratio(c, n, batch):
                act.wait_ge(k_dif[c], batch * 99 + n + 1)
                act.activation(rho[:, c, :].rearrange("p (t i j) -> p t i j", i=4, j=4)[:, :, :, 1:4],
                               dif[:, c, 0:3 * CP].rearrange("p (t j) -> p t j", j=3)
                               .unsqueeze(2).broadcast_to([P, CP, 4, 3]), ACT.Exp
                               ).then_inc(k_rho[c], 1)

            def k_steps(m0, m1, nb, batch):
                for m in range(m0, m1):
                    for c in range(NCHAIN):
                        act.wait_ge(k_sum[c], batch * 99 + nb + m + 1)
                        act.activation((lcol if m % 2 == 0 else lrow)[:, c, :]
                                       .rearrange("p (t j) -> p t j", j=4), sums(c), ACT.Ln
                                       ).then_inc(k_ln[c], 1)
                    for c in range(NCHAIN):
                        k_ratio(c, nb + m, batch)

            def k_matrix(c, done):
                z = zz[:, c, :].rearrange("p (t i j) -> p t j i", i=4, j=4)
                act.activation(kc[:, c, :].rearrange("p (t j i) -> p t j i", i=4, j=4), z, ACT.Exp)
                act.activation(kr[:, c, :], zz[:, c, :], ACT.Exp).then_inc(done[c], 1)

            def k_start(batch):
                for u in range(2):
                    act.wait_ge(ms_ok[u], (batch + 1) * BPB)
                act.wait_ge(zeros_ok, 3)
                for c in range(NCHAIN):
                    p0 = (batch * NCHAIN + c) * CP
                    act.activation(rstd[:, c, :], ms_all[:, p0:p0 + CP], ACT.Ln, scale=1.0 / D,
                                   bias=eps_c[:, 0:1]).then_inc(k_ia[c], 1)
                    act.wait_ge(k_ia[c], batch * 4 + 1)
                    act.activation(rstd[:, c, :], rstd[:, c, :], ACT.Exp, scale=-0.5
                                   ).then_inc(k_ia[c], 1)
                for c in range(NCHAIN):
                    act.wait_ge(k_i[c], batch * 12 + 5)
                    act.activation(st[:, c, :], zz[:, c, :], ACT.Exp).then_inc(k_ia[c], 1)
                    act.wait_ge(k_i[c], batch * 12 + 7)
                    act.activation(hp[:, c, :, :], hp[:, c, :, :], ACT.Exp).then_inc(k_ia[c], 1)
                for c in range(NCHAIN):
                    act.wait_ge(k_i[c], batch * 12 + 9)
                    k_matrix(c, k_m)
                    act.wait_ge(k_sum[c], batch * 99 + 1)
                    act.activation(lrow[:, c, :], small[:, c, :], ACT.Ln).then_inc(k_ln[c], 1)
                    k_ratio(c, 0, batch)

            def k_middle(batch):
                for c in range(NCHAIN):
                    act.wait_ge(k_sum[c], batch * 99 + HALF)
                    act.activation(lcol[:, c, :].rearrange("p (t j) -> p t j", j=4),
                                   sums(c), ACT.Ln
                                   ).then_inc(k_ln[c], 1)
                for c in range(NCHAIN):
                    act.wait_ge(k_dif[c], batch * 99 + HALF)
                    k_matrix(c, k_rho)
                for c in range(NCHAIN):
                    act.wait_ge(k_sum[c], batch * 99 + HALF + 1)
                    act.activation(lrow[:, c, :], small[:, c, :], ACT.Ln).then_inc(k_ln[c], 1)
                    k_ratio(c, HALF, batch)

            def body_a(body, nb=None, batch=0):
                def k(m0, m1):
                    if nb is not None:
                        k_steps(m0, m1, nb, batch)
                k(0, 2)
                turned(0, body)
                k(2, 4)
                query(0, body)
                k(4, 6)
                turned(1, body)
                sigmoid(0, 0, body)
                k(6, 7)
                sigmoid(0, 1, body)
                k(7, 8)
                query(1, body)
                k(8, 9)
                weight(0, 0, body)
                k(9, 10)
                weight(0, 1, body)
                k(10, 12)
                keep_o(0, body)
                k(12, 13)
                sigmoid(1, 0, body)
                k(13, 14)
                sigmoid(1, 1, body)
                k(14, 15)
                turned2(0, body)
                weight(1, 0, body)
                k(15, 17)
                weight(1, 1, body)
                k(17, 20)
                keep_o(1, body)
                k(20, 22)
                turned2(1, body)
                k(22, 24)

            def turned_u(u, j, body):
                b, n = j % 2, 4 * u + j
                act.wait_ge(ut_mm[b], 4 * body + n // 2 + 1)
                act.wait_ge(f_mm[j], 4 * body)
                act.activation(ut[:, u, j, :], ps[:, b, :], ACT.Copy).then_inc(ut_ok[b], 1)

            def body_c(body, nb=None, batch=0):
                def k(m0, m1):
                    if nb is not None:
                        k_steps(m0, m1, nb, batch)
                turned_u(0, 0, body)
                turned_u(0, 1, body)
                k(0, 2)
                turned_u(0, 2, body)
                k(2, 4)
                turned_u(0, 3, body)
                k(4, 8)
                turned_u(1, 0, body)
                k(8, 10)
                turned_u(1, 1, body)
                k(10, 14)
                turned_u(1, 2, body)
                k(14, 16)
                turned_u(1, 3, body)
                k(16, 24)

            with act.Fori(0, BPB) as i:
                body_a(i)
            k_start(0)
            for part in range(2):
                with act.Fori(0, 2) as i:
                    body_a(BPB + 2 * part + i, HALF * part + 1 + i * PER_BODY, 0)
                if part == 0:
                    k_middle(0)
            k_start(1)
            for part in range(2):
                with act.Fori(0, 2) as i:
                    body_c(2 * part + i, HALF * part + 1 + i * PER_BODY, 1)
                if part == 0:
                    k_middle(1)
            with act.Fori(0, BPB) as i:
                body_c(BPB + i)

        @block.vector
        def _(dve):
            nc.vector.memset(rho[:, :, :], 0.0).then_inc(zeros_ok, 1)
            nc.vector.memset(eps_c[:, :], EPS).then_inc(zeros_ok, 1)
            nc.vector.memset(bal[:, :], 0.0).then_inc(zeros_ok, 1)
            n_link = [0]

            def link(ins):
                n_link[0] += 1
                ins.then_inc(link_ok, 1)
                dve.wait_ge(link_ok, n_link[0])

            dve.wait_ge(zeros_ok, 3)
            dve.wait_ge(in_bv, 16)
            link(dve.scalar_tensor_tensor(out=bst[:, :, :], in0=bvt[:, :, :], scalar=-1.0,
                                          in1=bvt[:, :, :], op0=ALU.mult, op1=ALU.max))
            link(dve.tensor_reduce(bal[:, 0:3], bst[:, :, :], AX, ALU.add))
            link(dve.tensor_scalar(bal[:, 0:3], bal[:, 0:3], 1.0 / HD, None, ALU.mult))
            link(dve.tensor_scalar(bst[:, :, :], bvt[:, :, :], 0.0, 2.0, ALU.is_ge, ALU.mult))
            link(dve.tensor_tensor(bst[:, :, :], bst[:, :, :], bc(bal[:, 0:3], 2, [H, 3, HD]),
                                   ALU.mult))
            link(dve.tensor_tensor(bst[:, :, :], bst[:, :, :], bc(bal[:, 0:3], 2, [H, 3, HD]),
                                   ALU.subtract))
            link(dve.tensor_tensor(bst[:, :, :], bst[:, :, :], bvt[:, :, :], ALU.subtract))
            link(dve.tensor_tensor(bst[:, :, :], bst[:, :, :], bvt[:, :, :], ALU.add))
            link(dve.tensor_tensor(bst[:, 0, :], bst[:, 0, :], bst[:, 1, :], ALU.mult))
            dve.tensor_copy(bst[:, 1, :], bst[:, 2, :]).then_inc(bind, 1)
            dve.wait_ge(bind_t, 1)
            turned = ps[:, 0, 0:16].rearrange("p (w k h) -> p w k h", w=2, k=2)
            dve.tensor_scalar(vqc[:, 0, :, :], turned[:, 0, :, :], SCALE, None, ALU.mult)
            link(dve.tensor_copy(vqc[:, 1, :, :], turned[:, 1, :, :]))
            dve.engine_nop().then_inc(bind_c, 1)
            dve.wait_ge(in_a1, 32)
            for w, dst in enumerate((a1qk, a1v)):
                dve.tensor_tensor(dst.rearrange("p (h k c) -> p h k c", h=H, k=2),
                                  a1c.rearrange("p (h k c) -> p h k c", h=H, k=2),
                                  bc(vqc[:, w, :, :].rearrange("p k h -> p h k"), 3, [P, H, 2, P]),
                                  ALU.mult).then_inc(a1_scaled, 1)
            dve.wait_ge(vrow, 1)
            for k in range(2):
                dve.tensor_tensor(a1t[:, 512 * k:512 * k + 512], a1t[:, 512 * k:512 * k + 512],
                                  ps[:, 1 + k, :], ALU.mult).then_inc(avt_made, 1)
            dve.wait_ge(tm_mm, 1)
            dve.wait_ge(in_con, 64)
            link(dve.tensor_tensor(mst.rearrange("p h (i r) -> p h i r", r=R),
                                   ps[:, 3, :].rearrange("p (h i r) -> p h i r", h=H, r=R),
                                   con[:, C_M8:C_M8 + 8].unsqueeze(1).unsqueeze(3)
                                   .broadcast_to([P, H, 8, R]), ALU.mult))
            dve.tensor_reduce(mout.rearrange("p (h r) -> p h r", h=H),
                              mst.rearrange("p h (i r) -> p h r i", r=R), AX, ALU.add
                              ).then_inc(tm_made, 1)
            link(dve.scalar_tensor_tensor(out=idx_m[:, :], in0=id1r[:, :], scalar=float(R),
                                          in1=rowno[:, :], op0=ALU.mult, op1=ALU.add))
            dve.scalar_tensor_tensor(out=idx_c[:, :], in0=idx_m[:, :], scalar=float(NA2),
                                     in1=id2r[:, :], op0=ALU.mult, op1=ALU.add
                                     ).then_inc(idx_ok, 1)
            dve.scalar_tensor_tensor(out=idx_l[:, :], in0=id2r[:, :], scalar=float(R),
                                     in1=rowno[:, :], op0=ALU.mult, op1=ALU.add
                                     ).then_inc(idx_ok, 1)
            dve.wait_ge(gexp, 2)
            link(dve.tensor_scalar(gate[:, 3:4], gate[:, 2:3], 1.0, None, ALU.add))
            link(dve.reciprocal(gate[:, 4:5], gate[:, 3:4]))
            link(dve.tensor_scalar(gate[:, 1:2], gate[:, 0:1], 0.0, None, ALU.is_ge))
            link(dve.tensor_tensor(gate[:, 5:6], gate[:, 1:2], gate[:, 2:3], ALU.mult))
            link(dve.tensor_tensor(gate[:, 3:4], gate[:, 1:2], gate[:, 2:3], ALU.add))
            link(dve.tensor_tensor(gate[:, 3:4], gate[:, 3:4], gate[:, 5:6], ALU.subtract))
            link(dve.tensor_tensor(gate[:, 3:4], gate[:, 3:4], gate[:, 4:5], ALU.mult))
            link(dve.tensor_tensor(gate[:, 5:6], gate[:, 5:6], gate[:, 1:2], ALU.subtract))
            link(dve.tensor_scalar(gate[:, 5:6], gate[:, 5:6], 1.0, None, ALU.add))
            link(dve.tensor_tensor(gate[:, 5:6], gate[:, 5:6], gate[:, 4:5], ALU.mult))
            link(dve.tensor_scalar(eyeg[:, :], con[:, C_EYE:C_EYE + 16], gate[:, 5:6], None,
                                   ALU.mult))

            mq = con[:, C_MQ:C_MQ + 2].unsqueeze(1).unsqueeze(3).broadcast_to([P, 4, 2, R])

            def split(u, body):
                dve.wait_ge(xb_mm[u], body + 1)
                v = ps[:, u, 0:256].rearrange("p (j q w r) -> p w j q r", q=2, w=2, r=R)
                for w, dst in enumerate((bn1, bn2)):
                    if w == 0:
                        dve.wait_ge(o_mm[u], 4 * body)
                    else:
                        dve.wait_ge(b2t_mm[u], body)
                    dve.tensor_tensor(dst[:, u, :].rearrange("p (j q r) -> p j q r", q=2, r=R),
                                      v[:, w], mq, ALU.mult).then_inc(bn_ok[u], 1)

            def minus(u, k, body):
                dve.wait_ge(s_ln[u], 2 * body + k + 1)
                dve.scalar_tensor_tensor(out=prob[:, u, 2 * k:2 * k + 2, :],
                                         in0=ps[:, 4 + 2 * k:6 + 2 * k, 0:H * T], scalar=0.0,
                                         in1=soft[:, u, 2 * k:2 * k + 2, :], op0=ALU.min,
                                         op1=ALU.subtract).then_inc(s_min[u], 1)

            def diag_o(u, body):
                dve.wait_ge(o_mm[u], 4 * body + 4)
                dve.wait_ge(c_mm[u], body)
                dve.tensor_tensor(obd[:, u, :].rearrange("p (h q t) -> p h q t", h=H, q=2),
                                  bc(ps[:, 2 + u, 0:256].rearrange("p (h t) -> p h t", h=H), 2,
                                     [P, H, 2, T]),
                                  con[:, C_MR:C_MR + 2].unsqueeze(1).unsqueeze(3)
                                  .broadcast_to([P, H, 2, T]), ALU.mult).then_inc(obd_ok[u], 1)

            def u2(u, body):
                dve.wait_ge(c_mm[u], body + 1)
                dve.tensor_tensor(cr[:, u, :].rearrange("p (j q r) -> p j q r", q=2, r=R),
                                  bc(ps[:, 2 + u, 256:320].rearrange("p (j r) -> p j r", r=R), 2,
                                     [P, 4, 2, R]), mq, ALU.mult).then_inc(cr_ok[u], 1)
                dve.wait_ge(cr_ok[u], body + 1)
                dve.tensor_tensor(bn2[:, u, :], bn2[:, u, :], cr[:, u, :], ALU.add
                                  ).then_inc(b2_ok[u], 1)
                dve.wait_ge(b2_ok[u], body + 1)
                v = bn2[:, u, :].rearrange("p (j q r) -> p j q r", q=2, r=R)
                dve.tensor_tensor(u2_all[:, bass.ds((2 * body + u) * 4, 4), :], v[:, :, 0, :],
                                  v[:, :, 1, :], ALU.add).then_inc(u2_ok[u], 1)

            def logits(u, body):
                dve.wait_ge(lg_mm[u], body + 1)
                v = ps[:, 2 + u, 0:4 * NLG].rearrange("p (j c) -> p j c", c=NLG)
                dve.tensor_copy(lg_all[:, bass.ds((2 * body + u) * 4, 4), :], v[:, :, 0:24])
                dve.wait_ge(u2_ok[u], body + 1)
                dve.wait_ge(ms_ok[u], body)
                g = gy[:, u, :].rearrange("p (j r) -> p j r", r=R)
                dve.tensor_tensor(g, v[:, :, 24:NLG], u2_all[:, bass.ds((2 * body + u) * 4, 4), :],
                                  ALU.mult).then_inc(gy_ok[u], 1)
                dve.wait_ge(gy_ok[u], body + 1)
                dve.tensor_reduce(ms_all[:, bass.ds((2 * body + u) * 4, 4)], g, AX, ALU.add
                                  ).then_inc(ms_ok[u], 1)

            def k_diff(c, n, batch, row):
                dve.wait_ge(k_ln[c], batch * 99 + n + 1)
                src = (lrow if row else lcol)[:, c, :].rearrange("p (t j) -> p t j", j=4)
                dve.tensor_tensor(dif[:, c, 0:3 * CP].rearrange("p (t j) -> p t j", j=3),
                                  src[:, :, 1:4], src[:, :, 0:3], ALU.subtract
                                  ).then_inc(k_dif[c], 1)

            def k_scan(c, n, batch, row):
                dve.wait_ge(k_rho[c], batch * 99 + n)
                dve.tensor_tensor_scan(st[:, c, :], rho[:, c, :], (kr if row else kc)[:, c, :],
                                       0.0, ALU.mult, ALU.add).then_inc(k_sum[c], 1)

            def k_steps(m0, m1, nb, batch):
                for m in range(m0, m1):
                    for c in range(NCHAIN):
                        k_scan(c, nb + m, batch, m % 2 == 1)
                    for c in range(NCHAIN):
                        k_diff(c, nb + m, batch, m % 2 == 1)

            def k_start(batch):
                for c in range(NCHAIN):
                    p0 = (batch * NCHAIN + c) * CP
                    e = batch * 12
                    z = z24[:, c, :, :]
                    z4 = zz[:, c, :].rearrange("p (t i j) -> p t i j", i=4, j=4)
                    s4 = small[:, c, :].rearrange("p (t i) -> p t i", i=4)
                    d4 = dif[:, c, :].rearrange("p (t i) -> p t i", i=4)
                    h4 = hp[:, c, :, :].rearrange("p t (w j) -> p t w j", w=2)
                    s2 = lrow[:, c, 0:2 * CP].rearrange("p (t w) -> p t w", w=2)
                    dve.wait_ge(k_ia[c], batch * 4 + 2)
                    for u in range(2):
                        dve.wait_ge(ms_ok[u], (batch + 1) * BPB)
                    dve.tensor_tensor(z, lg_all[:, p0:p0 + CP, :],
                                      bc(rstd[:, c, :], 2, [P, CP, 24]), ALU.mult
                                      ).then_inc(k_i[c], 1)
                    dve.wait_ge(k_i[c], e + 1)
                    dve.tensor_tensor(z, z, bc(base24[:, :], 1, [P, CP, 24]), ALU.add
                                      ).then_inc(k_i[c], 1)
                    dve.wait_ge(k_i[c], e + 2)
                    dve.tensor_scalar(zz[:, c, :].rearrange("p (t i) -> p t i", i=16),
                                      z[:, :, 0:16], 1.0 / TAU, None, ALU.mult
                                      ).then_inc(k_i[c], 1)
                    dve.wait_ge(k_i[c], e + 3)
                    dve.tensor_reduce(s4, z4, AX, ALU.max).then_inc(k_i[c], 1)
                    dve.wait_ge(k_i[c], e + 4)
                    dve.tensor_tensor(z4, z4, bc(s4, 3, [P, CP, 4, 4]), ALU.subtract
                                      ).then_inc(k_i[c], 1)
                    dve.tensor_reduce(s2, z[:, :, 16:24].rearrange("p t (w j) -> p t w j", w=2), AX,
                                      ALU.max).then_inc(k_i[c], 1)
                    dve.wait_ge(k_i[c], e + 6)
                    dve.tensor_tensor(h4, z[:, :, 16:24].rearrange("p t (w j) -> p t w j", w=2),
                                      bc(s2, 3, [P, CP, 2, 4]), ALU.subtract).then_inc(k_i[c], 1)
                    dve.tensor_reduce(d4, z4.rearrange("p t i j -> p t j i"), AX, ALU.max
                                      ).then_inc(k_i[c], 1)
                    dve.wait_ge(k_i[c], e + 8)
                    dve.wait_ge(k_ia[c], batch * 4 + 3)
                    dve.tensor_tensor(z4, z4, bc(d4, 2, [P, CP, 4, 4]), ALU.subtract
                                      ).then_inc(k_i[c], 1)
                    dve.tensor_reduce(s4, st[:, c, :].rearrange("p (t i j) -> p t i j", i=4, j=4),
                                      AX, ALU.add).then_inc(k_sum[c], 1)
                    dve.wait_ge(k_ia[c], batch * 4 + 4)
                    dve.tensor_reduce(s2, h4, AX, ALU.add).then_inc(k_i[c], 1)
                    dve.wait_ge(k_i[c], e + 10)
                    dve.reciprocal(s2, s2).then_inc(k_i[c], 1)
                    dve.wait_ge(k_i[c], e + 11)
                    dve.tensor_tensor(h4, h4, bc(s2, 3, [P, CP, 2, 4]), ALU.mult
                                      ).then_inc(k_i[c], 1)
                for c in range(NCHAIN):
                    dve.wait_ge(k_i[c], batch * 12 + 12)
                    k_diff(c, 0, batch, True)
                    dve.wait_ge(k_m[c], batch + 1)

            def k_middle(batch):
                for c in range(NCHAIN):
                    k_scan(c, HALF - 1, batch, False)
                for c in range(NCHAIN):
                    l4 = lrow[:, c, :].rearrange("p (t i) -> p t i", i=4)
                    s4 = small[:, c, :].rearrange("p (t i) -> p t i", i=4)
                    z4 = zz[:, c, :].rearrange("p (t i j) -> p t i j", i=4, j=4)
                    dve.tensor_tensor(s4, l4[:, :, 3:4].broadcast_to([P, CP, 4]), l4, ALU.subtract
                                      ).then_inc(k_b[c], 1)
                    dve.wait_ge(k_b[c], 2 * batch + 1)
                    dve.tensor_tensor(z4, z4, bc(s4, 3, [P, CP, 4, 4]), ALU.add).then_inc(k_b[c], 1)
                    dve.wait_ge(k_b[c], 2 * batch + 2)
                    dve.wait_ge(k_ln[c], batch * 99 + HALF)
                    dve.tensor_tensor(z4, z4, bc(lcol[:, c, :].rearrange("p (t j) -> p t j", j=4), 2,
                                                 [P, CP, 4, 4]), ALU.subtract).then_inc(k_dif[c], 1)
                for c in range(NCHAIN):
                    dve.wait_ge(k_rho[c], batch * 99 + HALF)
                    dve.tensor_reduce(small[:, c, :].rearrange("p (t i) -> p t i", i=4),
                                      kr[:, c, :].rearrange("p (t i j) -> p t i j", i=4, j=4), AX,
                                      ALU.add).then_inc(k_sum[c], 1)
                    k_diff(c, HALF, batch, True)

            def k_final(batch):
                for c in range(NCHAIN):
                    e = batch * 5
                    p0 = (batch * NCHAIN + c) * CP
                    s4 = small[:, c, :].rearrange("p (t i) -> p t i", i=4)
                    d4 = dif[:, c, :].rearrange("p (t i) -> p t i", i=4)
                    t4 = st[:, c, :].rearrange("p (t i j) -> p t i j", i=4, j=4)
                    k4 = kr[:, c, :].rearrange("p (t i j) -> p t i j", i=4, j=4)
                    dve.wait_ge(k_rho[c], batch * 99 + 99)
                    dve.reciprocal(s4, t4[:, :, :, 3]).then_inc(k_f[c], 1)
                    dve.wait_ge(k_f[c], e + 1)
                    dve.tensor_tensor(t4, k4, bc(s4, 3, [P, CP, 4, 4]), ALU.mult
                                      ).then_inc(k_f[c], 1)
                    dve.wait_ge(k_f[c], e + 2)
                    dve.tensor_reduce(d4, t4.rearrange("p t i j -> p t j i"), AX, ALU.add
                                      ).then_inc(k_f[c], 1)
                    dve.wait_ge(k_f[c], e + 3)
                    dve.reciprocal(s4, d4).then_inc(k_f[c], 1)
                    dve.wait_ge(k_f[c], e + 4)
                    dve.tensor_tensor(t4, t4, bc(s4, 2, [P, CP, 4, 4]), ALU.mult
                                      ).then_inc(k_f[c], 1)
                    dve.wait_ge(k_f[c], e + 5)
                    dd = d_all[:, p0:p0 + CP, :].rearrange("p t (n w j) -> p t n w j", n=4, w=2)
                    dve.scalar_tensor_tensor(
                        out=dd[:, :, :, 0, :].rearrange("p t n j -> p t n j"),
                        in0=t4, scalar=gate[:, 3:4],
                        in1=bc(eyeg[:, :].rearrange("p (i j) -> p i j", i=4), 1, [P, CP, 4, 4]),
                        op0=ALU.mult, op1=ALU.add).then_inc(d_ok[c], 1)
                    dve.tensor_tensor(dd[:, :, :, 1, :],
                                      bc(hp[:, c, :, 4:8], 3, [P, CP, 4, 4]),
                                      bc(hp[:, c, :, 0:4], 2, [P, CP, 4, 4]), ALU.mult
                                      ).then_inc(d_ok[c], 1)
                for c in range(NCHAIN):
                    dve.wait_ge(d_ok[c], 2 * batch + 2)

            def body_a(body, nb=None, batch=0):
                def k(m0, m1):
                    if nb is not None:
                        k_steps(m0, m1, nb, batch)
                k(0, 2)
                split(0, body)
                k(2, 4)
                split(1, body)
                k(4, 8)
                minus(0, 0, body)
                k(8, 9)
                minus(0, 1, body)
                k(9, 12)
                diag_o(0, body)
                k(12, 14)
                u2(0, body)
                k(14, 15)
                minus(1, 0, body)
                k(15, 16)
                minus(1, 1, body)
                k(16, 18)
                logits(0, body)
                k(18, 20)
                diag_o(1, body)
                k(20, 22)
                u2(1, body)
                k(22, 24)
                logits(1, body)

            def add(u, half, j, body):
                dve.wait_ge(f_mm[j], 4 * body + 2 * u + half + 1)
                if half == 0:
                    dve.wait_ge(x_in[2 * u + j // 2], 16 * (NBODY + body + 1))
                v = xt[:, u, j, :].rearrange("p (n k c) -> p n k c", n=H, k=2)[:, :, half, :]
                dve.tensor_tensor(v, v, ps[:, 4 + j, :].rearrange("p (n c) -> p n c", n=H), ALU.add
                                  ).then_inc(f_ok[j], 1)

            def body_c(body, nb=None, batch=0):
                def k(m0, m1):
                    if nb is not None:
                        k_steps(m0, m1, nb, batch)
                for u in range(2):
                    k(12 * u, 12 * u + 6)
                    for n in range(8):
                        add(u, n // 4, n % 4, body)
                        if n < 6:
                            k(12 * u + 6 + n, 12 * u + 7 + n)

            with dve.Fori(0, BPB) as i:
                body_a(i)
            k_start(0)
            for part in range(2):
                with dve.Fori(0, 2) as i:
                    body_a(BPB + 2 * part + i, HALF * part + 1 + i * PER_BODY, 0)
                if part == 0:
                    k_middle(0)
            k_final(0)
            k_start(1)
            for part in range(2):
                with dve.Fori(0, 2) as i:
                    body_c(2 * part + i, HALF * part + 1 + i * PER_BODY, 1)
                if part == 0:
                    k_middle(1)
            k_final(1)
            with dve.Fori(0, BPB) as i:
                body_c(BPB + i)

        @block.gpsimd
        def _(pool):
            pool.wait_ge(idx_ok, 2)
            pool.wait_ge(tab_out, 32)
            pool.wait_ge(tc_out, 32)
            pool.wait_ge(tg_out, 32)
            for g in range(NGRP):
                for dst, tab, idx in ((m_g, tab_m, idx_m), (c_g, tab_c, idx_c),
                                      (lg_g, tab_lg, idx_l)):
                    pool.indirect_dma_start(dst[:, g, :], None, tab,
                                            bass.IndirectOffsetOnAxis(idx[:, g:g + 1], 0)
                                            ).then_inc(gathered, 16)
            pool.wait_ge(gathered, 48 * NGRP)
            m8 = con[:, C_M8:C_M8 + 8]
            m4 = con[:, C_M4:C_M4 + 4]

            def spread(u, body):
                g = bass.ds(2 * body + u, 1)
                pool.wait_ge(q_mm[u], body)
                pool.tensor_tensor(mbd[:, u, :, :].rearrange("p h (k r) -> p h k r", r=R),
                                   bc(m_g[:, g, :].rearrange("p g (h r) -> p (g h) r", r=R), 2,
                                      [P, H, 8, R]),
                                   m8.unsqueeze(1).unsqueeze(3).broadcast_to([P, H, 8, R]),
                                   ALU.mult).then_inc(bd_ok[u], 1)
                pool.wait_ge(c_mm[u], body)
                pool.tensor_tensor(cbd[:, u, :, :].rearrange("p h (j r) -> p h j r", r=R),
                                   bc(c_g[:, g, :].rearrange("p g (h r) -> p (g h) r", r=R), 2,
                                      [P, H, 4, R]),
                                   m4.unsqueeze(1).unsqueeze(3).broadcast_to([P, H, 4, R]),
                                   ALU.mult).then_inc(bd_ok[u], 1)
                pool.wait_ge(lg_mm[u], body)
                pool.tensor_tensor(lbd[:, u, :].rearrange("p (j c) -> p j c", c=NLG),
                                   lg_g[:, g, :].broadcast_to([P, 4, NLG]),
                                   bc(m4, 2, [P, 4, NLG]), ALU.mult).then_inc(bd_ok[u], 1)

            def mask(u, k, body):
                pool.wait_ge(s_exp[u], 2 * body + k + 1)
                v = prob[:, u, 2 * k:2 * k + 2, :].rearrange("p j (h t) -> p (j h) t", h=H)
                pool.tensor_tensor(v, v, bc(con[:, C_CAU:C_CAU + T], 1, [P, 2 * H, T]), ALU.mult
                                   ).then_inc(p_ok[u], 1)

            with pool.Fori(0, NBODY) as body:
                spread(0, body)
                spread(1, body)
                for u in range(2):
                    for k in range(2):
                        mask(u, k, body)

            def attn_rows(u, body):
                g = bass.ds(2 * body + u, 1)
                pool.wait_ge(f_mm[3], 4 * body)
                pool.wait_ge(av_in[u], 16 * body)
                pool.tensor_copy(idx_av[:, u:u + 1], idx_m[:, g]).then_inc(ix_ok[u], 1)
                pool.wait_ge(ix_ok[u], body + 1)
                pool.tensor_tensor(obd[:, u, :].rearrange("p (h q t) -> p h q t", h=H, q=2),
                                   bc(o_all[:, g, :].rearrange("p g (h t) -> p (g h) t", h=H), 2,
                                      [P, H, 2, T]),
                                   con[:, C_MR:C_MR + 2].unsqueeze(1).unsqueeze(3)
                                   .broadcast_to([P, H, 2, T]), ALU.mult).then_inc(ob_ok[u], 1)
                pool.indirect_dma_start(av[:, u, :], None, tab_av,
                                        bass.IndirectOffsetOnAxis(idx_av[:, u:u + 1], 0)
                                        ).then_inc(av_in[u], 16)

            def spread_u2(u, j, body):
                b, n = j % 2, 4 * u + j
                pair = bass.ds((2 * body + u) * 4 + j, 1)
                pool.wait_ge(ut_mm[b], 4 * body + n // 2)
                pool.tensor_tensor(ubuf[:, b, :].rearrange("p (k r) -> p k r", r=R),
                                   bc(d_all[:, pair, :].rearrange("p g k -> p (g k)"), 2,
                                      [P, 32, R]),
                                   u2_all[:, pair, :].broadcast_to([P, 32, R]), ALU.mult
                                   ).then_inc(u_ok[b], 1)

            for u in range(2):
                pool.wait_ge(c_mm[u], NBODY)
                pool.wait_ge(oc_ok[u], NBODY)
                pool.wait_ge(u2_ok[u], NBODY)
            for batch in range(NBATCH):
                for c in range(NCHAIN):
                    pool.wait_ge(d_ok[c], 2 * (batch + 1))
                with pool.Fori(0, BPB) as i:
                    body = batch * BPB + i
                    for u in range(2):
                        attn_rows(u, body)
                        for j in range(4):
                            spread_u2(u, j, body)


def constants():
    import numpy as np
    p = np.arange(P)
    con = np.zeros((P, NCON), np.float32)
    con[:, C_ID:C_ID + P] = np.eye(P)
    con[:, C_I2:C_I2 + T] = (p[:, None] % T) == np.arange(T)
    con[:, C_MQ:C_MQ + 2] = (p[:, None] // T) == np.arange(2)
    con[:, C_MR:C_MR + 2] = (p[:, None] // R % 2) == np.arange(2)
    con[:, C_M8:C_M8 + 8] = (p[:, None] // R) == np.arange(8)
    con[:, C_M4:C_M4 + 4] = (p[:, None] // (2 * R)) == np.arange(4)
    con[:, C_CAU:C_CAU + T] = (p[:, None] % T) <= np.arange(T)
    con[:, C_EYE:C_EYE + 16] = np.eye(4).reshape(-1)
    rowno = np.broadcast_to((p % R).astype(np.int32)[:, None], (P, NGRP))
    return con, np.ascontiguousarray(rowno)


def kernel(**inputs):
    import numpy as np
    import concourse.bacc as bacc
    from concourse.bass_utils import run_bass_kernel_spmd

    v = {k: np.asarray(a) for k, a in inputs.items()}
    con, rowno = constants()
    a1, b1 = v["L0_cond_A"], v["L0_cond_B"]
    a2, b2 = v["L0_cond2_A"], v["L0_cond2_B"]
    i1, i2 = v["itok_B_3_7"], v["itok_B_4_50"]

    def rows(i):
        return np.repeat(i.reshape(NGRP, 8).T, R, axis=0)

    def by_channel(w):
        return w.reshape(w.shape[0], R, NCH, P).transpose(0, 3, 2, 1)

    arrays = {
        "x": v["x"].reshape(NPAIR, 2, T, NCH, P).transpose(0, 4, 3, 1, 2).reshape(NPAIR, P, NCH * P),
        "ids1": i1, "ids2": i2, "id1r": rows(i1), "id2r": rows(i2), "rowno": rowno, "con": con,
        "a1c": a1.reshape(NA1, NCH, P, R).transpose(2, 1, 0, 3).reshape(P, D),
        "a1t": a1.transpose(0, 2, 1).reshape(NA1 * R, D),
        "b1g": by_channel(b1).reshape(NA1, P, NCH * R),
        "b2g": by_channel(b2).reshape(NA2, P, NCH * R),
        "a2c": a2.reshape(NA2, NCH, P, R).transpose(2, 1, 0, 3).reshape(P, NCH * NA2 * R),
        "a2t": a2.reshape(NA2, H, HD, R).transpose(0, 1, 3, 2).reshape(NA2, H * R, HD),
        "bv": np.stack([v["L0_attn_bv_q"], v["L0_attn_bv_k"], v["L0_attn_bv_v"]]),
        "wct": np.concatenate([v["L0_ffn_W_res"], v["L0_ffn_W_pre"], v["L0_ffn_W_post"]])
        .reshape(24, NCH, P).transpose(2, 1, 0).reshape(P, NCH * 24),
        "w_branch": v["L0_ffn_W_branch"],
        "h_res": v["L0_ffn_H_res_base"].reshape(-1), "h_pre": v["L0_ffn_H_pre_base"],
        "h_post": v["L0_ffn_H_post_base"], "gate": v["L0_ffn_gate"],
    }
    arrays = {k: np.ascontiguousarray(a) for k, a in arrays.items()}
    nc = bacc.Bacc("TRN2", target_bir_lowering=False, num_devices=1)
    io = {k: nc.dram_tensor(f"in_{k}", a.shape, mybir.dt.from_np(a.dtype), kind="ExternalInput").ap()
          for k, a in arrays.items()}
    io["out"] = nc.dram_tensor("out", (NPAIR, P, NCH * P), F32, kind="ExternalOutput").ap()
    program(nc, io)
    r = run_bass_kernel_spmd(nc, [{f"in_{k}": a for k, a in arrays.items()}], core_ids=[0])
    out = r.results[0]["out"].reshape(NPAIR, P, NCH, 2, T).transpose(0, 3, 4, 2, 1)
    return np.ascontiguousarray(out.reshape(B, T, D))
```

```python
from contextlib import ExitStack

import concourse.bass as bass
from concourse import mybir

ALU = mybir.AluOpType
ACT = mybir.ActivationFunctionType
AX = mybir.AxisListType.X
F32 = mybir.dt.float32
I32 = mybir.dt.int32
U32 = mybir.dt.uint32

P = 128
B, T, D = 128, 64, 1024
H, HD, R = 4, 256, 16
NA1, NA2 = 8, 64
NPAIR = B // 2
NGRP = NPAIR // 4
NBODY = NGRP // 2
NCH = D // P
NLG = 24 + R
TAU = 0.1
EPS = 1.1920929e-07
SCALE = 4.0 * float(HD) ** -0.5
CP = 16
NCHAIN = 2
NBATCH = NPAIR // (CP * NCHAIN)
HALF = 50
PER_BODY = 24
BPB = NBODY // NBATCH

C_ID, C_SEL, C_MQ, C_MR, C_M8, C_M4, C_CAU, C_EYE = 0, 128, 192, 194, 196, 204, 208, 272
NCON = 288


def program(nc, io):
    with ExitStack() as ctx:
        def sb(name, shape, dt=F32):
            return ctx.enter_context(nc.sbuf_tensor(name, shape, dt))

        def sem(name, n=None):
            if n is None:
                return ctx.enter_context(nc.semaphore(name))
            return [ctx.enter_context(nc.semaphore(f"{name}{i}")) for i in range(n)]

        tab_m = nc.dram_tensor("tab_m", [NA1 * R, H * R], F32).ap()
        tab_c = nc.dram_tensor("tab_c", [NA1 * R * NA2, H * R], F32).ap()
        tab_lg = nc.dram_tensor("tab_lg", [NA2 * R, NLG], F32).ap()
        tab_av = nc.dram_tensor("tab_av", [NA1 * R, D], F32).ap()
        tab_t2 = nc.dram_tensor("tab_t2", [NA2, P, HD], F32).ap()

        con = sb("con", [P, NCON])
        ident = con[:, C_ID:C_ID + P]
        select = con[:, C_SEL:C_SEL + 4 * R]
        ids = sb("ids", [1, B], I32)
        rowno = sb("rowno", [P, NGRP], I32)
        id1r = sb("id1r", [P, NGRP], I32)
        id2r = sb("id2r", [P, NGRP], I32)
        idx = sb("idx", [P, NGRP, 3], U32)
        idx_now = sb("idx_now", [P, 2, 3], U32)
        m_g = sb("m_g", [P, 2, H * R])
        c_g = sb("c_g", [P, 2, H * R])
        lg_g = sb("lg_g", [P, 2, NLG])
        o_all = sb("o_all", [P, NGRP, H * T])
        lg_all = sb("lg_all", [P, NPAIR, 24])
        ms_all = sb("ms_all", [P, NPAIR])
        u2_all = sb("u2_all", [P, NPAIR, R])
        d_all = sb("d_all", [P, NPAIR, H * 8])
        base24 = sb("base24", [P, 24])
        gate = sb("gate", [P, 6])
        eyeg = sb("eyeg", [P, 16])

        xt = sb("xt", [P, 2, 4, NCH * P])
        b2_tab = xt[:, :, :, :].rearrange("p u j c -> p (u j c)")
        brow = sb("brow", [P, 2, 2, D])
        bt = sb("bt", [P, 2, 2, NCH, P])
        cbuf = sb("cbuf", [P, 8192])
        a2_tab = cbuf[:, :]
        ut = cbuf[:, 0:4096].rearrange("p (u j c) -> p u j c", u=2, j=4)
        t2 = cbuf[:, 4096:8192].rearrange("p (u k c) -> p u k c", u=2, k=8)
        av = sb("av", [P, 2, D])
        soft = sb("soft", [P, 2, 4, H * T])
        prob = sb("prob", [P, 2, 4, H * T])
        c_stage = soft[:, :, :, :].rearrange("p u j c -> p (u j c)")
        obd = sb("obd", [P, 2, H * P])
        ubuf = sb("ubuf", [P, 2, H * P])
        mbd = sb("mbd", [P, 2, H, P])
        cbd = sb("cbd", [P, 2, H, 4 * R])
        lbd = sb("lbd", [P, 2, 4 * NLG])
        bn1 = sb("bn1", [P, 2, P])
        bn2 = sb("bn2", [P, 2, P])
        xb2 = sb("xb2", [P, 2, P])
        btc = sb("btc", [P, 2, P + T])
        qt = sb("qt", [P, 2, H * T])
        b2t = sb("b2t", [P, 2, P])
        gy = sb("gy", [P, 2, 4 * R])

        z24 = sb("z24", [P, NCHAIN, CP, 24])
        zz = sb("zz", [P, NCHAIN, 16 * CP])
        kr = sb("kr", [P, NCHAIN, 16 * CP])
        kc = sb("kc", [P, NCHAIN, 16 * CP])
        rho = sb("rho", [P, NCHAIN, 16 * CP])
        st = sb("st", [P, NCHAIN, 16 * CP])
        lrow = sb("lrow", [P, NCHAIN, 4 * CP])
        lcol = sb("lcol", [P, NCHAIN, 4 * CP])
        dif = sb("dif", [P, NCHAIN, 4 * CP])
        small = sb("small", [P, NCHAIN, 4 * CP])
        hp = sb("hp", [P, NCHAIN, CP, 8])
        rstd = sb("rstd", [P, NCHAIN, CP])

        ps = ctx.enter_context(nc.psum_tensor("ps", [P, 8, 512], F32))

        a1c = o_all[:, 0:4, :].rearrange("p g c -> p (g c)")
        a1qk = o_all[:, 4:8, :].rearrange("p g c -> p (g c)")
        a1v = o_all[:, 8:12, :].rearrange("p g c -> p (g c)")
        a1t = o_all[:, 12:16, :].rearrange("p g c -> p (g c)")
        wct = ubuf[:, 0, 0:NCH * 24]
        wbr = ubuf[:, 1, :]
        bvt = sb("bvt", [H, 3, HD])
        bst = sb("bst", [H, 3, HD])
        bal = sb("bal", [H, 4])
        vqc = sb("vqc", [P, 2, 2, H])
        mst = mbd[:, 0, :, :]
        c24 = mbd[0:24, :, :, :].rearrange("p u h c -> p (u h c)")
        ws = av[:, :, :].rearrange("p u (j c) -> p u j c", j=H)
        eps_c = sb("eps_c", [P, 1])
        idx_av = sb("idx_av", [P, 2], U32)
        mout = cbd[:, 0, 0, :]
        lgs = prob[:, 0, :, :].rearrange("p j c -> p (j c)")
        lgo = prob[:, 1, :, :].rearrange("p j c -> p (j c)")

        in_con = sem("in_con"); in_ids = sem("in_ids"); in_a1 = sem("in_a1"); in_b2 = sem("in_b2")
        in_a2 = sem("in_a2"); in_w = sem("in_w"); in_bv = sem("in_bv"); in_h = sem("in_h")
        bind = sem("bind"); bind_t = sem("bind_t"); bind_c = sem("bind_c")
        a1_scaled = sem("a1_scaled"); vrow = sem("vrow"); avt_made = sem("avt_made")
        tm_mm = sem("tm_mm"); tm_mask = sem("tm_mask"); tm_made = sem("tm_made")
        tc_mm = sem("tc_mm"); tc_ev = sem("tc_ev"); tc_out = sem("tc_out")
        tl_mm = sem("tl_mm"); tl_ev = sem("tl_ev"); tl_t = sem("tl_t"); tl_ev2 = sem("tl_ev2")
        tw_mm = sem("tw_mm"); tw_ev = sem("tw_ev")
        tw_out = sem("tw_out", 2)
        tab_out = sem("tab_out"); tg_out = sem("tg_out"); gate_ok = sem("gate_ok")
        gexp = sem("gexp"); link_ok = sem("link_ok"); ix_ok = sem("ix_ok", 2)
        idx_ok = sem("idx_ok"); nx_ok = sem("nx_ok", 2); t2_copy = sem("t2_copy"); zeros_ok = sem("zeros_ok")

        x_in = sem("x_in", 4); b_in = sem("b_in", 2); rows_in = sem("rows_in", 2)
        wt_mm = sem("wt_mm", 2); wt_ok = sem("wt_ok", 2); cp_ok = sem("cp_ok", 2)
        xb_mm = sem("xb_mm", 2); bn_ok = sem("bn_ok", 2);
        bt_ok = sem("bt_ok", 2); q_mm = sem("q_mm", 2); q_ok = sem("q_ok", 2)
        s_mm = sem("s_mm", 2); s_abs = sem("s_abs", 2); s_e = sem("s_e", 2); s_ln = sem("s_ln", 2)
        s_min = sem("s_min", 2); s_exp = sem("s_exp", 2); p_ok = sem("p_ok", 2)
        o_mm = sem("o_mm", 2); obd_ok = sem("obd_ok", 2); oc_ok = sem("oc_ok", 2)
        c_mm = sem("c_mm", 2); b2_ok = sem("b2_ok", 2)
        u2_ok = sem("u2_ok", 2); b2t_mm = sem("b2t_mm", 2); b2t_ok = sem("b2t_ok", 2)
        lg_mm = sem("lg_mm", 2); lg_ok = sem("lg_ok", 2); gy_ok = sem("gy_ok", 2)
        ms_ok = sem("ms_ok", 2); bd_ok = sem("bd_ok", 2)

        k_sum = sem("k_sum", 2); k_ln = sem("k_ln", 2); k_dif = sem("k_dif", 2)
        k_rho = sem("k_rho", 2); k_m = sem("k_m", 2); k_b = sem("k_b", 2)
        k_i = sem("k_i", 2); k_ia = sem("k_ia", 2); k_f = sem("k_f", 2)
        d_ok = sem("d_ok", 2)

        t2_in = sem("t2_in", 2); av_in = sem("av_in", 2); ob_ok = sem("ob_ok", 2)
        u_ok = sem("u_ok", 2); ut_mm = sem("ut_mm", 2); ut_ok = sem("ut_ok", 2)
        f_mm = sem("f_mm", 4); f_ok = sem("f_ok", 4); out_ok = sem("out_ok", 4)

        def bc(ap, axis, shape):
            return ap.unsqueeze(axis).broadcast_to(shape)

        block = ctx.enter_context(nc.Block())

        @block.sync
        def _(sp):
            sp.dma_start(ids[:, :], io["ids2"].unsqueeze(0)).then_inc(in_ids, 16)
            sp.dma_start(bvt[:, :, :], io["bv"].rearrange("k h c -> h k c")).then_inc(in_bv, 16)
            sp.dma_start(con[:, :], io["con"]).then_inc(in_con, 16)
            sp.dma_start(rowno[:, :], io["rowno"]).then_inc(in_con, 16)
            sp.dma_start(id1r[:, :], io["id1r"]).then_inc(in_con, 16)
            sp.dma_start(id2r[:, :], io["id2r"]).then_inc(in_con, 16)
            sp.dma_start(a1c, io["a1c"]).then_inc(in_a1, 16)
            sp.dma_start(a1t, io["a1t"]).then_inc(in_a1, 16)
            sp.dma_start(b2_tab.rearrange("p (i c) -> p i c", i=NA2),
                         io["b2g"].rearrange("i p c -> p i c")).then_inc(in_b2, 16)
            sp.dma_start(wct, io["wct"]).then_inc(in_w, 16)
            sp.dma_start(wbr.rearrange("p (k c) -> p k c", k=2),
                         io["w_branch"].rearrange("(k p) c -> p k c", p=P)).then_inc(in_w, 16)
            sp.dma_start(a2_tab, io["a2c"]).then_inc(in_a2, 16)
            for k, w in enumerate(("h_res", "h_pre", "h_post")):
                n0, n1 = (0, 16, 20, 24)[k:k + 2]
                sp.dma_start(base24[:, n0:n1], bass.AP(io[w].tensor, 0, [[0, P], [1, n1 - n0]])
                             ).then_inc(in_h, 16)
            sp.dma_start(gate[:, 0:1], bass.AP(io["gate"].tensor, 0, [[0, P], [1, 1]])
                         ).then_inc(in_h, 16)
            sp.dma_start(tab_t2[:, 0:H * R, :], io["a2t"]).then_inc(t2_copy, 16)
            sp.wait_ge(avt_made, 2)
            sp.dma_start(tab_av, a1t).then_inc(tab_out, 16)
            sp.wait_ge(tm_made, 1)
            sp.dma_start(tab_m, mout).then_inc(tab_out, 16)
            for k in range(2):
                sp.wait_ge(tc_ev, 8 * (k + 1))
                sp.dma_start(tab_c.rearrange("(p i) c -> p i c", p=P)[:, 32 * k:32 * k + 32, :],
                             c_stage.rearrange("p (i c) -> p i c", c=H * R)).then_inc(tc_out, 16)
                sp.wait_ge(tc_out, 16 * (k + 1))
            sp.wait_ge(tl_ev2, 8)
            sp.dma_start(tab_lg.rearrange("(k p) c -> p k c", p=P)[:, :, 0:24],
                         lgo[:, 0:8 * 24].rearrange("p (k c) -> p k c", c=24)).then_inc(tg_out, 16)
            sp.wait_ge(tl_ev, 3)
            gram = tab_lg.rearrange("(i k s r) c -> k s r i c", k=4, s=2, r=R)
            for k in range(4):
                for s in range(2):
                    p0 = (2 * k + s) * R
                    sp.dma_start(gram[k, s, :, :, 24:NLG],
                                 lgs[p0:p0 + R, 0:256].rearrange("p (i s c) -> p s i c", s=2, c=R)
                                 [:, s]).then_inc(tg_out, 16)
            sp.wait_ge(tc_mm, 16)

            def load_a(body, first=False):
                for u in range(2):
                    if not first:
                        sp.wait_ge(xb_mm[u], 2 * body)
                    for k in range(2):
                        sp.dma_start(xt[:, u, 2 * k:2 * k + 2, :],
                                     io["x"][bass.ds(((body * 2 + u) * 2 + k) * 2, 2)]
                                     .rearrange("n p c -> p n c")).then_inc(x_in[2 * u + k], 16)

            load_a(0, first=True)
            with sp.Fori(1, NBODY) as body:
                load_a(body)
            sp.wait_ge(in_ids, 16)

            def adapters(u, body):
                return [sp.value_load(ids[0:1, bass.ds((body * 2 + u) * 8 + q, 1)], min_val=0,
                                      max_val=NA2 - 1) for q in range(8)]

            def load_t2(u, i2):
                for q in range(8):
                    sp.dma_start(t2[:, u, q, :],
                                 tab_t2[bass.ds(i2[q], 1)].rearrange("i k c -> (i k) c")
                                 ).then_inc(t2_in[u], 16)

            def load_x(u, body, first=False):
                for k in range(2):
                    if not first:
                        sp.wait_ge(out_ok[2 * u + k], 16 * body)
                    sp.dma_start(xt[:, u, 2 * k:2 * k + 2, :],
                                 io["xrow"][bass.ds(((body * 2 + u) * 2 + k) * 2, 2)]
                                 .rearrange("n p c -> p n c")).then_inc(x_in[2 * u + k], 16)

            def store_c(u, body):
                for k in range(2):
                    for j in (2 * k, 2 * k + 1):
                        sp.wait_ge(f_ok[j], 4 * body + 2 * u + 2)
                    sp.dma_start(io["out"][bass.ds(((body * 2 + u) * 2 + k) * 2, 2)]
                                 .rearrange("n p c -> p n c"),
                                 xt[:, u, 2 * k:2 * k + 2, :]).then_inc(out_ok[2 * u + k], 16)

            for u in range(2):
                sp.wait_ge(xb_mm[u], 2 * NBODY)
                sp.wait_ge(tw_out[u], 16 * 16)
            sp.wait_ge(t2_copy, 16)
            sp.wait_ge(tw_mm, 32)
            for u in range(2):
                load_t2(u, adapters(u, 0))
                load_x(u, 0, first=True)
            with sp.Fori(0, NBODY - 1) as body:
                for u in range(2):
                    i2 = adapters(u, body + 1)
                    store_c(u, body)
                    load_t2(u, i2)
                    load_x(u, body + 1)
            for u in range(2):
                store_c(u, NBODY - 1)
            for k in range(4):
                sp.wait_ge(out_ok[k], 16 * NBODY)

        @block.tensor
        def _(pe):
            pe.wait_ge(in_con, 64)
            pe.wait_ge(bind, 1)
            for w in range(2):
                for k in range(2):
                    mm = pe.transpose(ps[:, 0, (2 * w + k) * H:(2 * w + k + 1) * H],
                                      bst[:, w, k * P:(k + 1) * P], ident[0:H, 0:H])
            mm.then_inc(bind_t, 1)
            for h in range(H):
                mm = pe.matmul(ps[:, 1 + h // 2, (h % 2) * HD:(h % 2 + 1) * HD],
                               ident[0:H, h:h + 1].broadcast_to([H, P]), bst[:, 1, :],
                               start=True, stop=True)
            mm.then_inc(vrow, 1)
            pe.wait_ge(a1_scaled, 2)
            for h in range(H):
                for k in range(2):
                    c = (2 * h + k) * P
                    mm = pe.matmul(ps[:, 3, h * P:(h + 1) * P], a1qk[:, c:c + P], a1c[:, c:c + P],
                                   start=(k == 0), stop=(k == 1))
            mm.then_inc(tm_mm, 1)
            pe.wait_ge(in_b2, 16)
            b2v = b2_tab.rearrange("p (i k r) -> p i k r", i=NA2, k=NCH)
            n = 0
            for half in range(2):
                for h in range(H):
                    for s in range(2):
                        if n >= 4:
                            pe.wait_ge(tc_ev, n - 3)
                        for k in range(2):
                            c = 2 * h + k
                            mm = pe.matmul(ps[:, 4 + n % 4, 0:HD], a1v[:, c * P:(c + 1) * P],
                                           b2v[:, 32 * half + 16 * s:32 * half + 16 * s + 16, c, :],
                                           start=(k == 0), stop=(k == 1))
                        mm.then_inc(tc_mm, 1)
                        n += 1
            pe.wait_ge(in_w, 32)
            pe.wait_ge(in_a2, 16)
            pe.wait_ge(bind_c, 1)
            pe.wait_ge(avt_made, 2)
            for s in range(2):
                for c in range(NCH):
                    mm = pe.matmul(ps[0:24, s, :], wct[:, c * 24:(c + 1) * 24],
                                   a2_tab[:, c * D + s * 512:c * D + (s + 1) * 512],
                                   start=(c == 0), stop=(c == NCH - 1))
                mm.then_inc(tl_mm, 1)
            for i in range(8):
                for c in range(NCH):
                    for k in range(4):
                        a = a2_tab[:, c * D + (4 * i + k) * 2 * R:c * D + (4 * i + k + 1) * 2 * R]
                        mm = pe.matmul(ps[32 * k:32 * k + 32, 2, i * 2 * R:(i + 1) * 2 * R], a, a,
                                       start=(c == 0), stop=(c == NCH - 1))
            mm.then_inc(tl_mm, 1)
            pe.wait_ge(tl_ev, 2)
            for k in range(8):
                mm = pe.matmul(ps[:, 0, k * 24:(k + 1) * 24],
                               c24[:, k * P:(k + 1) * P], ident[0:24, 0:24],
                               start=True, stop=True)
            mm.then_inc(tl_t, 1)
            pe.wait_ge(tc_ev, 16)
            for g in range(8):
                for j in range(H):
                    n = 4 * g + j
                    if n >= 4:
                        pe.wait_ge(tw_ev, n - 3)
                    for k in range(2):
                        c = 2 * j + k
                        mm = pe.matmul(ps[:, 4 + j, 0:HD],
                                       a2_tab[:, c * D + g * P:c * D + (g + 1) * P],
                                       wbr[:, k * HD:(k + 1) * HD], start=(k == 0), stop=(k == 1))
                    mm.then_inc(tw_mm, 1)

            def turn_b(u, body, first=False):
                pe.wait_ge(b_in[u], 32 * (body + 1))
                for w in range(2):
                    for k in range(2):
                        if not (first and u == 0 and w == 0):
                            pe.wait_ge(wt_ok[k], 4 * body + 2 * u + w)
                        for c in range(4):
                            mm = pe.transpose(ps[:, k, c * P:(c + 1) * P],
                                              brow[:, u, w, (4 * k + c) * P:(4 * k + c + 1) * P],
                                              ident)
                        mm.then_inc(wt_mm[k], 1)

            def xb(u, w, body, first=False):
                if w == 0:
                    for k in range(2):
                        pe.wait_ge(x_in[2 * u + k], 16 * (body + 1))
                    if not first:
                        pe.wait_ge(ms_ok[u], body)
                for k in range(2):
                    pe.wait_ge(wt_ok[k], 4 * body + 2 * u + w + 1)
                for c in range(NCH):
                    for j in range(4):
                        mm = pe.matmul(ps[32 * j:32 * j + 32, 2 + u, w * P:(w + 1) * P],
                                       bt[:, u, w, c, 32 * j:32 * j + 32],
                                       xt[:, u, j, c * P:(c + 1) * P],
                                       start=(c == 0), stop=(c == NCH - 1))
                mm.then_inc(xb_mm[u], 1)

            def turn(u, body):
                pe.wait_ge(bn_ok[u], 2 * body + 2)
                pe.transpose(ps[:, 2 + u, 256:384], btc[:, u, 0:P], ident)

            def query(u, body):
                pe.wait_ge(cp_ok[u], body + 1)
                pe.wait_ge(bd_ok[u], 3 * body + 1)
                for h in range(H):
                    mm = pe.matmul(ps[:, 2 + u, h * T:(h + 1) * T], mbd[:, u, h, :],
                                   btc[:, u, P:P + T], start=True, stop=True)
                mm.then_inc(q_mm[u], 1)

            def score(u, body, first=False):
                pe.wait_ge(q_ok[u], body + 1)
                if not (first and u == 0):
                    pe.wait_ge(s_min[1 - u], 2 * body + 2 * u)
                for j in range(4):
                    pe.matmul(ps[:, 4 + j, 0:H * T], btc[32 * j:32 * j + 32, u, 0:P],
                              qt[32 * j:32 * j + 32, u, :], start=True,
                              stop=True).then_inc(s_mm[u], 1)

            def attend(u, body):
                pe.wait_ge(p_ok[u], 2 * body + 2)
                pe.wait_ge(bt_ok[u], body + 1)
                for j in range(4):
                    pe.matmul(ps[32 * j:32 * j + 32, 2 + u, 0:H * T],
                              bn1[:, u, 32 * j:32 * j + 32], prob[:, u, j, :], start=True,
                              stop=True).then_inc(o_mm[u], 1)

            def cross(u, body):
                pe.wait_ge(obd_ok[u], body + 1)
                pe.wait_ge(oc_ok[u], body + 1)
                pe.wait_ge(bd_ok[u], 3 * body + 2)
                for h in range(H):
                    pe.matmul(ps[:, 2 + u, 256:320], obd[:, u, h * P:(h + 1) * P],
                              cbd[:, u, h, :], start=(h == 0), stop=False)
                pe.matmul(ps[:, 2 + u, 256:320], xb2[:, u, :], select, start=False,
                          stop=True).then_inc(c_mm[u], 1)

            def turn2(u, body):
                pe.wait_ge(b2_ok[u], body + 1)
                pe.wait_ge(u2_ok[u], body + 1)
                pe.transpose(ps[:, 2 + u, 320:448], bn2[:, u, :], ident).then_inc(b2t_mm[u], 1)

            def logit(u, body):
                pe.wait_ge(b2t_ok[u], body + 1)
                pe.wait_ge(bd_ok[u], 3 * body + 3)
                pe.matmul(ps[:, 2 + u, 0:4 * NLG], b2t[:, u, :], lbd[:, u, :], start=True,
                          stop=True).then_inc(lg_mm[u], 1)

            def slot(f, b, first=False):
                if f:
                    turn_b(*f, first)
                    xb(f[0], 0, f[1], first)
                if b:
                    attend(*b)
                if f:
                    xb(f[0], 1, f[1])
                if b:
                    cross(*b)
                if f:
                    turn(*f)
                    query(*f)
                if b:
                    turn2(*b)
                if f:
                    score(*f, first)
                if b:
                    logit(*b)

            def body_a(body, first=False, last=False):
                slot((1, body), (0, body), first)
                slot(None if last else (0, body + 1), (1, body))

            pe.wait_ge(tl_ev2, 8)
            pe.wait_ge(tl_ev, 3)
            pe.wait_ge(tw_ev, 32)
            slot((0, 0), None, first=True)
            body_a(0, first=True)
            with pe.Fori(1, NBODY - 1) as body:
                body_a(body)
            body_a(NBODY - 1, last=True)

            def turn_u(u, k, body, first=False):
                for j in (2 * k, 2 * k + 1):
                    n = 4 * u + j
                    pe.wait_ge(u_ok[j % 2], 4 * body + n // 2 + 1)
                    if not (first and n < 2):
                        pe.wait_ge(ut_ok[j % 2], 4 * body + n // 2)
                    for h in range(H):
                        mm = pe.transpose(ps[:, j % 2, h * P:(h + 1) * P],
                                          ubuf[:, j % 2, h * P:(h + 1) * P], ident)
                    mm.then_inc(ut_mm[j % 2], 1)

            def final(u, half, body, first=False):
                if half == 0:
                    pe.wait_ge(t2_in[u], 128 * (body + 1))
                    pe.wait_ge(av_in[u], 16 * (body + 1))
                    pe.wait_ge(ob_ok[u], body + 1)
                for j in range(4):
                    if half == 0 and j < 2:
                        pe.wait_ge(ut_ok[0], 4 * body + 2 * u + j + 1)
                        pe.wait_ge(ut_ok[1], 4 * body + 2 * u + j + 1)
                    if not (first and u == 0 and half == 0):
                        pe.wait_ge(f_ok[j], 4 * body + 2 * u + half)
                    for h in range(2):
                        n = 2 * half + h
                        for q in range(2):
                            pe.matmul(ps[64 * q:64 * q + 64, 4 + j, h * HD:(h + 1) * HD],
                                      ut[:, u, j, n * P + 64 * q:n * P + 64 * q + 64],
                                      t2[:, u, 2 * j + q, :], start=(h == 0), stop=False,
                                      skip_group_check=True)
                for h in range(2):
                    n = 2 * half + h
                    for j in range(4):
                        rows = slice(32 * j, 32 * j + 32)
                        mm = pe.matmul(ps[:, 4 + j, h * HD:(h + 1) * HD],
                                       obd[rows, u, n * P:(n + 1) * P],
                                       av[rows, u, n * HD:(n + 1) * HD], start=False,
                                       stop=True, skip_group_check=True)
                        if h == 1:
                            mm.then_inc(f_mm[j], 1)

            def body_c(body, first=False, last=False):
                final(0, 0, body, first)
                turn_u(1, 0, body)
                final(0, 1, body)
                turn_u(1, 1, body)
                final(1, 0, body)
                if not last:
                    turn_u(0, 0, body + 1)
                final(1, 1, body)
                if not last:
                    turn_u(0, 1, body + 1)

            for u in range(2):
                pe.wait_ge(q_ok[u], NBODY)
                pe.wait_ge(s_min[u], 2 * NBODY)
            for batch in range(NBATCH):
                b0, first = batch * BPB, batch == 0
                for k in range(2):
                    turn_u(0, k, b0, first)
                body_c(b0, first=first)
                with pe.Fori(b0 + 1, b0 + BPB - 1) as body:
                    body_c(body)
                body_c(b0 + BPB - 1, last=True)

        @block.scalar
        def _(act):
            act.preload_act_table_set("natural_log_exp_and_others")
            for n in range(16):
                act.wait_ge(tc_mm, n + 1)
                half, h, s = n // 8, (n // 2) % 4, n % 2
                if n == 8:
                    act.wait_ge(tc_out, 16)
                dst = c_stage.rearrange("p (i h r) -> p i h r", h=H, r=R)[:, 16 * s:16 * s + 16, h, :]
                act.activation(dst, ps[:, 4 + n % 4, 0:HD].rearrange("p (i r) -> p i r", r=R),
                               ACT.Copy).then_inc(tc_ev, 1)
            act.wait_ge(in_h, 64)
            act.activation(gate[:, 1:2], gate[:, 0:1], ACT.Abs).then_inc(gexp, 1)
            act.wait_ge(gexp, 1)
            act.activation(gate[:, 2:3], gate[:, 1:2], ACT.Exp, scale=-1.0).then_inc(gexp, 1)
            for s in range(2):
                act.wait_ge(tl_mm, s + 1)
                act.activation(c24[:, s * 512:(s + 1) * 512], ps[0:24, s, :], ACT.Copy
                               ).then_inc(tl_ev, 1)
            act.wait_ge(tl_mm, 3)
            act.activation(lgs[:, 0:256], ps[:, 2, 0:256], ACT.Copy).then_inc(tl_ev, 1)
            act.wait_ge(tl_t, 1)
            for k in range(8):
                act.activation(lgo[:, k * 24:(k + 1) * 24], ps[:, 0, k * 24:(k + 1) * 24],
                               ACT.Copy).then_inc(tl_ev2, 1)
            aw = tab_t2.rearrange("i (w j r) c -> w i j r c", w=2, j=H)[1]
            for g in range(8):
                if g >= 2:
                    act.wait_ge(tw_out[g % 2], 16 * 4 * (g // 2))
                for j in range(H):
                    act.wait_ge(tw_mm, 4 * g + j + 1)
                    act.activation(ws[:, g % 2, j, :], ps[:, 4 + j, 0:HD], ACT.Copy
                                   ).then_inc(tw_ev, 1)
                for j in range(H):
                    act.wait_ge(tw_ev, 4 * g + j + 1)
                    act.dma_start(aw[8 * g:8 * g + 8, j], ws[:, g % 2, j, :]
                                  ).then_inc(tw_out[g % 2], 16)

            def copy_b(u, w, body, first=False):
                act.wait_ge(wt_mm[0], 4 * body + 2 * u + w + 1)
                if not first:
                    act.wait_ge(xb_mm[u], 2 * body)
                act.activation(bt[:, u, w, 0:4, :], ps[:, 0, :].rearrange(
                    "p (k c) -> p k c", k=4), ACT.Copy).then_inc(wt_ok[0], 1)

            def turned(u, body, first=False):
                act.wait_ge(q_mm[u], body + 1)
                if not first:
                    act.wait_ge(o_mm[u], 4 * body)
                act.activation(bn1[:, u, :], ps[:, 2 + u, 256:384], ACT.Copy).then_inc(bt_ok[u], 1)

            def query(u, body):
                act.wait_ge(q_mm[u], body + 1)
                act.activation(qt[:, u, :], ps[:, 2 + u, 0:256], ACT.Copy).then_inc(q_ok[u], 1)

            def sigmoid(u, k, body):
                act.wait_ge(s_mm[u], 4 * body + 2 * k + 2)
                w = soft[:, u, 2 * k:2 * k + 2, :]
                e = 2 * body + k + 1
                act.activation(w, ps[:, 4 + 2 * k:6 + 2 * k, 0:H * T], ACT.Abs).then_inc(s_abs[u], 1)
                act.wait_ge(s_abs[u], e)
                act.activation(w, w, ACT.Exp, scale=-1.0).then_inc(s_e[u], 1)
                act.wait_ge(s_e[u], e)
                act.activation(w, w, ACT.Ln, bias=1.0).then_inc(s_ln[u], 1)

            def weight(u, k, body):
                e = 2 * body + k + 1
                act.wait_ge(s_min[u], e)
                w = prob[:, u, 2 * k:2 * k + 2, :]
                act.activation(w, w, ACT.Exp).then_inc(s_exp[u], 1)

            def keep_o(u, body):
                act.wait_ge(o_mm[u], 4 * body + 4)
                act.wait_ge(obd_ok[u], body + 1)
                act.activation(o_all[:, bass.ds(2 * body + u, 1), :],
                               ps[:, 2 + u, 0:H * T].unsqueeze(1), ACT.Copy).then_inc(oc_ok[u], 1)

            def turned2(u, body):
                act.wait_ge(b2t_mm[u], body + 1)
                act.activation(b2t[:, u, :], ps[:, 2 + u, 320:448], ACT.Copy).then_inc(b2t_ok[u], 1)

            def sums(c):
                return st[:, c, :].rearrange("p (t j k) -> p t j k", j=4, k=4)[:, :, :, 3]

            def k_ratio(c, n, batch):
                act.wait_ge(k_dif[c], batch * 99 + n + 1)
                act.activation(rho[:, c, :].rearrange("p (t i j) -> p t i j", i=4, j=4)[:, :, :, 1:4],
                               dif[:, c, 0:3 * CP].rearrange("p (t j) -> p t j", j=3)
                               .unsqueeze(2).broadcast_to([P, CP, 4, 3]), ACT.Exp
                               ).then_inc(k_rho[c], 1)

            def k_steps(m0, m1, nb, batch):
                for m in range(m0, m1):
                    for c in range(NCHAIN):
                        act.wait_ge(k_sum[c], batch * 99 + nb + m + 1)
                        act.activation((lcol if m % 2 == 0 else lrow)[:, c, :]
                                       .rearrange("p (t j) -> p t j", j=4), sums(c), ACT.Ln
                                       ).then_inc(k_ln[c], 1)
                    for c in range(NCHAIN):
                        k_ratio(c, nb + m, batch)

            def k_matrix(c, done):
                z = zz[:, c, :].rearrange("p (t i j) -> p t j i", i=4, j=4)
                act.activation(kc[:, c, :].rearrange("p (t j i) -> p t j i", i=4, j=4), z, ACT.Exp)
                act.activation(kr[:, c, :], zz[:, c, :], ACT.Exp).then_inc(done[c], 1)

            def k_start(batch):
                for u in range(2):
                    act.wait_ge(ms_ok[u], (batch + 1) * BPB)
                act.wait_ge(zeros_ok, 3)
                for c in range(NCHAIN):
                    p0 = (batch * NCHAIN + c) * CP
                    act.activation(rstd[:, c, :], ms_all[:, p0:p0 + CP], ACT.Ln, scale=1.0 / D,
                                   bias=eps_c[:, 0:1]).then_inc(k_ia[c], 1)
                    act.wait_ge(k_ia[c], batch * 4 + 1)
                    act.activation(rstd[:, c, :], rstd[:, c, :], ACT.Exp, scale=-0.5
                                   ).then_inc(k_ia[c], 1)
                for c in range(NCHAIN):
                    act.wait_ge(k_i[c], batch * 12 + 5)
                    act.activation(st[:, c, :], zz[:, c, :], ACT.Exp).then_inc(k_ia[c], 1)
                    act.wait_ge(k_i[c], batch * 12 + 7)
                    act.activation(hp[:, c, :, :], hp[:, c, :, :], ACT.Exp).then_inc(k_ia[c], 1)
                for c in range(NCHAIN):
                    act.wait_ge(k_i[c], batch * 12 + 9)
                    k_matrix(c, k_m)
                    act.wait_ge(k_sum[c], batch * 99 + 1)
                    act.activation(lrow[:, c, :], small[:, c, :], ACT.Ln).then_inc(k_ln[c], 1)
                    k_ratio(c, 0, batch)

            def k_middle(batch):
                for c in range(NCHAIN):
                    act.wait_ge(k_sum[c], batch * 99 + HALF)
                    act.activation(lcol[:, c, :].rearrange("p (t j) -> p t j", j=4),
                                   sums(c), ACT.Ln
                                   ).then_inc(k_ln[c], 1)
                for c in range(NCHAIN):
                    act.wait_ge(k_dif[c], batch * 99 + HALF)
                    k_matrix(c, k_rho)
                for c in range(NCHAIN):
                    act.wait_ge(k_sum[c], batch * 99 + HALF + 1)
                    act.activation(lrow[:, c, :], small[:, c, :], ACT.Ln).then_inc(k_ln[c], 1)
                    k_ratio(c, HALF, batch)

            def slot(f, b, first=False, k=lambda m0, m1: None):
                if b:
                    sigmoid(b[0], 0, b[1])
                k(0, 1)
                if f:
                    copy_b(f[0], 0, f[1], first)
                k(1, 2)
                if b:
                    sigmoid(b[0], 1, b[1])
                k(2, 3)
                if f:
                    copy_b(f[0], 1, f[1], first)
                k(3, 4)
                if b:
                    weight(b[0], 0, b[1])
                k(4, 5)
                if b:
                    weight(b[0], 1, b[1])
                k(5, 8)
                if b:
                    keep_o(*b)
                k(8, 10)
                if f:
                    query(*f)
                    turned(*f, first)
                k(10, 11)
                if b:
                    turned2(*b)
                k(11, 12)

            def body_a(body, nb=None, batch=0, first=False, last=False):
                def k(n):
                    if nb is None:
                        return lambda m0, m1: None
                    return lambda m0, m1: k_steps(n + m0, n + m1, nb, batch)
                slot((1, body), (0, body), first, k(0))
                slot(None if last else (0, body + 1), (1, body), False, k(12))

            def turned_u(u, j, body, first=False):
                b, n = j % 2, 4 * u + j
                act.wait_ge(ut_mm[b], 4 * body + n // 2 + 1)
                if not first:
                    act.wait_ge(f_mm[j], 4 * body + 2 * u - 2)
                act.activation(ut[:, u, j, :], ps[:, b, :], ACT.Copy).then_inc(ut_ok[b], 1)

            def body_c(body, nb=None, batch=0, first=False, last=False):
                for n in range(8):
                    if n < 4:
                        turned_u(1, n, body, first)
                    elif not last:
                        turned_u(0, n - 4, body + 1)
                    if nb is not None:
                        k_steps(3 * n, 3 * n + 3, nb, batch)

            slot((0, 0), None, first=True)
            body_a(0, first=True)
            with act.Fori(1, BPB) as i:
                body_a(i)
            k_start(0)
            with act.Fori(0, 2) as i:
                body_a(BPB + i, 1 + i * PER_BODY, 0)
            k_middle(0)
            for i in range(2):
                body_a(BPB + 2 + i, HALF + 1 + i * PER_BODY, 0, last=(i == 1))
            k_start(1)
            for j in range(4):
                turned_u(0, j, 0, first=True)
            for i in range(2):
                body_c(i, 1 + i * PER_BODY, 1, first=(i == 0))
            k_middle(1)
            for i in range(2):
                body_c(2 + i, HALF + 1 + i * PER_BODY, 1, last=(i == 1))
            for j in range(4):
                turned_u(0, j, BPB)
            with act.Fori(0, BPB - 1) as i:
                body_c(BPB + i)
            body_c(NBODY - 1, last=True)

        @block.vector
        def _(dve):
            nc.vector.memset(rho[:, :, :], 0.0).then_inc(zeros_ok, 1)
            nc.vector.memset(eps_c[:, :], EPS).then_inc(zeros_ok, 1)
            nc.vector.memset(bal[:, :], 0.0).then_inc(zeros_ok, 1)
            n_link = [0]

            def link(ins):
                n_link[0] += 1
                ins.then_inc(link_ok, 1)
                dve.wait_ge(link_ok, n_link[0])

            dve.wait_ge(zeros_ok, 3)
            dve.wait_ge(in_bv, 16)
            link(dve.scalar_tensor_tensor(out=bst[:, :, :], in0=bvt[:, :, :], scalar=-1.0,
                                          in1=bvt[:, :, :], op0=ALU.mult, op1=ALU.max))
            link(dve.tensor_reduce(bal[:, 0:3], bst[:, :, :], AX, ALU.add))
            link(dve.tensor_scalar(bal[:, 0:3], bal[:, 0:3], 1.0 / HD, None, ALU.mult))
            link(dve.tensor_scalar(bst[:, :, :], bvt[:, :, :], 0.0, 2.0, ALU.is_ge, ALU.mult))
            link(dve.tensor_tensor(bst[:, :, :], bst[:, :, :], bc(bal[:, 0:3], 2, [H, 3, HD]),
                                   ALU.mult))
            link(dve.tensor_tensor(bst[:, :, :], bst[:, :, :], bc(bal[:, 0:3], 2, [H, 3, HD]),
                                   ALU.subtract))
            link(dve.tensor_tensor(bst[:, :, :], bst[:, :, :], bvt[:, :, :], ALU.subtract))
            link(dve.tensor_tensor(bst[:, :, :], bst[:, :, :], bvt[:, :, :], ALU.add))
            link(dve.tensor_tensor(bst[:, 0, :], bst[:, 0, :], bst[:, 1, :], ALU.mult))
            dve.tensor_copy(bst[:, 1, :], bst[:, 2, :]).then_inc(bind, 1)
            dve.wait_ge(bind_t, 1)
            turned = ps[:, 0, 0:16].rearrange("p (w k h) -> p w k h", w=2, k=2)
            dve.tensor_scalar(vqc[:, 0, :, :], turned[:, 0, :, :], SCALE, None, ALU.mult)
            link(dve.tensor_copy(vqc[:, 1, :, :], turned[:, 1, :, :]))
            dve.engine_nop().then_inc(bind_c, 1)
            dve.wait_ge(in_a1, 32)
            for w, dst in enumerate((a1qk, a1v)):
                dve.tensor_tensor(dst.rearrange("p (h k c) -> p h k c", h=H, k=2),
                                  a1c.rearrange("p (h k c) -> p h k c", h=H, k=2),
                                  bc(vqc[:, w, :, :].rearrange("p k h -> p h k"), 3, [P, H, 2, P]),
                                  ALU.mult).then_inc(a1_scaled, 1)
            dve.wait_ge(vrow, 1)
            for k in range(2):
                dve.tensor_tensor(a1t[:, 512 * k:512 * k + 512], a1t[:, 512 * k:512 * k + 512],
                                  ps[:, 1 + k, :], ALU.mult).then_inc(avt_made, 1)
            dve.wait_ge(tm_mm, 1)
            dve.wait_ge(in_con, 64)
            link(dve.tensor_tensor(mst.rearrange("p h (i r) -> p h i r", r=R),
                                   ps[:, 3, :].rearrange("p (h i r) -> p h i r", h=H, r=R),
                                   con[:, C_M8:C_M8 + 8].unsqueeze(1).unsqueeze(3)
                                   .broadcast_to([P, H, 8, R]), ALU.mult))
            dve.tensor_reduce(mout.rearrange("p (h r) -> p h r", h=H),
                              mst.rearrange("p h (i r) -> p h r i", r=R), AX, ALU.add
                              ).then_inc(tm_made, 1)
            idx_m, idx_c, idx_l = (idx[:, :, k] for k in range(3))
            link(dve.scalar_tensor_tensor(out=idx_m, in0=id1r[:, :], scalar=float(R),
                                          in1=rowno[:, :], op0=ALU.mult, op1=ALU.add))
            dve.scalar_tensor_tensor(out=idx_c, in0=idx_m, scalar=float(NA2),
                                     in1=id2r[:, :], op0=ALU.mult, op1=ALU.add
                                     ).then_inc(idx_ok, 1)
            dve.scalar_tensor_tensor(out=idx_l, in0=id2r[:, :], scalar=float(R),
                                     in1=rowno[:, :], op0=ALU.mult, op1=ALU.add
                                     ).then_inc(idx_ok, 1)
            dve.wait_ge(gexp, 2)
            link(dve.tensor_scalar(gate[:, 3:4], gate[:, 2:3], 1.0, None, ALU.add))
            link(dve.reciprocal(gate[:, 4:5], gate[:, 3:4]))
            link(dve.tensor_scalar(gate[:, 1:2], gate[:, 0:1], 0.0, None, ALU.is_ge))
            link(dve.tensor_tensor(gate[:, 5:6], gate[:, 1:2], gate[:, 2:3], ALU.mult))
            link(dve.tensor_tensor(gate[:, 3:4], gate[:, 1:2], gate[:, 2:3], ALU.add))
            link(dve.tensor_tensor(gate[:, 3:4], gate[:, 3:4], gate[:, 5:6], ALU.subtract))
            link(dve.tensor_tensor(gate[:, 3:4], gate[:, 3:4], gate[:, 4:5], ALU.mult))
            link(dve.tensor_tensor(gate[:, 5:6], gate[:, 5:6], gate[:, 1:2], ALU.subtract))
            link(dve.tensor_scalar(gate[:, 5:6], gate[:, 5:6], 1.0, None, ALU.add))
            link(dve.tensor_tensor(gate[:, 5:6], gate[:, 5:6], gate[:, 4:5], ALU.mult))
            link(dve.tensor_scalar(eyeg[:, :], con[:, C_EYE:C_EYE + 16], gate[:, 5:6], None,
                                   ALU.mult))

            mq = con[:, C_MQ:C_MQ + 2].unsqueeze(1).unsqueeze(3).broadcast_to([P, 4, 2, R])

            mr = con[:, C_MR:C_MR + 2].unsqueeze(2).broadcast_to([P, 2, T])

            def copy_b(u, w, body, first=False):
                dve.wait_ge(wt_mm[1], 4 * body + 2 * u + w + 1)
                if not first:
                    dve.wait_ge(xb_mm[u], 2 * body)
                dve.tensor_copy(bt[:, u, w, 4:8, :], ps[:, 1, :].rearrange(
                    "p (k c) -> p k c", k=4)).then_inc(wt_ok[1], 1)

            def split(u, body, first=False):
                for w, dst in enumerate((btc, xb2)):
                    dve.wait_ge(xb_mm[u], 2 * body + 2)
                    if not first:
                        dve.wait_ge(c_mm[u], body)
                    dve.tensor_tensor(dst[:, u, 0:P].rearrange("p (q t) -> p q t", q=2),
                                      ps[:, 2 + u, w * P:(w + 1) * P]
                                      .rearrange("p (q t) -> p q t", q=2), mr, ALU.mult
                                      ).then_inc(bn_ok[u], 1)
                dve.wait_ge(bn_ok[u], 2 * body + 1)
                dve.tensor_tensor(btc[:, u, P:P + T], btc[:, u, 0:T], btc[:, u, T:P], ALU.add
                                  ).then_inc(cp_ok[u], 1)

            def minus(u, k, body):
                dve.wait_ge(s_ln[u], 2 * body + k + 1)
                dve.scalar_tensor_tensor(out=prob[:, u, 2 * k:2 * k + 2, :],
                                         in0=ps[:, 4 + 2 * k:6 + 2 * k, 0:H * T], scalar=0.0,
                                         in1=soft[:, u, 2 * k:2 * k + 2, :], op0=ALU.min,
                                         op1=ALU.subtract).then_inc(s_min[u], 1)

            def diag_o(u, body):
                dve.wait_ge(o_mm[u], 4 * body + 4)
                dve.tensor_tensor(obd[:, u, :].rearrange("p (h q t) -> p h q t", h=H, q=2),
                                  bc(ps[:, 2 + u, 0:256].rearrange("p (h t) -> p h t", h=H), 2,
                                     [P, H, 2, T]),
                                  con[:, C_MR:C_MR + 2].unsqueeze(1).unsqueeze(3)
                                  .broadcast_to([P, H, 2, T]), ALU.mult).then_inc(obd_ok[u], 1)

            def u2(u, body):
                dve.wait_ge(c_mm[u], body + 1)
                v = ps[:, 2 + u, 256:320].rearrange("p (j r) -> p j r", r=R)
                dve.tensor_tensor(bn2[:, u, :].rearrange("p (j q r) -> p j q r", q=2, r=R),
                                  bc(v, 2, [P, 4, 2, R]), mq, ALU.mult).then_inc(b2_ok[u], 1)
                dve.tensor_copy(u2_all[:, bass.ds((2 * body + u) * 4, 4), :], v
                                ).then_inc(u2_ok[u], 1)

            def logits(u, body, first=False):
                dve.wait_ge(lg_mm[u], body + 1)
                v = ps[:, 2 + u, 0:4 * NLG].rearrange("p (j c) -> p j c", c=NLG)
                dve.tensor_copy(lg_all[:, bass.ds((2 * body + u) * 4, 4), :], v[:, :, 0:24])
                dve.wait_ge(u2_ok[u], body + 1)
                if not first:
                    dve.wait_ge(ms_ok[u], body)
                g = gy[:, u, :].rearrange("p (j r) -> p j r", r=R)
                dve.tensor_tensor(g, v[:, :, 24:NLG], u2_all[:, bass.ds((2 * body + u) * 4, 4), :],
                                  ALU.mult).then_inc(gy_ok[u], 1)
                dve.wait_ge(gy_ok[u], body + 1)
                dve.tensor_reduce(ms_all[:, bass.ds((2 * body + u) * 4, 4)], g, AX, ALU.add
                                  ).then_inc(ms_ok[u], 1)

            def k_diff(c, n, batch, row):
                dve.wait_ge(k_ln[c], batch * 99 + n + 1)
                src = (lrow if row else lcol)[:, c, :].rearrange("p (t j) -> p t j", j=4)
                dve.tensor_tensor(dif[:, c, 0:3 * CP].rearrange("p (t j) -> p t j", j=3),
                                  src[:, :, 1:4], src[:, :, 0:3], ALU.subtract
                                  ).then_inc(k_dif[c], 1)

            def k_scan(c, n, batch, row):
                dve.wait_ge(k_rho[c], batch * 99 + n)
                dve.tensor_tensor_scan(st[:, c, :], rho[:, c, :], (kr if row else kc)[:, c, :],
                                       0.0, ALU.mult, ALU.add).then_inc(k_sum[c], 1)

            def k_steps(m0, m1, nb, batch):
                for m in range(m0, m1):
                    for c in range(NCHAIN):
                        k_scan(c, nb + m, batch, m % 2 == 1)
                    for c in range(NCHAIN):
                        k_diff(c, nb + m, batch, m % 2 == 1)

            def k_start(batch):
                for c in range(NCHAIN):
                    p0 = (batch * NCHAIN + c) * CP
                    e = batch * 12
                    z = z24[:, c, :, :]
                    z4 = zz[:, c, :].rearrange("p (t i j) -> p t i j", i=4, j=4)
                    s4 = small[:, c, :].rearrange("p (t i) -> p t i", i=4)
                    d4 = dif[:, c, :].rearrange("p (t i) -> p t i", i=4)
                    h4 = hp[:, c, :, :].rearrange("p t (w j) -> p t w j", w=2)
                    s2 = lrow[:, c, 0:2 * CP].rearrange("p (t w) -> p t w", w=2)
                    dve.wait_ge(k_ia[c], batch * 4 + 2)
                    for u in range(2):
                        dve.wait_ge(ms_ok[u], (batch + 1) * BPB)
                    dve.tensor_tensor(z, lg_all[:, p0:p0 + CP, :],
                                      bc(rstd[:, c, :], 2, [P, CP, 24]), ALU.mult
                                      ).then_inc(k_i[c], 1)
                    dve.wait_ge(k_i[c], e + 1)
                    dve.tensor_tensor(z, z, bc(base24[:, :], 1, [P, CP, 24]), ALU.add
                                      ).then_inc(k_i[c], 1)
                    dve.wait_ge(k_i[c], e + 2)
                    dve.tensor_scalar(zz[:, c, :].rearrange("p (t i) -> p t i", i=16),
                                      z[:, :, 0:16], 1.0 / TAU, None, ALU.mult
                                      ).then_inc(k_i[c], 1)
                    dve.wait_ge(k_i[c], e + 3)
                    dve.tensor_reduce(s4, z4, AX, ALU.max).then_inc(k_i[c], 1)
                    dve.wait_ge(k_i[c], e + 4)
                    dve.tensor_tensor(z4, z4, bc(s4, 3, [P, CP, 4, 4]), ALU.subtract
                                      ).then_inc(k_i[c], 1)
                    dve.tensor_reduce(s2, z[:, :, 16:24].rearrange("p t (w j) -> p t w j", w=2), AX,
                                      ALU.max).then_inc(k_i[c], 1)
                    dve.wait_ge(k_i[c], e + 6)
                    dve.tensor_tensor(h4, z[:, :, 16:24].rearrange("p t (w j) -> p t w j", w=2),
                                      bc(s2, 3, [P, CP, 2, 4]), ALU.subtract).then_inc(k_i[c], 1)
                    dve.tensor_reduce(d4, z4.rearrange("p t i j -> p t j i"), AX, ALU.max
                                      ).then_inc(k_i[c], 1)
                    dve.wait_ge(k_i[c], e + 8)
                    dve.wait_ge(k_ia[c], batch * 4 + 3)
                    dve.tensor_tensor(z4, z4, bc(d4, 2, [P, CP, 4, 4]), ALU.subtract
                                      ).then_inc(k_i[c], 1)
                    dve.tensor_reduce(s4, st[:, c, :].rearrange("p (t i j) -> p t i j", i=4, j=4),
                                      AX, ALU.add).then_inc(k_sum[c], 1)
                    dve.wait_ge(k_ia[c], batch * 4 + 4)
                    dve.tensor_reduce(s2, h4, AX, ALU.add).then_inc(k_i[c], 1)
                    dve.wait_ge(k_i[c], e + 10)
                    dve.reciprocal(s2, s2).then_inc(k_i[c], 1)
                    dve.wait_ge(k_i[c], e + 11)
                    dve.tensor_tensor(h4, h4, bc(s2, 3, [P, CP, 2, 4]), ALU.mult
                                      ).then_inc(k_i[c], 1)
                for c in range(NCHAIN):
                    dve.wait_ge(k_i[c], batch * 12 + 12)
                    k_diff(c, 0, batch, True)
                    dve.wait_ge(k_m[c], batch + 1)

            def k_middle(batch):
                for c in range(NCHAIN):
                    k_scan(c, HALF - 1, batch, False)
                for c in range(NCHAIN):
                    l4 = lrow[:, c, :].rearrange("p (t i) -> p t i", i=4)
                    s4 = small[:, c, :].rearrange("p (t i) -> p t i", i=4)
                    z4 = zz[:, c, :].rearrange("p (t i j) -> p t i j", i=4, j=4)
                    dve.tensor_tensor(s4, l4[:, :, 3:4].broadcast_to([P, CP, 4]), l4, ALU.subtract
                                      ).then_inc(k_b[c], 1)
                    dve.wait_ge(k_b[c], 2 * batch + 1)
                    dve.tensor_tensor(z4, z4, bc(s4, 3, [P, CP, 4, 4]), ALU.add).then_inc(k_b[c], 1)
                    dve.wait_ge(k_b[c], 2 * batch + 2)
                    dve.wait_ge(k_ln[c], batch * 99 + HALF)
                    dve.tensor_tensor(z4, z4, bc(lcol[:, c, :].rearrange("p (t j) -> p t j", j=4), 2,
                                                 [P, CP, 4, 4]), ALU.subtract).then_inc(k_dif[c], 1)
                for c in range(NCHAIN):
                    dve.wait_ge(k_rho[c], batch * 99 + HALF)
                    dve.tensor_reduce(small[:, c, :].rearrange("p (t i) -> p t i", i=4),
                                      kr[:, c, :].rearrange("p (t i j) -> p t i j", i=4, j=4), AX,
                                      ALU.add).then_inc(k_sum[c], 1)
                    k_diff(c, HALF, batch, True)

            def k_final(batch):
                for c in range(NCHAIN):
                    e = batch * 5
                    p0 = (batch * NCHAIN + c) * CP
                    s4 = small[:, c, :].rearrange("p (t i) -> p t i", i=4)
                    d4 = dif[:, c, :].rearrange("p (t i) -> p t i", i=4)
                    t4 = st[:, c, :].rearrange("p (t i j) -> p t i j", i=4, j=4)
                    k4 = kr[:, c, :].rearrange("p (t i j) -> p t i j", i=4, j=4)
                    dve.wait_ge(k_rho[c], batch * 99 + 99)
                    dve.reciprocal(s4, t4[:, :, :, 3]).then_inc(k_f[c], 1)
                    dve.wait_ge(k_f[c], e + 1)
                    dve.tensor_tensor(t4, k4, bc(s4, 3, [P, CP, 4, 4]), ALU.mult
                                      ).then_inc(k_f[c], 1)
                    dve.wait_ge(k_f[c], e + 2)
                    dve.tensor_reduce(d4, t4.rearrange("p t i j -> p t j i"), AX, ALU.add
                                      ).then_inc(k_f[c], 1)
                    dve.wait_ge(k_f[c], e + 3)
                    dve.reciprocal(s4, d4).then_inc(k_f[c], 1)
                    dve.wait_ge(k_f[c], e + 4)
                    dve.tensor_tensor(t4, t4, bc(s4, 2, [P, CP, 4, 4]), ALU.mult
                                      ).then_inc(k_f[c], 1)
                    dve.wait_ge(k_f[c], e + 5)
                    dd = d_all[:, p0:p0 + CP, :].rearrange("p t (n w j) -> p t n w j", n=4, w=2)
                    dve.scalar_tensor_tensor(
                        out=dd[:, :, :, 0, :].rearrange("p t n j -> p t n j"),
                        in0=t4, scalar=gate[:, 3:4],
                        in1=bc(eyeg[:, :].rearrange("p (i j) -> p i j", i=4), 1, [P, CP, 4, 4]),
                        op0=ALU.mult, op1=ALU.add).then_inc(d_ok[c], 1)
                    dve.tensor_tensor(dd[:, :, :, 1, :],
                                      bc(hp[:, c, :, 4:8], 3, [P, CP, 4, 4]),
                                      bc(hp[:, c, :, 0:4], 2, [P, CP, 4, 4]), ALU.mult
                                      ).then_inc(d_ok[c], 1)
                for c in range(NCHAIN):
                    dve.wait_ge(d_ok[c], 2 * batch + 2)

            def slot(f, b, first=False, k=lambda m0, m1: None):
                k(0, 1)
                if f:
                    copy_b(f[0], 0, f[1], first)
                k(1, 2)
                if b:
                    minus(b[0], 0, b[1])
                k(2, 3)
                if f:
                    copy_b(f[0], 1, f[1], first)
                k(3, 4)
                if b:
                    minus(b[0], 1, b[1])
                k(4, 7)
                if b:
                    diag_o(*b)
                k(7, 9)
                if f:
                    split(*f, first)
                k(9, 10)
                if b:
                    u2(*b)
                k(10, 12)
                if b:
                    logits(*b, first)

            def body_a(body, nb=None, batch=0, first=False, last=False):
                def k(n):
                    if nb is None:
                        return lambda m0, m1: None
                    return lambda m0, m1: k_steps(n + m0, n + m1, nb, batch)
                slot((1, body), (0, body), first, k(0))
                slot(None if last else (0, body + 1), (1, body), False, k(12))

            def add(u, half, j, body):
                dve.wait_ge(f_mm[j], 4 * body + 2 * u + half + 1)
                if half == 0:
                    dve.wait_ge(x_in[2 * u + j // 2], 16 * (NBODY + body + 1))
                v = xt[:, u, j, half * 512:(half + 1) * 512]
                dve.tensor_tensor(v, v, ps[:, 4 + j, :], ALU.add).then_inc(f_ok[j], 1)

            def body_c(body, nb=None, batch=0):
                for n in range(16):
                    add(n // 8, n // 4 % 2, n % 4, body)
                    if nb is not None:
                        k_steps(3 * n // 2, 3 * (n + 1) // 2, nb, batch)

            slot((0, 0), None, first=True)
            body_a(0, first=True)
            with dve.Fori(1, BPB) as i:
                body_a(i)
            k_start(0)
            with dve.Fori(0, 2) as i:
                body_a(BPB + i, 1 + i * PER_BODY, 0)
            k_middle(0)
            for i in range(2):
                body_a(BPB + 2 + i, HALF + 1 + i * PER_BODY, 0, last=(i == 1))
            k_final(0)
            k_start(1)
            with dve.Fori(0, 2) as i:
                body_c(i, 1 + i * PER_BODY, 1)
            k_middle(1)
            with dve.Fori(0, 2) as i:
                body_c(2 + i, HALF + 1 + i * PER_BODY, 1)
            k_final(1)
            with dve.Fori(0, BPB) as i:
                body_c(BPB + i)

        @block.gpsimd
        def _(pool):
            def fetch_b(u):
                for w, src in enumerate(("b1r", "b2r")):
                    pool.indirect_dma_start(
                        brow[:, u, w, :], None, io[src],
                        bass.IndirectOffsetOnAxis(idx_now[:, u, 2 * w:2 * w + 1], 0)
                        ).then_inc(b_in[u], 16)

            def fetch_rows(u):
                for k, (dst, tab) in enumerate(((m_g, tab_m), (c_g, tab_c), (lg_g, tab_lg))):
                    pool.indirect_dma_start(dst[:, u, :], None, tab,
                                            bass.IndirectOffsetOnAxis(idx_now[:, u, k:k + 1], 0)
                                            ).then_inc(rows_in[u], 16)

            pool.wait_ge(idx_ok, 2)
            for u in range(2):
                pool.tensor_copy(idx_now[:, u, :], idx[:, u, :]).then_inc(nx_ok[u], 1)
                pool.wait_ge(nx_ok[u], 1)
                fetch_b(u)
            pool.wait_ge(tab_out, 32)
            pool.wait_ge(tc_out, 32)
            pool.wait_ge(tg_out, 144)
            fetch_rows(0)
            fetch_rows(1)
            m8 = con[:, C_M8:C_M8 + 8]
            m4 = con[:, C_M4:C_M4 + 4]

            def spread_m(u, body, first=False):
                pool.wait_ge(rows_in[u], 48 * (body + 1))
                if not first:
                    pool.wait_ge(q_mm[u], body)
                pool.tensor_tensor(mbd[:, u, :, :].rearrange("p h (k r) -> p h k r", r=R),
                                   bc(m_g[:, u, :].rearrange("p (h r) -> p h r", r=R), 2,
                                      [P, H, 8, R]),
                                   m8.unsqueeze(1).unsqueeze(3).broadcast_to([P, H, 8, R]),
                                   ALU.mult).then_inc(bd_ok[u], 1)

            def spread_cl(u, body, first=False):
                if not first:
                    pool.wait_ge(c_mm[u], body)
                pool.tensor_tensor(cbd[:, u, :, :].rearrange("p h (j r) -> p h j r", r=R),
                                   bc(c_g[:, u, :].rearrange("p (h r) -> p h r", r=R), 2,
                                      [P, H, 4, R]),
                                   m4.unsqueeze(1).unsqueeze(3).broadcast_to([P, H, 4, R]),
                                   ALU.mult).then_inc(bd_ok[u], 1)
                if not first:
                    pool.wait_ge(lg_mm[u], body)
                pool.tensor_tensor(lbd[:, u, :].rearrange("p (j c) -> p j c", c=NLG),
                                   bc(lg_g[:, u, :], 1, [P, 4, NLG]),
                                   bc(m4, 2, [P, 4, NLG]), ALU.mult).then_inc(bd_ok[u], 1)

            def mask(u, k, body):
                pool.wait_ge(s_exp[u], 2 * body + k + 1)
                v = prob[:, u, 2 * k:2 * k + 2, :].rearrange("p j (h t) -> p (j h) t", h=H)
                pool.tensor_tensor(v, v, bc(con[:, C_CAU:C_CAU + T], 1, [P, 2 * H, T]), ALU.mult
                                   ).then_inc(p_ok[u], 1)

            def next_rows(u, body, first):
                pool.wait_ge(b_in[u], 32 * (body + 1))
                for k in range(2):
                    pool.wait_ge(wt_mm[k], 4 * body + 2 * u + 2)
                pool.tensor_copy(idx_now[:, u, :], idx[:, bass.ds(2 * body + 2 + u, 1), :]
                                 .rearrange("p g k -> p (g k)")).then_inc(nx_ok[u], 1)
                pool.wait_ge(nx_ok[u], body + 2)
                pool.wait_ge(bd_ok[u], 3 * (body + 1))

            def slot(f, b, first=False, fetch=True):
                if f:
                    spread_m(*f, first)
                    spread_cl(*f, first)
                    if fetch:
                        next_rows(*f, first)
                if b:
                    mask(b[0], 0, b[1])
                    mask(b[0], 1, b[1])
                if f and fetch:
                    fetch_b(f[0])
                    fetch_rows(f[0])

            def body_a(body, first=False, last=False, next_last=False):
                slot((1, body), (0, body), first, fetch=not last)
                slot(None if last else (0, body + 1), (1, body), fetch=not next_last)

            slot((0, 0), None, first=True)
            body_a(0, first=True)
            with pool.Fori(1, NBODY - 2) as body:
                body_a(body)
            body_a(NBODY - 2, next_last=True)
            body_a(NBODY - 1, last=True)

            def attn_rows(u, body, first=False):
                g = bass.ds(2 * body + u, 1)
                if not first:
                    pool.wait_ge(f_mm[3], 4 * body + 2 * u - 2)
                    pool.wait_ge(av_in[u], 16 * body)
                pool.tensor_copy(idx_av[:, u:u + 1], idx[:, g, 0]).then_inc(ix_ok[u], 1)
                pool.wait_ge(ix_ok[u], body + 1)
                pool.tensor_tensor(obd[:, u, :].rearrange("p (h q t) -> p h q t", h=H, q=2),
                                   bc(o_all[:, g, :].rearrange("p g (h t) -> p (g h) t", h=H), 2,
                                      [P, H, 2, T]),
                                   con[:, C_MR:C_MR + 2].unsqueeze(1).unsqueeze(3)
                                   .broadcast_to([P, H, 2, T]), ALU.mult).then_inc(ob_ok[u], 1)
                pool.indirect_dma_start(av[:, u, :], None, tab_av,
                                        bass.IndirectOffsetOnAxis(idx_av[:, u:u + 1], 0)
                                        ).then_inc(av_in[u], 16)

            def spread_u2(u, j, body, first=False):
                b, n = j % 2, 4 * u + j
                pair = bass.ds((2 * body + u) * 4 + j, 1)
                if not (first and n < 2):
                    pool.wait_ge(ut_mm[b], 4 * body + n // 2)
                pool.tensor_tensor(ubuf[:, b, :].rearrange("p (k r) -> p k r", r=R),
                                   bc(d_all[:, pair, :].rearrange("p g k -> p (g k)"), 2,
                                      [P, 32, R]),
                                   u2_all[:, pair, :].broadcast_to([P, 32, R]), ALU.mult
                                   ).then_inc(u_ok[b], 1)

            def rows_and_u(u, body, first=False):
                for j in range(4):
                    spread_u2(u, j, body, first)
                attn_rows(u, body, first)

            def body_c(body, first=False, last=False):
                rows_and_u(1, body, first)
                if not last:
                    rows_and_u(0, body + 1)

            for u in range(2):
                pool.wait_ge(c_mm[u], NBODY)
                pool.wait_ge(oc_ok[u], NBODY)
                pool.wait_ge(u2_ok[u], NBODY)
                pool.wait_ge(tw_out[u], 16 * 16)
            for batch in range(NBATCH):
                for c in range(NCHAIN):
                    pool.wait_ge(d_ok[c], 2 * (batch + 1))
                b0, first = batch * BPB, batch == 0
                rows_and_u(0, b0, first)
                body_c(b0, first)
                with pool.Fori(b0 + 1, b0 + BPB - 1) as body:
                    body_c(body)
                body_c(b0 + BPB - 1, last=True)


def constants():
    import numpy as np
    p = np.arange(P)
    con = np.zeros((P, NCON), np.float32)
    con[:, C_ID:C_ID + P] = np.eye(P)
    c = np.arange(4 * R)
    con[:, C_SEL:C_SEL + 4 * R] = (p[:, None] // (2 * R) == c // R) & (p[:, None] % R == c % R)
    con[:, C_MQ:C_MQ + 2] = (p[:, None] // T) == np.arange(2)
    con[:, C_MR:C_MR + 2] = (p[:, None] // R % 2) == np.arange(2)
    con[:, C_M8:C_M8 + 8] = (p[:, None] // R) == np.arange(8)
    con[:, C_M4:C_M4 + 4] = (p[:, None] // (2 * R)) == np.arange(4)
    con[:, C_CAU:C_CAU + T] = (p[:, None] % T) <= np.arange(T)
    con[:, C_EYE:C_EYE + 16] = np.eye(4).reshape(-1)
    rowno = np.broadcast_to((p % R).astype(np.int32)[:, None], (P, NGRP))
    return con, np.ascontiguousarray(rowno)


def kernel(**inputs):
    import numpy as np
    import concourse.bacc as bacc
    from concourse.bass_utils import run_bass_kernel_spmd

    v = {k: np.asarray(a) for k, a in inputs.items()}
    con, rowno = constants()
    a1, b1 = v["L0_cond_A"], v["L0_cond_B"]
    a2, b2 = v["L0_cond2_A"], v["L0_cond2_B"]
    i1, i2 = v["itok_B_3_7"], v["itok_B_4_50"]

    def rows(i):
        return np.repeat(i.reshape(NGRP, 8).T, R, axis=0)

    def by_channel(w):
        return w.reshape(w.shape[0], R, NCH, P).transpose(0, 3, 2, 1)

    arrays = {
        "x": v["x"].reshape(NPAIR, 2, T, NCH, P).transpose(0, 4, 3, 1, 2).reshape(NPAIR, P, NCH * P),
        "xrow": v["x"].reshape(NPAIR, P, D), "ids2": i2, "id1r": rows(i1), "id2r": rows(i2), "rowno": rowno, "con": con,
        "a1c": a1.reshape(NA1, NCH, P, R).transpose(2, 1, 0, 3).reshape(P, D),
        "a1t": a1.transpose(0, 2, 1).reshape(NA1 * R, D),
        "b1r": b1.reshape(NA1 * R, D), "b2r": b2.reshape(NA2 * R, D),
        "b2g": by_channel(b2).reshape(NA2, P, NCH * R),
        "a2c": a2.reshape(NA2, NCH, P, R).transpose(2, 1, 0, 3).reshape(P, NCH * NA2 * R),
        "a2t": a2.reshape(NA2, H, HD, R).transpose(0, 1, 3, 2).reshape(NA2, H * R, HD),
        "bv": np.stack([v["L0_attn_bv_q"], v["L0_attn_bv_k"], v["L0_attn_bv_v"]]),
        "wct": np.concatenate([v["L0_ffn_W_res"], v["L0_ffn_W_pre"], v["L0_ffn_W_post"]])
        .reshape(24, NCH, P).transpose(2, 1, 0).reshape(P, NCH * 24),
        "w_branch": v["L0_ffn_W_branch"],
        "h_res": v["L0_ffn_H_res_base"].reshape(-1), "h_pre": v["L0_ffn_H_pre_base"],
        "h_post": v["L0_ffn_H_post_base"], "gate": v["L0_ffn_gate"],
    }
    arrays = {k: np.ascontiguousarray(a) for k, a in arrays.items()}
    nc = bacc.Bacc("TRN2", target_bir_lowering=False, num_devices=1)
    io = {k: nc.dram_tensor(f"in_{k}", a.shape, mybir.dt.from_np(a.dtype), kind="ExternalInput").ap()
          for k, a in arrays.items()}
    io["out"] = nc.dram_tensor("out", (NPAIR, P, D), F32, kind="ExternalOutput").ap()
    program(nc, io)
    r = run_bass_kernel_spmd(nc, [{f"in_{k}": a for k, a in arrays.items()}], core_ids=[0])
    return r.results[0]["out"].reshape(B, T, D)
```

```python
from contextlib import ExitStack

import concourse.bass as bass
from concourse import mybir

ALU = mybir.AluOpType
ACT = mybir.ActivationFunctionType
AX = mybir.AxisListType.X
F32 = mybir.dt.float32
I32 = mybir.dt.int32
U32 = mybir.dt.uint32

P = 128
B, T, D = 128, 64, 1024
H, HD, R = 4, 256, 16
NA1, NA2 = 8, 64
NPAIR = B // 2
NGRP = NPAIR // 4
NBODY = NGRP // 2
NCH = D // P
NLG = 24 + R
TAU = 0.1
EPS = 1.1920929e-07
SCALE = 4.0 * float(HD) ** -0.5
CP = 16
NCHAIN = 2
NBATCH = NPAIR // (CP * NCHAIN)
HALF = 50
PER_BODY = 24
EARLY = 36
START = 4
SETUP_BODY = (2 * PER_BODY + START) // 2
BPB = NBODY // NBATCH

C_ID, C_SEL, C_MQ, C_MR, C_M8, C_M4, C_CAU, C_EYE = 0, 128, 192, 194, 196, 204, 208, 272
NCON = 288


def program(nc, io):
    with ExitStack() as ctx:
        def sb(name, shape, dt=F32):
            return ctx.enter_context(nc.sbuf_tensor(name, shape, dt))

        def sem(name, n=None):
            if n is None:
                return ctx.enter_context(nc.semaphore(name))
            return [ctx.enter_context(nc.semaphore(f"{name}{i}")) for i in range(n)]

        tab_m = nc.dram_tensor("tab_m", [NA1 * R, H * R], F32).ap()
        tab_c = nc.dram_tensor("tab_c", [NA1 * R * NA2, H * R], F32).ap()
        tab_lg = nc.dram_tensor("tab_lg", [NA2 * R, NLG], F32).ap()
        tab_av = nc.dram_tensor("tab_av", [NA1 * R, D], F32).ap()
        tab_t2 = nc.dram_tensor("tab_t2", [NA2, P, HD], F32).ap()

        con = sb("con", [P, NCON])
        ident = con[:, C_ID:C_ID + P]
        select = con[:, C_SEL:C_SEL + 4 * R]
        ids = sb("ids", [1, B], I32)
        rowno = sb("rowno", [P, NGRP], I32)
        id1r = sb("id1r", [P, NGRP], I32)
        id2r = sb("id2r", [P, NGRP], I32)
        idx = sb("idx", [P, NGRP, 3], U32)
        idx_now = sb("idx_now", [P, 2, 3], U32)
        m_g = sb("m_g", [P, 2, H * R])
        c_g = sb("c_g", [P, 2, H * R])
        lg_g = sb("lg_g", [P, 2, NLG])
        o_all = sb("o_all", [P, NGRP, H * T])
        lg_all = sb("lg_all", [P, NPAIR, 24])
        ms_all = sb("ms_all", [P, NPAIR])
        u2_all = sb("u2_all", [P, NPAIR, R])
        d_all = sb("d_all", [P, NPAIR, H * 8])
        base24 = sb("base24", [P, 24])
        gate = sb("gate", [P, 6])
        eyeg = sb("eyeg", [P, 16])

        xt = sb("xt", [P, 2, 4, NCH * P])
        b2_tab = xt[:, :, :, :].rearrange("p u j c -> p (u j c)")
        brow = sb("brow", [P, 2, 2, D])
        bt = sb("bt", [P, 2, 2, NCH, P])
        cbuf = sb("cbuf", [P, 8192])
        a2_tab = cbuf[:, :]
        ut = cbuf[:, 0:4096].rearrange("p (u j c) -> p u j c", u=2, j=4)
        t2 = cbuf[:, 4096:8192].rearrange("p (u k c) -> p u k c", u=2, k=8)
        av = sb("av", [P, 2, D])
        soft = sb("soft", [P, 2, 4, H * T])
        prob = sb("prob", [P, 2, 4, H * T])
        c_stage = bt[:, :, :, :, :].rearrange("p u w k c -> p (u w k c)")
        obd = sb("obd", [P, 2, H * P])
        ubuf = sb("ubuf", [P, 2, H * P])
        mbd = sb("mbd", [P, 2, H, P])
        cbd = sb("cbd", [P, 2, H, 4 * R])
        lbd = sb("lbd", [P, 2, 4 * NLG])
        bn1 = sb("bn1", [P, 2, P])
        bn2 = sb("bn2", [P, 2, P])
        xb2 = sb("xb2", [P, 2, P])
        btc = sb("btc", [P, 2, P + T])
        qt = sb("qt", [P, 2, H * T])
        b2t = sb("b2t", [P, 2, P])
        gy = sb("gy", [P, 2, 4 * R])

        z24 = sb("z24", [P, NCHAIN, CP, 24])
        zz = sb("zz", [P, NCHAIN, 16 * CP])
        kr = sb("kr", [P, NCHAIN, 16 * CP])
        kc = sb("kc", [P, NCHAIN, 16 * CP])
        rho = sb("rho", [P, NCHAIN, 16 * CP])
        st = sb("st", [P, NCHAIN, 16 * CP])
        lrow = sb("lrow", [P, NCHAIN, 4 * CP])
        lcol = sb("lcol", [P, NCHAIN, 4 * CP])
        dif = sb("dif", [P, NCHAIN, 4 * CP])
        small = sb("small", [P, NCHAIN, 4 * CP])
        hp = sb("hp", [P, NCHAIN, CP, 8])
        hsum = sb("hsum", [P, NCHAIN, 2 * CP])
        rstd = sb("rstd", [P, NCHAIN, CP])

        ps = ctx.enter_context(nc.psum_tensor("ps", [P, 8, 512], F32))

        a1c = o_all[:, 0:4, :].rearrange("p g c -> p (g c)")
        a1qk = o_all[:, 4:8, :].rearrange("p g c -> p (g c)")
        a1v = o_all[:, 8:12, :].rearrange("p g c -> p (g c)")
        a1t = o_all[:, 12:16, :].rearrange("p g c -> p (g c)")
        wct = ubuf[:, 0, 0:NCH * 24]
        wbr = ubuf[:, 1, :]
        bvt = sb("bvt", [H, 3, HD])
        bst = sb("bst", [H, 3, HD])
        bal = sb("bal", [H, 4])
        vqc = sb("vqc", [P, 2, 2, H])
        mst = mbd[:, 0, :, :]
        c24 = mbd[:, 0, :, :].rearrange("p h c -> p (h c)")
        ws = [av[:, u, :].rearrange("p (j c) -> p j c", j=H) for u in range(2)]
        ws += [soft[:, u, :, :].rearrange("p j c -> p (j c)").rearrange("p (j c) -> p j c", j=H)
               for u in range(2)]
        eps_c = sb("eps_c", [P, 1])
        idx_av = sb("idx_av", [P, 2], U32)
        mout = cbd[:, 0, 0, :]
        lgs = prob[:, 0, :, :].rearrange("p j c -> p (j c)")
        lgo = prob[:, 1, :, :].rearrange("p j c -> p (j c)")

        in_con = sem("in_con"); in_ids = sem("in_ids"); in_a1 = sem("in_a1"); in_b2 = sem("in_b2")
        in_a2 = sem("in_a2"); in_w = sem("in_w"); in_bv = sem("in_bv"); in_h = sem("in_h")
        bind = sem("bind"); bind_t = sem("bind_t"); bind_c = sem("bind_c")
        a1_scaled = sem("a1_scaled"); vrow = sem("vrow"); avt_made = sem("avt_made")
        tm_mm = sem("tm_mm"); tm_made = sem("tm_made")
        tc_mm = sem("tc_mm"); tc_ev = sem("tc_ev"); tc_out = sem("tc_out")
        tl_mm = sem("tl_mm"); tl_ev = sem("tl_ev"); tl_t = sem("tl_t"); tl_ev2 = sem("tl_ev2")
        tw_mm = sem("tw_mm"); tw_ev = sem("tw_ev")
        tw_out = sem("tw_out", 4)
        tab_out = sem("tab_out"); tg_out = sem("tg_out")
        gexp = sem("gexp"); link_ok = sem("link_ok"); ix_ok = sem("ix_ok", 2)
        idx_ok = sem("idx_ok"); nx_ok = sem("nx_ok", 2)
        t2_copy = sem("t2_copy"); zeros_ok = sem("zeros_ok")

        x_in = sem("x_in", 4); b_in = sem("b_in", 2); rows_in = sem("rows_in", 2)
        wt_mm = sem("wt_mm", 2); wt_ok = sem("wt_ok", 2); cp_ok = sem("cp_ok", 2)
        xb_mm = sem("xb_mm", 2); bn_ok = sem("bn_ok", 2)
        bt_ok = sem("bt_ok", 2); q_mm = sem("q_mm", 2); q_ok = sem("q_ok", 2)
        s_mm = sem("s_mm", 2); s_abs = sem("s_abs", 2); s_e = sem("s_e", 2); s_ln = sem("s_ln", 2)
        s_min = sem("s_min", 2); s_exp = sem("s_exp", 2); p_ok = sem("p_ok", 2)
        p_ok2 = sem("p_ok2", 2)
        o_mm = sem("o_mm", 2); obd_ok = sem("obd_ok", 2); oc_ok = sem("oc_ok", 2)
        c_mm = sem("c_mm", 2); b2_ok = sem("b2_ok", 2)
        u2_ok = sem("u2_ok", 2); b2t_mm = sem("b2t_mm", 2); b2t_ok = sem("b2t_ok", 2)
        lg_mm = sem("lg_mm", 2); gy_ok = sem("gy_ok", 2)
        ms_ok = sem("ms_ok", 2); bd_ok = sem("bd_ok", 2)

        k_sum = sem("k_sum", 2); k_ln = sem("k_ln", 2); k_dif = sem("k_dif", 2)
        k_rho = sem("k_rho", 2); k_m = sem("k_m", 2); k_b = sem("k_b", 2)
        k_i = sem("k_i", 2); k_ia = sem("k_ia", 2); k_f = sem("k_f", 2)
        d_ok = sem("d_ok", 2)

        t2_in = sem("t2_in", 2); av_in = sem("av_in", 2); ob_ok = sem("ob_ok", 2)
        u_ok = sem("u_ok", 2); ut_mm = sem("ut_mm", 2); ut_ok = sem("ut_ok", 2)
        f_mm = sem("f_mm", 4); f_ok = sem("f_ok", 4); out_ok = sem("out_ok", 4)

        def bc(ap, axis, shape):
            return ap.unsqueeze(axis).broadcast_to(shape)

        block = ctx.enter_context(nc.Block())

        @block.sync
        def _(sp):
            sp.dma_start(ids[:, :], io["ids2"].unsqueeze(0)).then_inc(in_ids, 16)
            sp.dma_start(bvt[:, :, :], io["bv"].rearrange("k h c -> h k c")).then_inc(in_bv, 16)
            sp.dma_start(con[:, :], io["con"]).then_inc(in_con, 16)
            sp.dma_start(rowno[:, :], io["rowno"]).then_inc(in_con, 16)
            sp.dma_start(id1r[:, :], io["id1r"]).then_inc(in_con, 16)
            sp.dma_start(id2r[:, :], io["id2r"]).then_inc(in_con, 16)
            sp.dma_start(a1c, io["a1c"]).then_inc(in_a1, 16)
            sp.dma_start(a1t, io["a1t"]).then_inc(in_a1, 16)
            sp.dma_start(b2_tab.rearrange("p (i c) -> p i c", i=NA2),
                         io["b2g"].rearrange("i p c -> p i c")).then_inc(in_b2, 16)
            sp.dma_start(wct, io["wct"]).then_inc(in_w, 16)
            sp.dma_start(wbr.rearrange("p (k c) -> p k c", k=2),
                         io["w_branch"].rearrange("(k p) c -> p k c", p=P)).then_inc(in_w, 16)
            sp.dma_start(a2_tab, io["a2c"]).then_inc(in_a2, 16)
            for k, w in enumerate(("h_res", "h_pre", "h_post")):
                n0, n1 = (0, 16, 20, 24)[k:k + 2]
                sp.dma_start(base24[:, n0:n1], bass.AP(io[w].tensor, 0, [[0, P], [1, n1 - n0]])
                             ).then_inc(in_h, 16)
            sp.dma_start(gate[:, 0:1], bass.AP(io["gate"].tensor, 0, [[0, P], [1, 1]])
                         ).then_inc(in_h, 16)
            sp.wait_ge(avt_made, 2)
            sp.dma_start(tab_av, a1t).then_inc(tab_out, 16)
            sp.wait_ge(tm_made, 1)
            sp.dma_start(tab_m, mout).then_inc(tab_out, 16)
            sp.wait_ge(tc_ev, 16)
            sp.dma_start(tab_c.rearrange("(p i) c -> p (i c)", p=P), c_stage).then_inc(tc_out, 16)
            sp.wait_ge(tl_ev2, 4)
            sp.dma_start(tab_lg.rearrange("(k p) c -> p k c", p=P)[:, :, 0:24],
                         lgo[:, 0:8 * 24].rearrange("p (k c) -> p k c", c=24)).then_inc(tg_out, 16)
            sp.wait_ge(tl_ev, 5)
            gram = tab_lg.rearrange("(i k s r) c -> k s r i c", k=4, s=2, r=R)
            for k in range(4):
                for s in range(2):
                    p0 = (2 * k + s) * R
                    sp.dma_start(gram[k, s, :, :, 24:NLG],
                                 lgs[p0:p0 + R, 0:256].rearrange("p (i s c) -> p s i c", s=2, c=R)
                                 [:, s]).then_inc(tg_out, 16)
            sp.wait_ge(tc_mm, 16)

            def load_a(body, first=False):
                for u in range(2):
                    if not first:
                        sp.wait_ge(xb_mm[u], 2 * body)
                    for k in range(2):
                        sp.dma_start(xt[:, u, 2 * k:2 * k + 2, :],
                                     io["x"][bass.ds(((body * 2 + u) * 2 + k) * 2, 2)]
                                     .rearrange("n p c -> p n c")).then_inc(x_in[2 * u + k], 16)

            load_a(0, first=True)
            load_a(1)
            sp.dma_start(tab_t2[:, 0:H * R, :], io["a2t"]).then_inc(t2_copy, 16)
            with sp.Fori(2, NBODY) as body:
                load_a(body)
            sp.wait_ge(in_ids, 16)

            def adapters(u, body):
                return [sp.value_load(ids[0:1, bass.ds((body * 2 + u) * 8 + q, 1)], min_val=0,
                                      max_val=NA2 - 1) for q in range(8)]

            def load_t2(u, i2):
                for q in range(8):
                    sp.dma_start(t2[:, u, q, :],
                                 tab_t2[bass.ds(i2[q], 1)].rearrange("i k c -> (i k) c")
                                 ).then_inc(t2_in[u], 16)

            def load_x(u, body, first=False):
                for k in range(2):
                    if not first:
                        sp.wait_ge(out_ok[2 * u + k], 16 * body)
                    sp.dma_start(xt[:, u, 2 * k:2 * k + 2, :],
                                 io["xrow"][bass.ds(((body * 2 + u) * 2 + k) * 2, 2)]
                                 .rearrange("n p c -> p n c")).then_inc(x_in[2 * u + k], 16)

            def store_c(u, body):
                for k in range(2):
                    for j in (2 * k, 2 * k + 1):
                        sp.wait_ge(f_ok[j], 4 * body + 2 * u + 2)
                    sp.dma_start(io["out"][bass.ds(((body * 2 + u) * 2 + k) * 2, 2)]
                                 .rearrange("n p c -> p n c"),
                                 xt[:, u, 2 * k:2 * k + 2, :]).then_inc(out_ok[2 * u + k], 16)

            for u in range(2):
                sp.wait_ge(xb_mm[u], 2 * NBODY)
                for k in range(2):
                    sp.wait_ge(tw_out[2 * u + k], 16 * 8)
            sp.wait_ge(t2_copy, 16)
            sp.wait_ge(tw_mm, 32)
            for u in range(2):
                load_t2(u, adapters(u, 0))
                load_x(u, 0, first=True)
            with sp.Fori(0, NBODY - 1) as body:
                for u in range(2):
                    i2 = adapters(u, body + 1)
                    store_c(u, body)
                    load_t2(u, i2)
                    load_x(u, body + 1)
            for u in range(2):
                store_c(u, NBODY - 1)
            for k in range(4):
                sp.wait_ge(out_ok[k], 16 * NBODY)

        @block.tensor
        def _(pe):
            pe.wait_ge(in_con, 64)
            pe.wait_ge(bind, 1)
            for w in range(2):
                for k in range(2):
                    mm = pe.transpose(ps[:, 0, (2 * w + k) * H:(2 * w + k + 1) * H],
                                      bst[:, w, k * P:(k + 1) * P], ident[0:H, 0:H])
            mm.then_inc(bind_t, 1)
            for h in range(H):
                mm = pe.matmul(ps[:, 1 + h // 2, (h % 2) * HD:(h % 2 + 1) * HD],
                               ident[0:H, h:h + 1].broadcast_to([H, P]), bst[:, 1, :],
                               start=True, stop=True)
            mm.then_inc(vrow, 1)
            pe.wait_ge(a1_scaled, 2)
            for h in range(H):
                for k in range(2):
                    c = (2 * h + k) * P
                    mm = pe.matmul(ps[:, 3, h * P:(h + 1) * P], a1qk[:, c:c + P], a1c[:, c:c + P],
                                   start=(k == 0), stop=(k == 1))
            mm.then_inc(tm_mm, 1)
            pe.wait_ge(in_b2, 16)
            b2v = b2_tab.rearrange("p (i k r) -> p i k r", i=NA2, k=NCH)
            n = 0
            for half in range(2):
                for h in range(H):
                    for s in range(2):
                        if n >= 4:
                            pe.wait_ge(tc_ev, n - 3)
                        for k in range(2):
                            c = 2 * h + k
                            mm = pe.matmul(ps[:, 4 + n % 4, 0:HD], a1v[:, c * P:(c + 1) * P],
                                           b2v[:, 32 * half + 16 * s:32 * half + 16 * s + 16, c, :],
                                           start=(k == 0), stop=(k == 1))
                        mm.then_inc(tc_mm, 1)
                        n += 1
            pe.wait_ge(in_w, 32)
            pe.wait_ge(in_a2, 16)
            pe.wait_ge(bind_c, 1)
            pe.wait_ge(avt_made, 2)
            for c in range(NCH):
                for k in range(4):
                    mm = pe.matmul(ps[32 * k:32 * k + 24, 0, 0:256], wct[:, c * 24:(c + 1) * 24],
                                   a2_tab[:, c * D + k * 256:c * D + (k + 1) * 256],
                                   start=(c == 0), stop=(c == NCH - 1))
            mm.then_inc(tl_mm, 1)
            for i in range(8):
                for c in range(NCH):
                    for k in range(4):
                        a = a2_tab[:, c * D + (4 * i + k) * 2 * R:c * D + (4 * i + k + 1) * 2 * R]
                        mm = pe.matmul(ps[32 * k:32 * k + 32, 2, i * 2 * R:(i + 1) * 2 * R], a, a,
                                       start=(c == 0), stop=(c == NCH - 1))
            mm.then_inc(tl_mm, 1)
            pe.wait_ge(tl_ev, 4)
            pe.wait_ge(tc_ev, 16)
            for k in range(4):
                for s in range(2):
                    rows = slice(32 * k, 32 * k + 24)
                    mm = pe.matmul(ps[:, 4 + k, s * 24:(s + 1) * 24],
                                   c24[rows, s * P:(s + 1) * P], ident[rows, rows],
                                   start=True, stop=True)
            mm.then_inc(tl_t, 1)
            pe.wait_ge(tl_ev2, 4)
            for g in range(8):
                for j in range(H):
                    n = 4 * g + j
                    if n >= 4:
                        pe.wait_ge(tw_ev, n - 3)
                    for k in range(2):
                        c = 2 * j + k
                        mm = pe.matmul(ps[:, 4 + j, 0:HD],
                                       a2_tab[:, c * D + g * P:c * D + (g + 1) * P],
                                       wbr[:, k * HD:(k + 1) * HD], start=(k == 0), stop=(k == 1))
                    mm.then_inc(tw_mm, 1)

            def turn_b(u, body, first=False):
                pe.wait_ge(b_in[u], 32 * (body + 1))
                for w in range(2):
                    for k in range(2):
                        if not (first and u == 0 and w == 0):
                            pe.wait_ge(wt_ok[k], 4 * body + 2 * u + w)
                        for c in range(4):
                            mm = pe.transpose(ps[:, k, c * P:(c + 1) * P],
                                              brow[:, u, w, (4 * k + c) * P:(4 * k + c + 1) * P],
                                              ident)
                        mm.then_inc(wt_mm[k], 1)

            def xb(u, w, body, first=False):
                if w == 0:
                    for k in range(2):
                        pe.wait_ge(x_in[2 * u + k], 16 * (body + 1))
                    if not first:
                        pe.wait_ge(ms_ok[u], body)
                for k in range(2):
                    pe.wait_ge(wt_ok[k], 4 * body + 2 * u + w + 1)
                for c in range(NCH):
                    for j in range(4):
                        mm = pe.matmul(ps[32 * j:32 * j + 32, 2 + u, w * P:(w + 1) * P],
                                       bt[:, u, w, c, 32 * j:32 * j + 32],
                                       xt[:, u, j, c * P:(c + 1) * P],
                                       start=(c == 0), stop=(c == NCH - 1))
                mm.then_inc(xb_mm[u], 1)

            def turn(u, body):
                pe.wait_ge(bn_ok[u], 2 * body + 2)
                pe.transpose(ps[:, 2 + u, 256:384], btc[:, u, 0:P], ident)

            def query(u, body):
                pe.wait_ge(cp_ok[u], body + 1)
                pe.wait_ge(bd_ok[u], 3 * body + 1)
                for h in range(H):
                    mm = pe.matmul(ps[:, 2 + u, h * T:(h + 1) * T], mbd[:, u, h, :],
                                   btc[:, u, P:P + T], start=True, stop=True)
                mm.then_inc(q_mm[u], 1)

            def score(u, body, first=False):
                pe.wait_ge(q_ok[u], body + 1)
                if not (first and u == 0):
                    pe.wait_ge(s_min[1 - u], 2 * body + 2 * u)
                for j in range(4):
                    pe.matmul(ps[:, 4 + j, 0:H * T], btc[32 * j:32 * j + 32, u, 0:P],
                              qt[32 * j:32 * j + 32, u, :], start=True,
                              stop=True).then_inc(s_mm[u], 1)

            def attend(u, body):
                pe.wait_ge(p_ok[u], body + 1)
                pe.wait_ge(p_ok2[u], body + 1)
                pe.wait_ge(bt_ok[u], body + 1)
                for j in range(4):
                    pe.matmul(ps[32 * j:32 * j + 32, 2 + u, 0:H * T],
                              bn1[:, u, 32 * j:32 * j + 32], prob[:, u, j, :], start=True,
                              stop=True).then_inc(o_mm[u], 1)

            def cross(u, body):
                pe.wait_ge(obd_ok[u], body + 1)
                pe.wait_ge(oc_ok[u], body + 1)
                pe.wait_ge(bd_ok[u], 3 * body + 2)
                for h in range(H):
                    pe.matmul(ps[:, 2 + u, 256:320], obd[:, u, h * P:(h + 1) * P],
                              cbd[:, u, h, :], start=(h == 0), stop=False)
                pe.matmul(ps[:, 2 + u, 256:320], xb2[:, u, :], select, start=False,
                          stop=True).then_inc(c_mm[u], 1)

            def turn2(u, body):
                pe.wait_ge(b2_ok[u], body + 1)
                pe.wait_ge(u2_ok[u], body + 1)
                pe.transpose(ps[:, 2 + u, 320:448], bn2[:, u, :], ident).then_inc(b2t_mm[u], 1)

            def logit(u, body):
                pe.wait_ge(b2t_ok[u], body + 1)
                pe.wait_ge(bd_ok[u], 3 * body + 3)
                pe.matmul(ps[:, 2 + u, 0:4 * NLG], b2t[:, u, :], lbd[:, u, :], start=True,
                          stop=True).then_inc(lg_mm[u], 1)

            def slot(f, b, first=False):
                if f:
                    turn_b(*f, first)
                    xb(f[0], 0, f[1], first)
                if b:
                    attend(*b)
                if f:
                    xb(f[0], 1, f[1])
                if b:
                    cross(*b)
                if f:
                    turn(*f)
                    query(*f)
                if b:
                    turn2(*b)
                    logit(*b)
                if f:
                    score(*f, first)

            def body_a(body, first=False, last=False):
                slot((1, body), (0, body), first)
                slot(None if last else (0, body + 1), (1, body))

            pe.wait_ge(tl_ev, 5)
            pe.wait_ge(tw_ev, 32)
            slot((0, 0), None, first=True)
            body_a(0, first=True)
            with pe.Fori(1, NBODY - 1) as body:
                body_a(body)
            body_a(NBODY - 1, last=True)

            def turn_u(u, k, body, first=False):
                for j in (2 * k, 2 * k + 1):
                    n = 4 * u + j
                    pe.wait_ge(u_ok[j % 2], 4 * body + n // 2 + 1)
                    if not (first and n < 2):
                        pe.wait_ge(ut_ok[j % 2], 4 * body + n // 2)
                    for h in range(H):
                        mm = pe.transpose(ps[:, j % 2, h * P:(h + 1) * P],
                                          ubuf[:, j % 2, h * P:(h + 1) * P], ident)
                    mm.then_inc(ut_mm[j % 2], 1)

            def final(u, half, body, first=False):
                if half == 0:
                    pe.wait_ge(t2_in[u], 128 * (body + 1))
                    pe.wait_ge(av_in[u], 16 * (body + 1))
                    pe.wait_ge(ob_ok[u], body + 1)
                for k in range(2):
                    if half == 0:
                        pe.wait_ge(ut_ok[0], 4 * body + 2 * u + k + 1)
                        pe.wait_ge(ut_ok[1], 4 * body + 2 * u + k + 1)
                    for j in (2 * k, 2 * k + 1):
                        if not (first and u == 0 and half == 0):
                            pe.wait_ge(f_ok[j], 4 * body + 2 * u + half)
                        for h in range(2):
                            n = 2 * half + h
                            for q in range(2):
                                pe.matmul(ps[64 * q:64 * q + 64, 4 + j, h * HD:(h + 1) * HD],
                                          ut[:, u, j, n * P + 64 * q:n * P + 64 * q + 64],
                                          t2[:, u, 2 * j + q, :], start=(h == 0), stop=False,
                                          skip_group_check=True)
                    for h in range(2):
                        n = 2 * half + h
                        for j in (2 * k, 2 * k + 1):
                            rows = slice(32 * j, 32 * j + 32)
                            mm = pe.matmul(ps[:, 4 + j, h * HD:(h + 1) * HD],
                                           obd[rows, u, n * P:(n + 1) * P],
                                           av[rows, u, n * HD:(n + 1) * HD], start=False,
                                           stop=True, skip_group_check=True)
                            if h == 1:
                                mm.then_inc(f_mm[j], 1)

            def body_c(body, first=False, last=False):
                final(0, 0, body, first)
                turn_u(1, 0, body)
                final(0, 1, body)
                turn_u(1, 1, body)
                final(1, 0, body)
                if not last:
                    turn_u(0, 0, body + 1)
                final(1, 1, body)
                if not last:
                    turn_u(0, 1, body + 1)

            for u in range(2):
                pe.wait_ge(q_ok[u], NBODY)
                pe.wait_ge(s_min[u], 2 * NBODY)
            for batch in range(NBATCH):
                b0, first = batch * BPB, batch == 0
                for k in range(2):
                    turn_u(0, k, b0, first)
                body_c(b0, first=first)
                with pe.Fori(b0 + 1, b0 + BPB - 1) as body:
                    body_c(body)
                body_c(b0 + BPB - 1, last=True)

        @block.scalar
        def _(act):
            act.preload_act_table_set("natural_log_exp_and_others")
            for n in range(16):
                act.wait_ge(tc_mm, n + 1)
                half, h, s = n // 8, (n // 2) % 4, n % 2
                i0 = 32 * half + 16 * s
                dst = c_stage.rearrange("p (i h r) -> p i h r", h=H, r=R)[:, i0:i0 + 16, h, :]
                act.activation(dst, ps[:, 4 + n % 4, 0:HD].rearrange("p (i r) -> p i r", r=R),
                               ACT.Copy).then_inc(tc_ev, 1)
            act.wait_ge(in_h, 64)
            act.activation(gate[:, 1:2], gate[:, 0:1], ACT.Abs).then_inc(gexp, 1)
            act.wait_ge(gexp, 1)
            act.activation(gate[:, 2:3], gate[:, 1:2], ACT.Exp, scale=-1.0).then_inc(gexp, 1)
            act.wait_ge(tm_made, 1)
            act.wait_ge(tl_mm, 1)
            for k in range(4):
                rows = slice(32 * k, 32 * k + 24)
                act.activation(c24[rows, 0:256], ps[rows, 0, 0:256], ACT.Copy).then_inc(tl_ev, 1)
            act.wait_ge(tl_mm, 2)
            act.activation(lgs[:, 0:256], ps[:, 2, 0:256], ACT.Copy).then_inc(tl_ev, 1)
            act.wait_ge(tl_t, 1)
            for k in range(4):
                act.activation(lgo[:, k * 48:(k + 1) * 48], ps[:, 4 + k, 0:48],
                               ACT.Copy).then_inc(tl_ev2, 1)
            aw = tab_t2.rearrange("i (w j r) c -> w i j r c", w=2, j=H)[1]
            for g in range(8):
                if g >= 4:
                    act.wait_ge(tw_out[g % 4], 16 * 4)
                for j in range(H):
                    act.wait_ge(tw_mm, 4 * g + j + 1)
                    act.activation(ws[g % 4][:, j, :], ps[:, 4 + j, 0:HD], ACT.Copy
                                   ).then_inc(tw_ev, 1)
                for j in range(H):
                    act.wait_ge(tw_ev, 4 * g + j + 1)
                    act.dma_start(aw[8 * g:8 * g + 8, j], ws[g % 4][:, j, :]
                                  ).then_inc(tw_out[g % 4], 16)

            def copy_b(u, w, body, first=False):
                act.wait_ge(wt_mm[0], 4 * body + 2 * u + w + 1)
                if not first:
                    act.wait_ge(xb_mm[u], 2 * body)
                act.activation(bt[:, u, w, 0:4, :], ps[:, 0, :].rearrange(
                    "p (k c) -> p k c", k=4), ACT.Copy).then_inc(wt_ok[0], 1)

            def turned(u, body, first=False):
                act.wait_ge(q_mm[u], body + 1)
                if not first:
                    act.wait_ge(o_mm[u], 4 * body)
                act.activation(bn1[:, u, :], ps[:, 2 + u, 256:384], ACT.Copy).then_inc(bt_ok[u], 1)

            def query(u, body):
                act.wait_ge(q_mm[u], body + 1)
                act.activation(qt[:, u, :], ps[:, 2 + u, 0:256], ACT.Copy).then_inc(q_ok[u], 1)

            def magnitude(u, k, body):
                act.wait_ge(s_mm[u], 4 * body + 2 * k + 2)
                act.activation(soft[:, u, 2 * k:2 * k + 2, :], ps[:, 4 + 2 * k:6 + 2 * k, 0:H * T],
                               ACT.Abs).then_inc(s_abs[u], 1)

            def power(u, k, body):
                act.wait_ge(s_abs[u], 2 * body + k + 1)
                w = soft[:, u, 2 * k:2 * k + 2, :]
                act.activation(w, w, ACT.Exp, scale=-1.0).then_inc(s_e[u], 1)

            def logarithm(u, k, body):
                act.wait_ge(s_e[u], 2 * body + k + 1)
                w = soft[:, u, 2 * k:2 * k + 2, :]
                act.activation(w, w, ACT.Ln, bias=1.0).then_inc(s_ln[u], 1)

            def weight(u, k, body):
                e = 2 * body + k + 1
                act.wait_ge(s_min[u], e)
                w = prob[:, u, 2 * k:2 * k + 2, :]
                act.activation(w, w, ACT.Exp).then_inc(s_exp[u], 1)

            def keep_o(u, body):
                act.wait_ge(o_mm[u], 4 * body + 4)
                act.wait_ge(obd_ok[u], body + 1)
                act.activation(o_all[:, bass.ds(2 * body + u, 1), :],
                               ps[:, 2 + u, 0:H * T].unsqueeze(1), ACT.Copy).then_inc(oc_ok[u], 1)

            def turned2(u, body):
                act.wait_ge(b2t_mm[u], body + 1)
                act.activation(b2t[:, u, :], ps[:, 2 + u, 320:448], ACT.Copy).then_inc(b2t_ok[u], 1)

            def sums(c):
                return st[:, c, :].rearrange("p (t j k) -> p t j k", j=4, k=4)[:, :, :, 3]

            def k_ratio(c, n, batch):
                act.wait_ge(k_dif[c], batch * 99 + n + 1)
                act.activation(rho[:, c, :].rearrange("p (t i j) -> p t i j", i=4, j=4)[:, :, :, 1:4],
                               dif[:, c, 0:3 * CP].rearrange("p (t j) -> p t j", j=3)
                               .unsqueeze(2).broadcast_to([P, CP, 4, 3]), ACT.Exp
                               ).then_inc(k_rho[c], 1)

            def k_steps(m0, m1, nb, batch):
                for m in range(m0, m1):
                    for c in range(NCHAIN):
                        act.wait_ge(k_sum[c], batch * 99 + nb + m + 1)
                        act.activation((lcol if m % 2 == 0 else lrow)[:, c, :]
                                       .rearrange("p (t j) -> p t j", j=4), sums(c), ACT.Ln
                                       ).then_inc(k_ln[c], 1)
                    for c in range(NCHAIN):
                        k_ratio(c, nb + m, batch)

            def k_matrix(c, done):
                z = zz[:, c, :].rearrange("p (t i j) -> p t j i", i=4, j=4)
                act.activation(kc[:, c, :].rearrange("p (t j i) -> p t j i", i=4, j=4), z, ACT.Exp)
                act.activation(kr[:, c, :], zz[:, c, :], ACT.Exp).then_inc(done[c], 1)

            def k_rstd(batch):
                for u in range(2):
                    act.wait_ge(ms_ok[u], (batch + 1) * BPB)
                act.wait_ge(zeros_ok, 3)
                for c in range(NCHAIN):
                    p0 = (batch * NCHAIN + c) * CP
                    act.activation(rstd[:, c, :], ms_all[:, p0:p0 + CP], ACT.Ln, scale=1.0 / D,
                                   bias=eps_c[:, 0:1]).then_inc(k_ia[c], 1)
                for c in range(NCHAIN):
                    act.wait_ge(k_ia[c], batch * 4 + 1)
                    act.activation(rstd[:, c, :], rstd[:, c, :], ACT.Exp, scale=-0.5
                                   ).then_inc(k_ia[c], 1)

            def k_start(m, batch):
                if m == 0:
                    k_rstd(batch)
                elif m == 1:
                    for c in range(NCHAIN):
                        act.wait_ge(k_i[c], batch * 12 + 5)
                        act.activation(st[:, c, :], zz[:, c, :], ACT.Exp).then_inc(k_ia[c], 1)
                elif m == 2:
                    for c in range(NCHAIN):
                        act.wait_ge(k_sum[c], batch * 99 + 1)
                        act.activation(lrow[:, c, :], small[:, c, :], ACT.Ln).then_inc(k_ln[c], 1)
                    for c in range(NCHAIN):
                        act.wait_ge(k_i[c], batch * 12 + 7)
                        k_matrix(c, k_m)
                else:
                    for c in range(NCHAIN):
                        k_ratio(c, 0, batch)

            def k_begin(m0, m1, batch):
                for m in range(m0, m1):
                    if m < START:
                        k_start(m, batch)
                    else:
                        k_steps(m - START, m - START + 1, 1, batch)

            def k_middle(batch):
                for c in range(NCHAIN):
                    act.wait_ge(k_sum[c], batch * 99 + HALF)
                    act.activation(lcol[:, c, :].rearrange("p (t j) -> p t j", j=4),
                                   sums(c), ACT.Ln
                                   ).then_inc(k_ln[c], 1)
                for c in range(NCHAIN):
                    act.wait_ge(k_dif[c], batch * 99 + HALF)
                    k_matrix(c, k_rho)
                for c in range(NCHAIN):
                    act.wait_ge(k_i[c], batch * 12 + 9)
                    act.activation(hp[:, c, :, :], hp[:, c, :, :], ACT.Exp).then_inc(k_ia[c], 1)
                for c in range(NCHAIN):
                    act.wait_ge(k_sum[c], batch * 99 + HALF + 1)
                    act.activation(lrow[:, c, :], small[:, c, :], ACT.Ln).then_inc(k_ln[c], 1)
                    k_ratio(c, HALF, batch)

            def begin(base, batch):
                return lambda m0, m1: k_begin(base + m0, base + m1, batch)

            def steps_at(nb, batch):
                return lambda m0, m1: k_steps(m0, m1, nb, batch)

            def slot(f, b, first=False, k=lambda m0, m1: None):
                if b:
                    magnitude(b[0], 0, b[1])
                    magnitude(b[0], 1, b[1])
                k(0, 1)
                if b:
                    power(b[0], 0, b[1])
                if f:
                    copy_b(f[0], 0, f[1], first)
                k(1, 2)
                if b:
                    logarithm(b[0], 0, b[1])
                    power(b[0], 1, b[1])
                k(2, 3)
                if b:
                    logarithm(b[0], 1, b[1])
                if f:
                    copy_b(f[0], 1, f[1], first)
                k(3, 4)
                if b:
                    weight(b[0], 0, b[1])
                k(4, 5)
                if b:
                    weight(b[0], 1, b[1])
                k(5, 8)
                if b:
                    keep_o(*b)
                k(8, 10)
                if f:
                    query(*f)
                    turned(*f, first)
                k(10, 11)
                if b:
                    turned2(*b)
                k(11, 12)

            def body_a(body, steps=None, per=PER_BODY, first=False, last=False):
                def k(n):
                    if steps is None:
                        return lambda m0, m1: None
                    return lambda m0, m1: steps(per * (n + m0) // 24, per * (n + m1) // 24)
                slot((1, body), (0, body), first, k(0))
                slot(None if last else (0, body + 1), (1, body), False, k(12))

            def turned_u(u, j, body, first=False):
                b, n = j % 2, 4 * u + j
                act.wait_ge(ut_mm[b], 4 * body + n // 2 + 1)
                if not first:
                    act.wait_ge(f_mm[j], 4 * body + 2 * u - 2)
                act.activation(ut[:, u, j, :], ps[:, b, :], ACT.Copy).then_inc(ut_ok[b], 1)

            def body_c(body, steps=None, per=PER_BODY, first=False, last=False):
                if steps:
                    steps(0, per // 16)
                for n in range(8):
                    if n < 4:
                        turned_u(1, n, body, first)
                    elif not last:
                        turned_u(0, n - 4, body + 1)
                    if steps:
                        end = per // 2 if last else per
                        steps(min(end, per * (2 * n + 1) // 16),
                              min(end, per * (2 * n + 3) // 16))

            act.wait_ge(tc_out, 16)
            for k in range(4):
                act.wait_ge(tw_out[k], 16 * 8)
            slot((0, 0), None, first=True)
            body_a(0, first=True)
            with act.Fori(1, BPB) as i:
                body_a(i)
            body_a(BPB, begin(0, 0), SETUP_BODY)
            body_a(BPB + 1, begin(SETUP_BODY, 0), SETUP_BODY)
            k_middle(0)
            for i in range(2):
                body_a(BPB + 2 + i, steps_at(HALF + 1 + i * PER_BODY, 0), last=(i == 1))
            for j in range(4):
                k_start(j, 1)
                turned_u(0, j, 0, first=True)
            body_c(0, begin(START, 1), first=True)
            body_c(1, begin(START + PER_BODY, 1))
            k_middle(1)
            body_c(2, steps_at(HALF + 1, 1), EARLY)
            body_c(3, steps_at(HALF + 1 + EARLY, 1), 2 * (2 * PER_BODY - EARLY), last=True)
            for j in range(4):
                turned_u(0, j, BPB)
            with act.Fori(0, BPB - 1) as i:
                body_c(BPB + i)
            body_c(NBODY - 1, last=True)

        @block.vector
        def _(dve):
            nc.vector.memset(rho[:, :, :], 0.0).then_inc(zeros_ok, 1)
            nc.vector.memset(eps_c[:, :], EPS).then_inc(zeros_ok, 1)
            nc.vector.memset(bal[:, :], 0.0).then_inc(zeros_ok, 1)
            n_link = [0]

            def link(ins):
                n_link[0] += 1
                ins.then_inc(link_ok, 1)
                dve.wait_ge(link_ok, n_link[0])

            dve.wait_ge(zeros_ok, 3)
            dve.wait_ge(in_bv, 16)
            link(dve.scalar_tensor_tensor(out=bst[:, :, :], in0=bvt[:, :, :], scalar=-1.0,
                                          in1=bvt[:, :, :], op0=ALU.mult, op1=ALU.max))
            link(dve.tensor_reduce(bal[:, 0:3], bst[:, :, :], AX, ALU.add))
            link(dve.tensor_scalar(bal[:, 0:3], bal[:, 0:3], 1.0 / HD, None, ALU.mult))
            link(dve.tensor_scalar(bst[:, :, :], bvt[:, :, :], 0.0, 2.0, ALU.is_ge, ALU.mult))
            link(dve.tensor_tensor(bst[:, :, :], bst[:, :, :], bc(bal[:, 0:3], 2, [H, 3, HD]),
                                   ALU.mult))
            link(dve.tensor_tensor(bst[:, :, :], bst[:, :, :], bc(bal[:, 0:3], 2, [H, 3, HD]),
                                   ALU.subtract))
            link(dve.tensor_tensor(bst[:, :, :], bst[:, :, :], bvt[:, :, :], ALU.subtract))
            link(dve.tensor_tensor(bst[:, :, :], bst[:, :, :], bvt[:, :, :], ALU.add))
            link(dve.tensor_tensor(bst[:, 0, :], bst[:, 0, :], bst[:, 1, :], ALU.mult))
            dve.tensor_copy(bst[:, 1, :], bst[:, 2, :]).then_inc(bind, 1)
            dve.wait_ge(bind_t, 1)
            turned = ps[:, 0, 0:16].rearrange("p (w k h) -> p w k h", w=2, k=2)
            dve.tensor_scalar(vqc[:, 0, :, :], turned[:, 0, :, :], SCALE, None, ALU.mult)
            link(dve.tensor_copy(vqc[:, 1, :, :], turned[:, 1, :, :]))
            dve.engine_nop().then_inc(bind_c, 1)
            dve.wait_ge(in_a1, 32)
            for w, dst in enumerate((a1qk, a1v)):
                dve.tensor_tensor(dst.rearrange("p (h k c) -> p h k c", h=H, k=2),
                                  a1c.rearrange("p (h k c) -> p h k c", h=H, k=2),
                                  bc(vqc[:, w, :, :].rearrange("p k h -> p h k"), 3, [P, H, 2, P]),
                                  ALU.mult).then_inc(a1_scaled, 1)
            dve.wait_ge(vrow, 1)
            for k in range(2):
                dve.tensor_tensor(a1t[:, 512 * k:512 * k + 512], a1t[:, 512 * k:512 * k + 512],
                                  ps[:, 1 + k, :], ALU.mult).then_inc(avt_made, 1)
            dve.wait_ge(tm_mm, 1)
            dve.wait_ge(in_con, 64)
            link(dve.tensor_tensor(mst.rearrange("p h (i r) -> p h i r", r=R),
                                   ps[:, 3, :].rearrange("p (h i r) -> p h i r", h=H, r=R),
                                   con[:, C_M8:C_M8 + 8].unsqueeze(1).unsqueeze(3)
                                   .broadcast_to([P, H, 8, R]), ALU.mult))
            dve.tensor_reduce(mout.rearrange("p (h r) -> p h r", h=H),
                              mst.rearrange("p h (i r) -> p h r i", r=R), AX, ALU.add
                              ).then_inc(tm_made, 1)
            idx_m, idx_c, idx_l = (idx[:, :, k] for k in range(3))
            link(dve.scalar_tensor_tensor(out=idx_m, in0=id1r[:, :], scalar=float(R),
                                          in1=rowno[:, :], op0=ALU.mult, op1=ALU.add))
            dve.scalar_tensor_tensor(out=idx_c, in0=idx_m, scalar=float(NA2),
                                     in1=id2r[:, :], op0=ALU.mult, op1=ALU.add
                                     ).then_inc(idx_ok, 1)
            dve.scalar_tensor_tensor(out=idx_l, in0=id2r[:, :], scalar=float(R),
                                     in1=rowno[:, :], op0=ALU.mult, op1=ALU.add
                                     ).then_inc(idx_ok, 1)
            dve.wait_ge(gexp, 2)
            link(dve.tensor_scalar(gate[:, 3:4], gate[:, 2:3], 1.0, None, ALU.add))
            link(dve.reciprocal(gate[:, 4:5], gate[:, 3:4]))
            link(dve.tensor_scalar(gate[:, 1:2], gate[:, 0:1], 0.0, None, ALU.is_ge))
            link(dve.tensor_tensor(gate[:, 5:6], gate[:, 1:2], gate[:, 2:3], ALU.mult))
            link(dve.tensor_tensor(gate[:, 3:4], gate[:, 1:2], gate[:, 2:3], ALU.add))
            link(dve.tensor_tensor(gate[:, 3:4], gate[:, 3:4], gate[:, 5:6], ALU.subtract))
            link(dve.tensor_tensor(gate[:, 3:4], gate[:, 3:4], gate[:, 4:5], ALU.mult))
            link(dve.tensor_tensor(gate[:, 5:6], gate[:, 5:6], gate[:, 1:2], ALU.subtract))
            link(dve.tensor_scalar(gate[:, 5:6], gate[:, 5:6], 1.0, None, ALU.add))
            link(dve.tensor_tensor(gate[:, 5:6], gate[:, 5:6], gate[:, 4:5], ALU.mult))
            link(dve.tensor_scalar(eyeg[:, :], con[:, C_EYE:C_EYE + 16], gate[:, 5:6], None,
                                   ALU.mult))

            mq = con[:, C_MQ:C_MQ + 2].unsqueeze(1).unsqueeze(3).broadcast_to([P, 4, 2, R])

            mr = con[:, C_MR:C_MR + 2].unsqueeze(2).broadcast_to([P, 2, T])

            def copy_b(u, w, body, first=False):
                dve.wait_ge(wt_mm[1], 4 * body + 2 * u + w + 1)
                if not first:
                    dve.wait_ge(xb_mm[u], 2 * body)
                dve.tensor_copy(bt[:, u, w, 4:8, :], ps[:, 1, :].rearrange(
                    "p (k c) -> p k c", k=4)).then_inc(wt_ok[1], 1)

            def split(u, body, first=False):
                for w, dst in enumerate((btc, xb2)):
                    dve.wait_ge(xb_mm[u], 2 * body + 2)
                    if not first:
                        dve.wait_ge(c_mm[u], body)
                    dve.tensor_tensor(dst[:, u, 0:P].rearrange("p (q t) -> p q t", q=2),
                                      ps[:, 2 + u, w * P:(w + 1) * P]
                                      .rearrange("p (q t) -> p q t", q=2), mr, ALU.mult
                                      ).then_inc(bn_ok[u], 1)
                dve.wait_ge(bn_ok[u], 2 * body + 1)
                dve.tensor_tensor(btc[:, u, P:P + T], btc[:, u, 0:T], btc[:, u, T:P], ALU.add
                                  ).then_inc(cp_ok[u], 1)

            def minus(u, k, body):
                dve.wait_ge(s_ln[u], 2 * body + k + 1)
                dve.scalar_tensor_tensor(out=prob[:, u, 2 * k:2 * k + 2, :],
                                         in0=ps[:, 4 + 2 * k:6 + 2 * k, 0:H * T], scalar=0.0,
                                         in1=soft[:, u, 2 * k:2 * k + 2, :], op0=ALU.min,
                                         op1=ALU.subtract).then_inc(s_min[u], 1)

            def mask(u, body):
                dve.wait_ge(s_exp[u], 2 * body + 2)
                v = prob[:, u, 2:4, :].rearrange("p j (h t) -> p (j h) t", h=H)
                dve.tensor_tensor(v, v, bc(con[:, C_CAU:C_CAU + T], 1, [P, 2 * H, T]), ALU.mult
                                  ).then_inc(p_ok2[u], 1)

            def diag_o(u, body):
                dve.wait_ge(o_mm[u], 4 * body + 4)
                dve.tensor_tensor(obd[:, u, :].rearrange("p (h q t) -> p h q t", h=H, q=2),
                                  bc(ps[:, 2 + u, 0:256].rearrange("p (h t) -> p h t", h=H), 2,
                                     [P, H, 2, T]),
                                  con[:, C_MR:C_MR + 2].unsqueeze(1).unsqueeze(3)
                                  .broadcast_to([P, H, 2, T]), ALU.mult).then_inc(obd_ok[u], 1)

            def u2(u, body):
                dve.wait_ge(c_mm[u], body + 1)
                v = ps[:, 2 + u, 256:320].rearrange("p (j r) -> p j r", r=R)
                dve.tensor_tensor(bn2[:, u, :].rearrange("p (j q r) -> p j q r", q=2, r=R),
                                  bc(v, 2, [P, 4, 2, R]), mq, ALU.mult).then_inc(b2_ok[u], 1)
                dve.tensor_copy(u2_all[:, bass.ds((2 * body + u) * 4, 4), :], v
                                ).then_inc(u2_ok[u], 1)

            def logits(u, body, first=False):
                dve.wait_ge(lg_mm[u], body + 1)
                v = ps[:, 2 + u, 0:4 * NLG].rearrange("p (j c) -> p j c", c=NLG)
                dve.tensor_copy(lg_all[:, bass.ds((2 * body + u) * 4, 4), :], v[:, :, 0:24])
                dve.wait_ge(u2_ok[u], body + 1)
                if not first:
                    dve.wait_ge(ms_ok[u], body)
                g = gy[:, u, :].rearrange("p (j r) -> p j r", r=R)
                dve.tensor_tensor(g, v[:, :, 24:NLG], u2_all[:, bass.ds((2 * body + u) * 4, 4), :],
                                  ALU.mult).then_inc(gy_ok[u], 1)
                dve.wait_ge(gy_ok[u], body + 1)
                dve.tensor_reduce(ms_all[:, bass.ds((2 * body + u) * 4, 4)], g, AX, ALU.add
                                  ).then_inc(ms_ok[u], 1)

            def k_diff(c, n, batch, row):
                dve.wait_ge(k_ln[c], batch * 99 + n + 1)
                src = (lrow if row else lcol)[:, c, :].rearrange("p (t j) -> p t j", j=4)
                dve.tensor_tensor(dif[:, c, 0:3 * CP].rearrange("p (t j) -> p t j", j=3),
                                  src[:, :, 1:4], src[:, :, 0:3], ALU.subtract
                                  ).then_inc(k_dif[c], 1)

            def k_scan(c, n, batch, row):
                dve.wait_ge(k_rho[c], batch * 99 + n)
                dve.tensor_tensor_scan(st[:, c, :], rho[:, c, :], (kr if row else kc)[:, c, :],
                                       0.0, ALU.mult, ALU.add).then_inc(k_sum[c], 1)

            def k_steps(m0, m1, nb, batch):
                for m in range(m0, m1):
                    for c in range(NCHAIN):
                        k_scan(c, nb + m, batch, m % 2 == 1)
                    for c in range(NCHAIN):
                        k_diff(c, nb + m, batch, m % 2 == 1)

            def z4(c):
                return zz[:, c, :].rearrange("p (t i j) -> p t i j", i=4, j=4)

            def s4(c):
                return small[:, c, :].rearrange("p (t i) -> p t i", i=4)

            def d4(c):
                return dif[:, c, :].rearrange("p (t i) -> p t i", i=4)

            def t4(c):
                return st[:, c, :].rearrange("p (t i j) -> p t i j", i=4, j=4)

            def s2(c):
                return hsum[:, c, :].rearrange("p (t w) -> p t w", w=2)

            def h4(c):
                return hp[:, c, :, :].rearrange("p t (w j) -> p t w j", w=2)

            def zh(c):
                return z24[:, c, :, 16:24].rearrange("p t (w j) -> p t w j", w=2)

            def k_start(m, batch):
                e = batch * 12
                if m == 0:
                    for u in range(2):
                        dve.wait_ge(ms_ok[u], (batch + 1) * BPB)
                    for c in range(NCHAIN):
                        p0 = (batch * NCHAIN + c) * CP
                        dve.wait_ge(k_ia[c], batch * 4 + 2)
                        dve.tensor_tensor(z24[:, c, :, :], lg_all[:, p0:p0 + CP, :],
                                          bc(rstd[:, c, :], 2, [P, CP, 24]), ALU.mult
                                          ).then_inc(k_i[c], 1)
                    for c in range(NCHAIN):
                        dve.wait_ge(k_i[c], e + 1)
                        dve.tensor_tensor(z24[:, c, :, :], z24[:, c, :, :],
                                          bc(base24[:, :], 1, [P, CP, 24]), ALU.add
                                          ).then_inc(k_i[c], 1)
                    for c in range(NCHAIN):
                        dve.wait_ge(k_i[c], e + 2)
                        dve.tensor_scalar(zz[:, c, :].rearrange("p (t i) -> p t i", i=16),
                                          z24[:, c, :, 0:16], 1.0 / TAU, None, ALU.mult
                                          ).then_inc(k_i[c], 1)
                elif m == 1:
                    for c in range(NCHAIN):
                        dve.wait_ge(k_i[c], e + 3)
                        dve.tensor_reduce(s4(c), z4(c), AX, ALU.max).then_inc(k_i[c], 1)
                    for c in range(NCHAIN):
                        dve.wait_ge(k_i[c], e + 4)
                        dve.tensor_tensor(z4(c), z4(c), bc(s4(c), 3, [P, CP, 4, 4]), ALU.subtract
                                          ).then_inc(k_i[c], 1)
                elif m == 2:
                    for c in range(NCHAIN):
                        dve.wait_ge(k_i[c], e + 5)
                        dve.tensor_reduce(d4(c), z4(c).rearrange("p t i j -> p t j i"), AX,
                                          ALU.max).then_inc(k_i[c], 1)
                    for c in range(NCHAIN):
                        dve.wait_ge(k_ia[c], batch * 4 + 3)
                        dve.tensor_reduce(s4(c), t4(c), AX, ALU.add).then_inc(k_sum[c], 1)
                    for c in range(NCHAIN):
                        dve.wait_ge(k_i[c], e + 6)
                        dve.tensor_tensor(z4(c), z4(c), bc(d4(c), 2, [P, CP, 4, 4]), ALU.subtract
                                          ).then_inc(k_i[c], 1)
                else:
                    for c in range(NCHAIN):
                        dve.wait_ge(k_i[c], e + 7)
                        k_diff(c, 0, batch, True)
                    for c in range(NCHAIN):
                        dve.wait_ge(k_m[c], batch + 1)

            def k_begin(m0, m1, batch):
                for m in range(m0, m1):
                    if m < START:
                        k_start(m, batch)
                    else:
                        k_steps(m - START, m - START + 1, 1, batch)

            def k_middle(batch):
                e = batch * 12
                for c in range(NCHAIN):
                    k_scan(c, HALF - 1, batch, False)
                for c in range(NCHAIN):
                    l4 = lrow[:, c, :].rearrange("p (t i) -> p t i", i=4)
                    dve.tensor_tensor(s4(c), l4[:, :, 3:4].broadcast_to([P, CP, 4]), l4,
                                      ALU.subtract).then_inc(k_b[c], 1)
                for c in range(NCHAIN):
                    dve.wait_ge(k_b[c], 2 * batch + 1)
                    dve.tensor_tensor(z4(c), z4(c), bc(s4(c), 3, [P, CP, 4, 4]), ALU.add
                                      ).then_inc(k_b[c], 1)
                for c in range(NCHAIN):
                    dve.wait_ge(k_b[c], 2 * batch + 2)
                    dve.wait_ge(k_ln[c], batch * 99 + HALF)
                    dve.tensor_tensor(z4(c), z4(c),
                                      bc(lcol[:, c, :].rearrange("p (t j) -> p t j", j=4), 2,
                                         [P, CP, 4, 4]), ALU.subtract).then_inc(k_dif[c], 1)
                for c in range(NCHAIN):
                    dve.tensor_reduce(s2(c), zh(c), AX, ALU.max).then_inc(k_i[c], 1)
                for c in range(NCHAIN):
                    dve.wait_ge(k_i[c], e + 8)
                    dve.tensor_tensor(h4(c), zh(c), bc(s2(c), 3, [P, CP, 2, 4]), ALU.subtract
                                      ).then_inc(k_i[c], 1)
                for c in range(NCHAIN):
                    dve.wait_ge(k_rho[c], batch * 99 + HALF)
                    dve.tensor_reduce(s4(c), kr[:, c, :].rearrange("p (t i j) -> p t i j", i=4,
                                                                   j=4),
                                      AX, ALU.add).then_inc(k_sum[c], 1)
                for c in range(NCHAIN):
                    k_diff(c, HALF, batch, True)
                for c in range(NCHAIN):
                    dve.wait_ge(k_ia[c], batch * 4 + 4)
                    dve.tensor_reduce(s2(c), h4(c), AX, ALU.add).then_inc(k_i[c], 1)
                for c in range(NCHAIN):
                    dve.wait_ge(k_i[c], e + 10)
                    dve.reciprocal(s2(c), s2(c)).then_inc(k_i[c], 1)
                for c in range(NCHAIN):
                    dve.wait_ge(k_i[c], e + 11)
                    dve.tensor_tensor(h4(c), h4(c), bc(s2(c), 3, [P, CP, 2, 4]), ALU.mult
                                      ).then_inc(k_i[c], 1)

            def k_final(batch):
                e = batch * 5
                for c in range(NCHAIN):
                    dve.wait_ge(k_rho[c], batch * 99 + 99)
                    dve.reciprocal(s4(c), t4(c)[:, :, :, 3]).then_inc(k_f[c], 1)
                for c in range(NCHAIN):
                    k4 = kr[:, c, :].rearrange("p (t i j) -> p t i j", i=4, j=4)
                    dve.wait_ge(k_f[c], e + 1)
                    dve.tensor_tensor(t4(c), k4, bc(s4(c), 3, [P, CP, 4, 4]), ALU.mult
                                      ).then_inc(k_f[c], 1)
                for c in range(NCHAIN):
                    dve.wait_ge(k_f[c], e + 2)
                    dve.tensor_reduce(d4(c), t4(c).rearrange("p t i j -> p t j i"), AX, ALU.add
                                      ).then_inc(k_f[c], 1)
                for c in range(NCHAIN):
                    dve.wait_ge(k_f[c], e + 3)
                    dve.reciprocal(s4(c), d4(c)).then_inc(k_f[c], 1)
                for c in range(NCHAIN):
                    dve.wait_ge(k_f[c], e + 4)
                    dve.tensor_tensor(t4(c), t4(c), bc(s4(c), 2, [P, CP, 4, 4]), ALU.mult
                                      ).then_inc(k_f[c], 1)
                for c in range(NCHAIN):
                    p0 = (batch * NCHAIN + c) * CP
                    dd = d_all[:, p0:p0 + CP, :].rearrange("p t (n w j) -> p t n w j", n=4, w=2)
                    dve.wait_ge(k_i[c], (batch + 1) * 12)
                    dve.tensor_tensor(dd[:, :, :, 1, :],
                                      bc(hp[:, c, :, 4:8], 3, [P, CP, 4, 4]),
                                      bc(hp[:, c, :, 0:4], 2, [P, CP, 4, 4]), ALU.mult
                                      ).then_inc(d_ok[c], 1)
                    dve.wait_ge(k_f[c], e + 5)
                    dve.scalar_tensor_tensor(
                        out=dd[:, :, :, 0, :].rearrange("p t n j -> p t n j"),
                        in0=t4(c), scalar=gate[:, 3:4],
                        in1=bc(eyeg[:, :].rearrange("p (i j) -> p i j", i=4), 1, [P, CP, 4, 4]),
                        op0=ALU.mult, op1=ALU.add).then_inc(d_ok[c], 1)
                for c in range(NCHAIN):
                    dve.wait_ge(d_ok[c], 2 * batch + 2)

            def begin(base, batch):
                return lambda m0, m1: k_begin(base + m0, base + m1, batch)

            def steps_at(nb, batch):
                return lambda m0, m1: k_steps(m0, m1, nb, batch)

            def slot(f, b, first=False, k=lambda m0, m1: None):
                k(0, 1)
                if f:
                    copy_b(f[0], 0, f[1], first)
                k(1, 2)
                if b:
                    minus(b[0], 0, b[1])
                k(2, 3)
                if f:
                    copy_b(f[0], 1, f[1], first)
                k(3, 4)
                if b:
                    minus(b[0], 1, b[1])
                k(4, 6)
                if b:
                    mask(*b)
                k(6, 7)
                if b:
                    diag_o(*b)
                k(7, 9)
                if f:
                    split(*f, first)
                k(9, 10)
                if b:
                    u2(*b)
                k(10, 12)
                if b:
                    logits(*b, first)

            def body_a(body, steps=None, per=PER_BODY, first=False, last=False):
                def k(n):
                    if steps is None:
                        return lambda m0, m1: None
                    return lambda m0, m1: steps(per * (n + m0) // 24, per * (n + m1) // 24)
                slot((1, body), (0, body), first, k(0))
                slot(None if last else (0, body + 1), (1, body), False, k(12))

            def add(u, half, j, body):
                dve.wait_ge(f_mm[j], 4 * body + 2 * u + half + 1)
                if half == 0:
                    dve.wait_ge(x_in[2 * u + j // 2], 16 * (NBODY + body + 1))
                v = xt[:, u, j, half * 512:(half + 1) * 512]
                dve.tensor_tensor(v, v, ps[:, 4 + j, :], ALU.add).then_inc(f_ok[j], 1)

            def body_c(body, steps=None, per=PER_BODY, first=False, last=False):
                for n in range(16):
                    add(n // 8, n // 4 % 2, n % 4, body)
                    if steps and not (last and n > 7):
                        steps(per * n // 16, per * (n + 1) // 16)
                    if last and n == 7:
                        k_final(1)

            dve.wait_ge(tc_out, 16)
            slot((0, 0), None, first=True)
            body_a(0, first=True)
            with dve.Fori(1, BPB) as i:
                body_a(i)
            body_a(BPB, begin(0, 0), SETUP_BODY)
            body_a(BPB + 1, begin(SETUP_BODY, 0), SETUP_BODY)
            k_middle(0)
            for i in range(2):
                body_a(BPB + 2 + i, steps_at(HALF + 1 + i * PER_BODY, 0), last=(i == 1))
            k_final(0)
            k_begin(0, START, 1)
            body_c(0, begin(START, 1), first=True)
            body_c(1, begin(START + PER_BODY, 1))
            k_middle(1)
            body_c(2, steps_at(HALF + 1, 1), EARLY)
            body_c(3, steps_at(HALF + 1 + EARLY, 1), 2 * (2 * PER_BODY - EARLY), last=True)
            with dve.Fori(0, BPB) as i:
                body_c(BPB + i)

        @block.gpsimd
        def _(pool):
            def fetch_b(u):
                for w, src in enumerate(("b1r", "b2r")):
                    pool.indirect_dma_start(
                        brow[:, u, w, :], None, io[src],
                        bass.IndirectOffsetOnAxis(idx_now[:, u, 2 * w:2 * w + 1], 0)
                        ).then_inc(b_in[u], 16)

            def fetch_rows(u):
                for k, (dst, tab) in enumerate(((m_g, tab_m), (c_g, tab_c), (lg_g, tab_lg))):
                    pool.indirect_dma_start(dst[:, u, :], None, tab,
                                            bass.IndirectOffsetOnAxis(idx_now[:, u, k:k + 1], 0)
                                            ).then_inc(rows_in[u], 16)

            pool.wait_ge(idx_ok, 2)
            for u in range(2):
                pool.tensor_copy(idx_now[:, u, :], idx[:, u, :]).then_inc(nx_ok[u], 1)
                pool.wait_ge(nx_ok[u], 1)
                fetch_b(u)
            pool.wait_ge(tab_out, 32)
            pool.wait_ge(tc_out, 16)
            pool.wait_ge(tg_out, 144)
            fetch_rows(0)
            fetch_rows(1)
            m8 = con[:, C_M8:C_M8 + 8]
            m4 = con[:, C_M4:C_M4 + 4]

            def spread_m(u, body, first=False):
                pool.wait_ge(rows_in[u], 48 * (body + 1))
                if not first:
                    pool.wait_ge(q_mm[u], body)
                pool.tensor_tensor(mbd[:, u, :, :].rearrange("p h (k r) -> p h k r", r=R),
                                   bc(m_g[:, u, :].rearrange("p (h r) -> p h r", r=R), 2,
                                      [P, H, 8, R]),
                                   m8.unsqueeze(1).unsqueeze(3).broadcast_to([P, H, 8, R]),
                                   ALU.mult).then_inc(bd_ok[u], 1)

            def spread_cl(u, body, first=False):
                if not first:
                    pool.wait_ge(c_mm[u], body)
                pool.tensor_tensor(cbd[:, u, :, :].rearrange("p h (j r) -> p h j r", r=R),
                                   bc(c_g[:, u, :].rearrange("p (h r) -> p h r", r=R), 2,
                                      [P, H, 4, R]),
                                   m4.unsqueeze(1).unsqueeze(3).broadcast_to([P, H, 4, R]),
                                   ALU.mult).then_inc(bd_ok[u], 1)
                if not first:
                    pool.wait_ge(lg_mm[u], body)
                pool.tensor_tensor(lbd[:, u, :].rearrange("p (j c) -> p j c", c=NLG),
                                   bc(lg_g[:, u, :], 1, [P, 4, NLG]),
                                   bc(m4, 2, [P, 4, NLG]), ALU.mult).then_inc(bd_ok[u], 1)

            def mask(u, body):
                pool.wait_ge(s_exp[u], 2 * body + 1)
                v = prob[:, u, 0:2, :].rearrange("p j (h t) -> p (j h) t", h=H)
                pool.tensor_tensor(v, v, bc(con[:, C_CAU:C_CAU + T], 1, [P, 2 * H, T]), ALU.mult
                                   ).then_inc(p_ok[u], 1)

            def next_rows(u, body):
                pool.wait_ge(b_in[u], 32 * (body + 1))
                for k in range(2):
                    pool.wait_ge(wt_mm[k], 4 * body + 2 * u + 2)
                pool.tensor_copy(idx_now[:, u, :], idx[:, bass.ds(2 * body + 2 + u, 1), :]
                                 .rearrange("p g k -> p (g k)")).then_inc(nx_ok[u], 1)
                pool.wait_ge(nx_ok[u], body + 2)
                pool.wait_ge(bd_ok[u], 3 * (body + 1))

            def slot(f, b, first=False, fetch=True):
                if f:
                    spread_m(*f, first)
                    spread_cl(*f, first)
                    if fetch:
                        next_rows(*f)
                if b:
                    mask(*b)
                if f and fetch:
                    fetch_b(f[0])
                    fetch_rows(f[0])

            def body_a(body, first=False, last=False, next_last=False):
                slot((1, body), (0, body), first, fetch=not last)
                slot(None if last else (0, body + 1), (1, body), fetch=not next_last)

            slot((0, 0), None, first=True)
            body_a(0, first=True)
            with pool.Fori(1, NBODY - 2) as body:
                body_a(body)
            body_a(NBODY - 2, next_last=True)
            body_a(NBODY - 1, last=True)

            def attn_rows(u, body, first=False):
                g = bass.ds(2 * body + u, 1)
                if not first:
                    pool.wait_ge(f_mm[3], 4 * body + 2 * u - 2)
                    pool.wait_ge(av_in[u], 16 * body)
                pool.tensor_copy(idx_av[:, u:u + 1], idx[:, g, 0]).then_inc(ix_ok[u], 1)
                pool.wait_ge(ix_ok[u], body + 1)
                pool.tensor_tensor(obd[:, u, :].rearrange("p (h q t) -> p h q t", h=H, q=2),
                                   bc(o_all[:, g, :].rearrange("p g (h t) -> p (g h) t", h=H), 2,
                                      [P, H, 2, T]),
                                   con[:, C_MR:C_MR + 2].unsqueeze(1).unsqueeze(3)
                                   .broadcast_to([P, H, 2, T]), ALU.mult).then_inc(ob_ok[u], 1)
                pool.indirect_dma_start(av[:, u, :], None, tab_av,
                                        bass.IndirectOffsetOnAxis(idx_av[:, u:u + 1], 0)
                                        ).then_inc(av_in[u], 16)

            def spread_u2(u, j, body, first=False):
                b, n = j % 2, 4 * u + j
                pair = bass.ds((2 * body + u) * 4 + j, 1)
                if not (first and n < 2):
                    pool.wait_ge(ut_mm[b], 4 * body + n // 2)
                pool.tensor_tensor(ubuf[:, b, :].rearrange("p (k r) -> p k r", r=R),
                                   bc(d_all[:, pair, :].rearrange("p g k -> p (g k)"), 2,
                                      [P, 32, R]),
                                   u2_all[:, pair, :].broadcast_to([P, 32, R]), ALU.mult
                                   ).then_inc(u_ok[b], 1)

            def rows_and_u(u, body, first=False):
                for j in range(4):
                    spread_u2(u, j, body, first)
                attn_rows(u, body, first)

            def body_c(body, first=False, last=False):
                rows_and_u(1, body, first)
                if not last:
                    rows_and_u(0, body + 1)

            for u in range(2):
                pool.wait_ge(c_mm[u], NBODY)
                pool.wait_ge(oc_ok[u], NBODY)
                pool.wait_ge(u2_ok[u], NBODY)
                for k in range(2):
                    pool.wait_ge(tw_out[2 * u + k], 16 * 8)
            for batch in range(NBATCH):
                b0, first = batch * BPB, batch == 0
                attn_rows(0, b0, first)
                pool.wait_ge(d_ok[0], 2 * (batch + 1))
                for j in range(4):
                    spread_u2(0, j, b0, first)
                body_c(b0, first)
                pool.wait_ge(d_ok[1], 2 * (batch + 1))
                with pool.Fori(b0 + 1, b0 + BPB - 1) as body:
                    body_c(body)
                body_c(b0 + BPB - 1, last=True)


def constants():
    import numpy as np
    p = np.arange(P)
    con = np.zeros((P, NCON), np.float32)
    con[:, C_ID:C_ID + P] = np.eye(P)
    c = np.arange(4 * R)
    con[:, C_SEL:C_SEL + 4 * R] = (p[:, None] // (2 * R) == c // R) & (p[:, None] % R == c % R)
    con[:, C_MQ:C_MQ + 2] = (p[:, None] // T) == np.arange(2)
    con[:, C_MR:C_MR + 2] = (p[:, None] // R % 2) == np.arange(2)
    con[:, C_M8:C_M8 + 8] = (p[:, None] // R) == np.arange(8)
    con[:, C_M4:C_M4 + 4] = (p[:, None] // (2 * R)) == np.arange(4)
    con[:, C_CAU:C_CAU + T] = (p[:, None] % T) <= np.arange(T)
    con[:, C_EYE:C_EYE + 16] = np.eye(4).reshape(-1)
    rowno = np.broadcast_to((p % R).astype(np.int32)[:, None], (P, NGRP))
    return con, np.ascontiguousarray(rowno)


def kernel(**inputs):
    import numpy as np
    import concourse.bacc as bacc
    from concourse.bass_utils import run_bass_kernel_spmd

    v = {k: np.asarray(a) for k, a in inputs.items()}
    con, rowno = constants()
    a1, b1 = v["L0_cond_A"], v["L0_cond_B"]
    a2, b2 = v["L0_cond2_A"], v["L0_cond2_B"]
    i1, i2 = v["itok_B_3_7"], v["itok_B_4_50"]

    def rows(i):
        return np.repeat(i.reshape(NGRP, 8).T, R, axis=0)

    def by_channel(w):
        return w.reshape(w.shape[0], R, NCH, P).transpose(0, 3, 2, 1)

    arrays = {
        "x": v["x"].reshape(NPAIR, 2, T, NCH, P).transpose(0, 4, 3, 1, 2).reshape(NPAIR, P, NCH * P),
        "xrow": v["x"].reshape(NPAIR, P, D), "ids2": i2,
        "id1r": rows(i1), "id2r": rows(i2), "rowno": rowno, "con": con,
        "a1c": a1.reshape(NA1, NCH, P, R).transpose(2, 1, 0, 3).reshape(P, D),
        "a1t": a1.transpose(0, 2, 1).reshape(NA1 * R, D),
        "b1r": b1.reshape(NA1 * R, D), "b2r": b2.reshape(NA2 * R, D),
        "b2g": by_channel(b2).reshape(NA2, P, NCH * R),
        "a2c": a2.reshape(NA2, NCH, P, R).transpose(2, 1, 0, 3).reshape(P, NCH * NA2 * R),
        "a2t": a2.reshape(NA2, H, HD, R).transpose(0, 1, 3, 2).reshape(NA2, H * R, HD),
        "bv": np.stack([v["L0_attn_bv_q"], v["L0_attn_bv_k"], v["L0_attn_bv_v"]]),
        "wct": np.concatenate([v["L0_ffn_W_res"], v["L0_ffn_W_pre"], v["L0_ffn_W_post"]])
        .reshape(24, NCH, P).transpose(2, 1, 0).reshape(P, NCH * 24),
        "w_branch": v["L0_ffn_W_branch"],
        "h_res": v["L0_ffn_H_res_base"].reshape(-1), "h_pre": v["L0_ffn_H_pre_base"],
        "h_post": v["L0_ffn_H_post_base"], "gate": v["L0_ffn_gate"],
    }
    arrays = {k: np.ascontiguousarray(a) for k, a in arrays.items()}
    nc = bacc.Bacc("TRN2", target_bir_lowering=False, num_devices=1)
    io = {k: nc.dram_tensor(f"in_{k}", a.shape, mybir.dt.from_np(a.dtype), kind="ExternalInput").ap()
          for k, a in arrays.items()}
    io["out"] = nc.dram_tensor("out", (NPAIR, P, D), F32, kind="ExternalOutput").ap()
    program(nc, io)
    r = run_bass_kernel_spmd(nc, [{f"in_{k}": a for k, a in arrays.items()}], core_ids=[0])
    return r.results[0]["out"].reshape(B, T, D)
```
